# Optimizing a Trainium2 kernel written in Bass

```python
import numpy as np
import jax
import jax.numpy as jnp

def _softmax(x, axis=-1):
    return jax.nn.softmax(x, axis=axis)

def _gelu(x):
    return jax.nn.gelu(x, approximate=True)

def _silu(x):
    return jax.nn.silu(x)

def _sigmoid(x):
    return jax.nn.sigmoid(x)

def _layernorm(x, axis=-1, eps=1e-05):
    m = jnp.mean(x, axis=axis, keepdims=True)
    v = jnp.var(x, axis=axis, keepdims=True)
    return (x - m) / jnp.sqrt(v + eps)

def _scatter_add(tgt, idx, src, axis=0):
    return tgt.at[idx].add(src)

def _segment_sum(src, seg, n):
    return jax.ops.segment_sum(src, seg, n)
kernel_name = 'mk_sandwich_d2_jaxref_r8_3f8aa3'

def setup_inputs(seed: int=0):
    np.random.seed(seed)
    _w = jnp.asarray

    def _L0_attn_setup():
        import jax, jax.numpy as jnp
        import numpy as np
        K_FACTOR = 0.5
        key = jax.random.key(seed)
        k1, k2, k3, k4 = jax.random.split(key, 4)
        B, S, H, I = (1, 256, 512, 1376)
        x = jax.random.normal(k1, (B, S, H), dtype=jnp.float32)
        w_gate = jax.random.normal(k2, (I, H), dtype=jnp.float32) * 0.02
        w_up = jax.random.normal(k3, (I, H), dtype=jnp.float32) * 0.02
        w_down = jax.random.normal(k4, (H, I), dtype=jnp.float32) * 0.02
        return {'x': x, 'w_gate': w_gate, 'w_up': w_up, 'w_down': w_down}
    _L0_attn_in = _L0_attn_setup()

    def _L0_ffn_setup():
        import jax, jax.numpy as jnp
        import numpy as np
        K_TOP = 8
        key = jax.random.key(seed)
        k1, k2, k3 = jax.random.split(key, 3)
        B, S, H, E = (4, 512, 512, 64)
        hidden_states = jax.random.normal(k1, (B, S, H), dtype=jnp.float32)
        router_weight = jax.random.normal(k2, (E, H), dtype=jnp.float32)
        router_bias = jnp.zeros((E,), dtype=jnp.float32)
        expert_bias = jax.random.normal(k3, (E, H), dtype=jnp.float32) * 0.1
        return {'hidden_states': hidden_states, 'router_weight': router_weight, 'router_bias': router_bias, 'expert_bias': expert_bias}
    _L0_ffn_in = _L0_ffn_setup()

    def _L1_attn_setup():
        import jax, jax.numpy as jnp
        import numpy as np
        from jax import lax
        H = 512
        DIN = 1024
        N = 16
        K = 4
        R = 32
        B_SZ = 2
        L = 256
        EPS = 1e-06

        def rmsnorm(x, w):
            return x * lax.rsqrt(jnp.mean(x * x, axis=-1, keepdims=True) + EPS) * w

        def _selective_scan(x, dt, A, Bm, Cm):
            xT = jnp.transpose(x, (2, 0, 1))
            dtT = jnp.transpose(dt, (2, 0, 1))
            BT = jnp.transpose(Bm, (2, 0, 1))
            CT = jnp.transpose(Cm, (2, 0, 1))

            def step(h, inp):
                x_t, dt_t, B_t, C_t = inp
                dA = jnp.exp(dt_t[..., None] * A)
                dBx = dt_t[..., None] * B_t[:, None, :] * x_t[..., None]
                h = dA * h + dBx
                y = jnp.einsum('bdn,bn->bd', h, C_t)
                return (h, y)
            h0 = jnp.zeros((x.shape[0], x.shape[1], A.shape[1]), dtype=x.dtype)
            _, ys = lax.scan(step, h0, (xT, dtT, BT, CT))
            return jnp.transpose(ys, (1, 2, 0))
        key = jax.random.key(seed)
        ks = jax.random.split(key, 8)
        hidden_states = jax.random.normal(ks[0], (B_SZ, L, H), dtype=jnp.float32)
        s = 0.02
        in_proj_w = jax.random.normal(ks[1], (H, 2 * DIN), dtype=jnp.float32) * s
        conv_w = jax.random.normal(ks[2], (DIN, K), dtype=jnp.float32) * 0.2
        conv_b = jax.random.normal(ks[3], (DIN,), dtype=jnp.float32) * 0.02
        x_proj_w = jax.random.normal(ks[4], (R + 2 * N, DIN), dtype=jnp.float32) * s
        dt_proj_w = jax.random.normal(ks[5], (DIN, R), dtype=jnp.float32) * s
        dt_bias = jax.random.normal(ks[6], (DIN,), dtype=jnp.float32) * 0.5 - 4.0
        A_log = jnp.log(jnp.broadcast_to(jnp.arange(1, N + 1, dtype=jnp.float32)[None, :], (DIN, N)))
        D_param = jnp.ones((DIN,), dtype=jnp.float32)
        out_proj_w = jax.random.normal(ks[7], (H, DIN), dtype=jnp.float32) * s
        dt_ln_w = jnp.ones((R,), dtype=jnp.float32)
        B_ln_w = jnp.ones((N,), dtype=jnp.float32)
        C_ln_w = jnp.ones((N,), dtype=jnp.float32)
        return dict(hidden_states=hidden_states, in_proj_w=in_proj_w, conv_w=conv_w, conv_b=conv_b, x_proj_w=x_proj_w, dt_proj_w=dt_proj_w, dt_bias=dt_bias, A_log=A_log, D_param=D_param, out_proj_w=out_proj_w, dt_ln_w=dt_ln_w, B_ln_w=B_ln_w, C_ln_w=C_ln_w)
    _L1_attn_in = _L1_attn_setup()

    def _L1_ffn_setup():
        import jax, jax.numpy as jnp
        import numpy as np
        B, S, IN, OUT = (4, 256, 512, 512)
        E, K, R = (8, 2, 16)
        CAP_FACTOR = 3.0
        ALPHA = 1.0 / R
        LN_EPS = 1e-05
        key = jax.random.key(seed)
        ks = jax.random.split(key, 6)
        return {'x': jax.random.normal(ks[0], (B, S, IN), dtype=jnp.float32), 'weight': jax.random.normal(ks[1], (OUT, IN), dtype=jnp.float32) * 0.02, 'lora_A': jax.random.normal(ks[2], (E, IN, R), dtype=jnp.float32) / np.sqrt(R), 'lora_B': jax.random.normal(ks[3], (E, R, OUT), dtype=jnp.float32) * 0.02, 'gw1': jax.random.normal(ks[4], (4 * E, IN), dtype=jnp.float32) * 0.02, 'gb1': jnp.zeros((4 * E,), dtype=jnp.float32), 'ln_gamma': jnp.ones((4 * E,), dtype=jnp.float32), 'ln_beta': jnp.zeros((4 * E,), dtype=jnp.float32), 'gw2': jax.random.normal(ks[5], (E, 4 * E), dtype=jnp.float32) * 0.02, 'gb2': jnp.zeros((E,), dtype=jnp.float32)}
    _L1_ffn_in = _L1_ffn_setup()
    _d = {'L0_attn_x': _L0_attn_in['x'], 'L0_attn_w_gate': _L0_attn_in['w_gate'], 'L0_attn_w_up': _L0_attn_in['w_up'], 'L0_attn_w_down': _L0_attn_in['w_down'], 'L0_ffn_router_weight': _L0_ffn_in['router_weight'], 'L0_ffn_router_bias': _L0_ffn_in['router_bias'], 'L0_ffn_expert_bias': _L0_ffn_in['expert_bias'], 'L1_attn_in_proj_w': _L1_attn_in['in_proj_w'], 'L1_attn_conv_w': _L1_attn_in['conv_w'], 'L1_attn_conv_b': _L1_attn_in['conv_b'], 'L1_attn_x_proj_w': _L1_attn_in['x_proj_w'], 'L1_attn_dt_proj_w': _L1_attn_in['dt_proj_w'], 'L1_attn_dt_bias': _L1_attn_in['dt_bias'], 'L1_attn_A_log': _L1_attn_in['A_log'], 'L1_attn_D_param': _L1_attn_in['D_param'], 'L1_attn_out_proj_w': _L1_attn_in['out_proj_w'], 'L1_attn_dt_ln_w': _L1_attn_in['dt_ln_w'], 'L1_attn_B_ln_w': _L1_attn_in['B_ln_w'], 'L1_attn_C_ln_w': _L1_attn_in['C_ln_w'], 'L1_ffn_weight': _L1_ffn_in['weight'], 'L1_ffn_lora_A': _L1_ffn_in['lora_A'], 'L1_ffn_lora_B': _L1_ffn_in['lora_B'], 'L1_ffn_gw1': _L1_ffn_in['gw1'], 'L1_ffn_gb1': _L1_ffn_in['gb1'], 'L1_ffn_ln_gamma': _L1_ffn_in['ln_gamma'], 'L1_ffn_ln_beta': _L1_ffn_in['ln_beta'], 'L1_ffn_gw2': _L1_ffn_in['gw2'], 'L1_ffn_gb2': _L1_ffn_in['gb2']}
    _x0 = _d['L0_attn_x']
    _d['L0_attn_x'] = jax.random.normal(jax.random.fold_in(jax.random.key(seed), 1), (8, 256, 512), dtype=_x0.dtype)
    del _x0
    return _d

def reference(L0_attn_x, L0_attn_w_gate, L0_attn_w_up, L0_attn_w_down, L0_ffn_router_weight, L0_ffn_router_bias, L0_ffn_expert_bias, L1_attn_in_proj_w, L1_attn_conv_w, L1_attn_conv_b, L1_attn_x_proj_w, L1_attn_dt_proj_w, L1_attn_dt_bias, L1_attn_A_log, L1_attn_D_param, L1_attn_out_proj_w, L1_attn_dt_ln_w, L1_attn_B_ln_w, L1_attn_C_ln_w, L1_ffn_weight, L1_ffn_lora_A, L1_ffn_lora_B, L1_ffn_gw1, L1_ffn_gb1, L1_ffn_ln_gamma, L1_ffn_ln_beta, L1_ffn_gw2, L1_ffn_gb2):

    def _L0_attn_ref(x, w_gate, w_up, w_down):
        import jax, jax.numpy as jnp
        import numpy as np
        K_FACTOR = 0.5
        s = jax.nn.silu(jnp.einsum('bsh,ih->bsi', x, w_gate))
        B, S, I = s.shape
        k = int(K_FACTOR * I)
        _, idx = jax.lax.top_k(-jnp.abs(s), k)
        flat = s.reshape(B * S, I)
        rows = jnp.arange(B * S)[:, None]
        flat = flat.at[rows, idx.reshape(B * S, k)].set(0.0)
        s = flat.reshape(B, S, I)
        s = s * jnp.einsum('bsh,ih->bsi', x, w_up)
        return jnp.einsum('bsi,hi->bsh', s, w_down)

    def _L0_ffn_ref(hidden_states, router_weight, router_bias, expert_bias):
        import jax, jax.numpy as jnp
        import numpy as np
        K_TOP = 8
        B, S, H = hidden_states.shape
        E = router_weight.shape[0]
        T = B * S
        flat = hidden_states.reshape(T, H)
        logits = jnp.einsum('th,eh->te', flat, router_weight) + router_bias
        scores = jax.nn.softmax(logits, axis=-1)
        topk_w, topk_idx = jax.lax.top_k(scores, K_TOP)
        w_sum = topk_w.sum(axis=-1, keepdims=True)
        w_dense = jnp.zeros((T, E), dtype=scores.dtype).at[jnp.arange(T)[:, None], topk_idx].add(topk_w)
        bias_mix = jnp.einsum('te,eh->th', w_dense, expert_bias)
        out = flat * w_sum + bias_mix
        return out.reshape(B, S, H)

    def _L1_attn_ref(hidden_states, in_proj_w, conv_w, conv_b, x_proj_w, dt_proj_w, dt_bias, A_log, D_param, out_proj_w, dt_ln_w, B_ln_w, C_ln_w):
        import jax, jax.numpy as jnp
        import numpy as np
        from jax import lax
        H = 512
        DIN = 1024
        N = 16
        K = 4
        R = 32
        B_SZ = 2
        L = 256
        EPS = 1e-06

        def rmsnorm(x, w):
            return x * lax.rsqrt(jnp.mean(x * x, axis=-1, keepdims=True) + EPS) * w

        def _selective_scan(x, dt, A, Bm, Cm):
            xT = jnp.transpose(x, (2, 0, 1))
            dtT = jnp.transpose(dt, (2, 0, 1))
            BT = jnp.transpose(Bm, (2, 0, 1))
            CT = jnp.transpose(Cm, (2, 0, 1))

            def step(h, inp):
                x_t, dt_t, B_t, C_t = inp
                dA = jnp.exp(dt_t[..., None] * A)
                dBx = dt_t[..., None] * B_t[:, None, :] * x_t[..., None]
                h = dA * h + dBx
                y = jnp.einsum('bdn,bn->bd', h, C_t)
                return (h, y)
            h0 = jnp.zeros((x.shape[0], x.shape[1], A.shape[1]), dtype=x.dtype)
            _, ys = lax.scan(step, h0, (xT, dtT, BT, CT))
            return jnp.transpose(ys, (1, 2, 0))
        proj = hidden_states @ in_proj_w
        x, z = jnp.split(proj, 2, axis=-1)
        x = jnp.transpose(x, (0, 2, 1))
        z = jnp.transpose(z, (0, 2, 1))
        Lq = x.shape[-1]
        xp = jnp.pad(x, ((0, 0), (0, 0), (K - 1, 0)))
        xc = conv_b[None, :, None]
        for k in range(K):
            xc = xc + conv_w[None, :, k:k + 1] * xp[:, :, k:k + Lq]
        xc = jax.nn.silu(xc)
        ssm_p = jnp.einsum('bdl,ed->ble', xc, x_proj_w)
        dt_r = rmsnorm(ssm_p[..., :R], dt_ln_w)
        Bm = rmsnorm(ssm_p[..., R:R + N], B_ln_w)
        Cm = rmsnorm(ssm_p[..., R + N:], C_ln_w)
        dt = jnp.einsum('blr,dr->bdl', dt_r, dt_proj_w)
        dt = jax.nn.softplus(dt + dt_bias[None, :, None])
        A = -jnp.exp(A_log)
        Bm = jnp.transpose(Bm, (0, 2, 1))
        Cm = jnp.transpose(Cm, (0, 2, 1))
        ys = _selective_scan(xc, dt, A, Bm, Cm)
        y = (ys + D_param[None, :, None] * xc) * jax.nn.silu(z)
        return jnp.einsum('bdl,hd->blh', y, out_proj_w)

    def _L1_ffn_ref(x, weight, lora_A, lora_B, gw1, gb1, ln_gamma, ln_beta, gw2, gb2):
        import jax, jax.numpy as jnp
        import numpy as np
        B, S, IN, OUT = (4, 256, 512, 512)
        E, K, R = (8, 2, 16)
        CAP_FACTOR = 3.0
        ALPHA = 1.0 / R
        LN_EPS = 1e-05
        orig_shape = x.shape
        xf = x.reshape(-1, orig_shape[-1])
        N = xf.shape[0]
        capacity = int(CAP_FACTOR * N / E)
        h = xf @ gw1.T + gb1
        mu = jnp.mean(h, axis=-1, keepdims=True)
        var = jnp.mean((h - mu) ** 2, axis=-1, keepdims=True)
        h = (h - mu) * jax.lax.rsqrt(var + LN_EPS) * ln_gamma + ln_beta
        h = jax.nn.relu(h)
        gates = h @ gw2.T + gb2
        top_v, top_i = jax.lax.top_k(gates, K)
        top_g = jax.nn.softmax(top_v, axis=-1)
        onehot = (top_i[..., None] == jnp.arange(E)).astype(xf.dtype)
        counts = onehot.sum(axis=0)
        allowed = (counts <= capacity).astype(xf.dtype)
        w = jnp.einsum('nke,nk,ke->ne', onehot, top_g, allowed)
        main = xf @ weight.T
        tmp = jnp.einsum('ni,eir->enr', xf, lora_A)
        tmp = tmp * w.T[:, :, None]
        lora = jnp.einsum('enr,ero->no', tmp, lora_B) * ALPHA
        out = main + lora
        return out.reshape(*orig_shape[:-1], weight.shape[0])
    x = L0_attn_x
    x = x + _layernorm(_L0_attn_ref(_layernorm(x, axis=-1), L0_attn_w_gate, L0_attn_w_up, L0_attn_w_down), axis=-1)
    x = x + _layernorm(_L0_ffn_ref(_layernorm(x, axis=-1), L0_ffn_router_weight, L0_ffn_router_bias, L0_ffn_expert_bias), axis=-1)
    x = x + _layernorm(_L1_attn_ref(_layernorm(x, axis=-1), L1_attn_in_proj_w, L1_attn_conv_w, L1_attn_conv_b, L1_attn_x_proj_w, L1_attn_dt_proj_w, L1_attn_dt_bias, L1_attn_A_log, L1_attn_D_param, L1_attn_out_proj_w, L1_attn_dt_ln_w, L1_attn_B_ln_w, L1_attn_C_ln_w), axis=-1)
    x = x + _layernorm(_L1_ffn_ref(_layernorm(x, axis=-1), L1_ffn_weight, L1_ffn_lora_A, L1_ffn_lora_B, L1_ffn_gw1, L1_ffn_gb1, L1_ffn_ln_gamma, L1_ffn_ln_beta, L1_ffn_gw2, L1_ffn_gb2), axis=-1)
    return x

_drawn_inputs = setup_inputs


def setup_inputs(seed=0):
    import zlib

    import numpy as np

    out = dict(_drawn_inputs(seed))
    spreads = {'L0_ffn_router_bias': (0.0, 0.8),
     'L1_attn_D_param': (1.0, 0.2),
     'L1_attn_dt_ln_w': (1.0, 0.6),
     'L1_attn_B_ln_w': (1.0, 0.6),
     'L1_attn_C_ln_w': (1.0, 0.6),
     'L1_ffn_gb1': (0.0, 0.8),
     'L1_ffn_ln_gamma': (1.0, 0.6),
     'L1_ffn_ln_beta': (0.0, 0.8),
     'L1_ffn_gb2': (0.0, 0.548)}
    factors = {'L1_attn_dt_proj_w': 5.66,
     'L1_ffn_lora_A': 4.58,
     'L1_ffn_lora_B': 4.606,
     'L1_ffn_gw1': 5.854,
     'L1_ffn_gw2': 5.654}
    for name, (base, spread) in spreads.items():
        noise = np.random.default_rng([zlib.crc32(name.encode()), seed]).standard_normal(out[name].shape)
        drawn = base * np.exp(spread * noise) if base else spread * noise
        out[name] = jnp.asarray(drawn.astype(out[name].dtype))
    for name, factor in factors.items():
        out[name] = (out[name] * factor).astype(out[name].dtype)
    return out
```

```python
from contextlib import ExitStack

import concourse.bass as bass
from concourse import mybir

P = 128
F32 = mybir.dt.float32
BF16 = mybir.dt.bfloat16
I32 = mybir.dt.int32
U32 = mybir.dt.uint32
ALU = mybir.AluOpType
ACT = mybir.ActivationFunctionType
AX_X = mybir.AxisListType.X
LN_EPS = 1e-5


class Tile:

    def __init__(self, pair, offset):
        self.parity = offset % 2
        self.real = pair is not None or 0 <= offset
        self.n = offset if pair is None else pair * 2 + offset
        self.half = offset // 2 if pair is None else pair + offset // 2
        self.offset = offset
        self.looped = pair is not None

    def below(self, count):
        return self.real and (self.looped or self.offset < count)


def wait(eng, sem, value):
    if not isinstance(value, int) or value > 0:
        eng.wait_ge(sem, value)


def in_order(eng, sem):
    count = [0]

    def after(instruction):
        count[0] += 1
        instruction.then_inc(sem, 1)
        eng.wait_ge(sem, count[0])

    def restart():
        if count[0]:
            eng.sem_clear(sem)
        count[0] = 0

    return after, restart


def steps(eng, body, first, loop_from, loop_pairs, last):
    for s in range(first, loop_from):
        body(lambda d, s=s: Tile(None, s + d))
    with eng.Fori(0, loop_pairs) as pair:
        for k in range(2):
            body(lambda d, k=k: Tile(pair, loop_from + k + d))
    for s in range(loop_from + 2 * loop_pairs, last + 1):
        body(lambda d, s=s: Tile(None, s + d))


def mlp_and_router(nc, io, x_in_dram, x_out_dram):
    tokens, H = x_in_dram.shape
    I = io["w_gate"].shape[1]
    E = io["router_w"].shape[1]
    TILES = tokens // P
    HC = H // P
    IC = -(-I // P)
    DROP = I // 2
    TOP = 8
    CH = [(c, min(c + 512, I)) for c in range(0, I, 512)]
    NC = len(CH)
    ROUNDS = [range(r, min(r + 4, IC)) for r in range(0, IC, 4)]
    NR = len(ROUNDS)
    GUESS, AROUND, FAR = 0.81, 793.0, 4.0
    SEARCH = ["slope", "slope", "secant", "secant", None]
    x_in_t = x_in_dram.rearrange("(t p) h -> t p h", p=P)
    x_out_t = x_out_dram.rearrange("(t p) h -> t p h", p=P)

    with ExitStack() as ctx:
        def sb(name, shape, dt=F32):
            return ctx.enter_context(nc.sbuf_tensor("a_" + name, shape, dt))

        def bank(name):
            return ctx.enter_context(nc.psum_tensor("a_" + name, [P, 512], F32))

        def sem(name):
            return ctx.enter_context(nc.semaphore("a_" + name))

        w_gate = sb("w_gate", [P, HC, I])
        w_up = sb("w_up", [P, HC, I])
        w_down = sb("w_down", [P, IC, H])
        router_w = sb("router_w", [P, HC, E])
        router_b = sb("router_b", [P, E])
        expert_b = sb("expert_b", [E, H])
        ident = sb("ident", [P, P])
        minus_half = sb("minus_half", [P, 1])
        iota8 = sb("iota8", [P, TOP])
        x_in = sb("x_in", [P, 2, H])
        x_res = sb("x_res", [P, 2, H])
        x_out = sb("x_out", [P, 2, H])
        xn = sb("xn", [P, H])
        xnT = sb("xnT", [P, 2, HC, P])
        gate = sb("gate", [P, 2, I])
        mag = sb("mag", [P, 2, I])
        mag_sum = sb("mag_sum", [P, 2, 1])
        up = sb("up", [P, 2, I])
        work = sb("work", [P, I])
        act = sb("act", [P, IC * P])
        actT = sb("actT", [P, IC, P])
        normed = sb("normed", [P, H])
        x_mid = sb("x_mid", [P, H])
        xn2 = sb("xn2", [P, H])
        xn2T = sb("xn2T", [P, HC, P])
        mix = sb("mix", [P, H])
        logits = sb("logits", [P, E])
        logit8 = sb("logit8", [P, TOP])
        neg_max = sb("neg_max", [P, 1])
        probs = sb("probs", [P, E])
        prob_sum = sb("prob_sum", [P, 1])
        prob8 = sb("prob8", [P, TOP])
        prob8_sum = sb("prob8_sum", [P, 1])
        dense = sb("dense", [P, E])
        denseT = sb("denseT", [E, P])
        stat6 = sb("stat6", [P, 6])
        mean_var = sb("mean_var", [P, 2])
        var_eps = sb("var_eps", [P, 1])
        rstd = sb("rstd", [P, 1])
        at = sb("at", [P, 2])
        lo = sb("lo", [P, 2])
        hi = sb("hi", [P, 2])
        gap = sb("gap", [P, 2])
        slope = sb("slope", [P, 1])
        low = sb("low", [P, 1])
        far = sb("far", [P, 1])
        short = sb("short", [P, 1])
        top8 = sb("top8", [P, TOP])
        rank = sb("rank", [P, 1])
        cut = sb("cut", [P, 1])
        above = sb("above", [P, 1])
        few = sb("few", [P, 1])
        open_row = sb("open_row", [P, 1])
        any_open = sb("any_open", [P, 1])
        any_open_int = sb("any_open_int", [P, 1], I32)
        bit = sb("bit", [P, 1], I32)
        found = sb("found", [P, 1], I32)
        trial = sb("trial", [P, 1], I32)
        take = sb("take", [P, 1], I32)

        mm = [bank(f"mm{j}") for j in range(3)]
        tp = [bank(f"tp{j}") for j in range(2)]
        xt_bank = bank("xt_bank")
        down_bank = bank("down_bank")
        route_bank = bank("route_bank")

        weights_in = [sem(f"weights_in{j}") for j in range(4)]
        consts_ready = sem("consts_ready")
        dve_consts = sem("dve_consts")
        x_loaded = [sem(f"x_loaded{j}") for j in range(2)]
        res_loaded = [sem(f"res_loaded{j}") for j in range(2)]
        stored = [sem(f"stored{j}") for j in range(2)]
        var1, rstd1 = sem("var1"), sem("rstd1")
        var_down, rstd_down = sem("var_down"), sem("rstd_down")
        var2, rstd2 = sem("var2"), sem("rstd2")
        var_mix, rstd_mix = sem("var_mix"), sem("rstd_mix")
        xn_ready = sem("xn_ready")
        xnT_done, xnT_copied = sem("xnT_done"), sem("xnT_copied")
        mm_done, mm_moved = sem("mm_done"), sem("mm_moved")
        mag_ready = sem("mag_ready")
        open_ready, open_known = sem("open_ready"), sem("open_known")
        act_ready = sem("act_ready")
        actT_done, actT_copied = sem("actT_done"), sem("actT_copied")
        down_done, down_read = sem("down_done"), sem("down_read")
        x_mid_ready = sem("x_mid_ready")
        xn2_ready = sem("xn2_ready")
        xn2T_done, xn2T_copied = sem("xn2T_done"), sem("xn2T_copied")
        logits_done, logits_ready, probs_ready = sem("logits_done"), sem("logits_ready"), sem("probs_ready")
        dense_ready, denseT_done, denseT_copied = sem("dense_ready"), sem("denseT_done"), sem("denseT_copied")
        mix_done, mix_read = sem("mix_done"), sem("mix_read")
        x_ready = sem("x_ready")
        dve_order, pool_order = sem("dve_order"), sem("pool_order")
        pace = sem("pace")
        block = ctx.enter_context(nc.Block())
        SPAN = (-2, 3, (TILES - 6) // 2, TILES)
        assert TILES % 2 == 0 and TILES >= 8

        @block.sync
        def _(sp):
            def load_x(t):
                if t.below(TILES):
                    src = x_in_t[bass.ds(sp.snap(t.n), 1)] if t.looped else x_in_t[t.n:t.n + 1]
                    wait(sp, xn_ready, t.n - 1)
                    sp.sem_inc(pace, 1)
                    sp.dma_start(x_in[:, t.parity, :], src.rearrange("o p h -> (o p) h"))\
                        .then_inc(x_loaded[t.parity], 16)

            def load_res(t):
                if t.below(TILES):
                    src = x_in_t[bass.ds(sp.snap(t.n), 1)] if t.looped else x_in_t[t.n:t.n + 1]
                    wait(sp, x_mid_ready, t.n - 1)
                    sp.sem_inc(pace, 1)
                    sp.dma_start(x_res[:, t.parity, :], src.rearrange("o p h -> (o p) h"))\
                        .then_inc(res_loaded[t.parity], 16)

            def store_x(t):
                if t.below(TILES):
                    dst = x_out_t[bass.ds(sp.snap(t.n), 1)] if t.looped else x_out_t[t.n:t.n + 1]
                    sp.wait_ge(x_ready, t.n + 1)
                    sp.sem_inc(pace, 1)
                    sp.dma_start(dst.rearrange("o p h -> (o p) h"), x_out[:, t.parity, :])\
                        .then_inc(stored[t.parity], 16)

            load_x(Tile(None, 0))
            load_x(Tile(None, 1))
            sp.dma_start(w_gate[:], io["w_gate"].rearrange("(c p) i -> p c i", p=P)).then_inc(weights_in[0], 16)
            sp.dma_start(w_up[:], io["w_up"].rearrange("(c p) i -> p c i", p=P)).then_inc(weights_in[1], 16)
            sp.wait_ge(consts_ready, 4)
            whole = I // P * P
            sp.dma_start(w_down[:, 0:I // P, :], io["w_down"][0:whole, :].rearrange("(c p) h -> p c h", p=P))\
                .then_inc(weights_in[2], 16)
            sp.dma_start(w_down[0:I - whole, IC - 1, :], io["w_down"][whole:I, :]).then_inc(weights_in[2], 16)
            sp.dma_start(router_w[:], io["router_w"].rearrange("(c p) e -> p c e", p=P)).then_inc(weights_in[3], 16)
            sp.dma_start(router_b[:], io["router_bias"].rearrange("(o e) -> o e", o=1).to_broadcast([P, E]))\
                .then_inc(weights_in[3], 16)
            sp.dma_start(expert_b[:], io["expert_bias"]).then_inc(weights_in[3], 16)

            def step(tile):
                if tile(3).looped or tile(3).n >= 2:
                    load_x(tile(3))
                load_res(tile(0))
                store_x(tile(-1))

            steps(sp, step, *SPAN)
            for parity in range(2):
                sp.wait_ge(stored[parity], 16 * (TILES // 2))

        @block.gpsimd
        def _(pool):
            nc.gpsimd.memset(ident[:], 0.0).then_inc(consts_ready, 1)
            nc.gpsimd.memset(minus_half[:], -0.5).then_inc(consts_ready, 1)
            nc.gpsimd.memset(w_down[:, IC - 1, :], 0.0).then_inc(consts_ready, 1)
            nc.gpsimd.memset(act[:, I:IC * P], 0.0).then_inc(consts_ready, 1)
            pool.wait_ge(consts_ready, 4)
            nc.gpsimd.affine_select(out=ident[:], in_=ident[:], compare_op=ALU.not_equal, fill=1.0, base=0,
                                    pattern=[[-1, P]], channel_multiplier=1).then_inc(consts_ready, 1)
            nc.gpsimd.iota(iota8[:], pattern=[[1, TOP]], base=0, channel_multiplier=0,
                           allow_small_or_imprecise_dtypes=True).then_inc(consts_ready, 1)
            pool.wait_ge(consts_ready, 6)

            def inverse_root(var, done, t):
                if t.below(TILES):
                    pool.wait_ge(var, t.n + 1)
                    nc.gpsimd.tensor_tensor(rstd[:], var_eps[:], minus_half[:], ALU.pow).then_inc(done, 1)

            def any_row(t):
                if t.below(TILES):
                    pool.wait_ge(open_ready, t.n + 1)
                    pool.sem_inc(pace, 1)
                    nc.gpsimd.partition_all_reduce(any_open[:], open_row[:], P, bass.bass_isa.ReduceOp.max)\
                        .then_inc(pool_order, 1)
                    pool.wait_ge(pool_order, 1)
                    nc.gpsimd.tensor_copy(any_open_int[:], any_open[:]).then_inc(open_known, 1)
                    pool.sem_clear(pool_order)

            def step(tile):
                inverse_root(var_down, rstd_down, tile(-1))
                inverse_root(var2, rstd2, tile(-1))
                any_row(tile(0))
                inverse_root(var1, rstd1, tile(2))
                inverse_root(var_mix, rstd_mix, tile(-1))

            steps(pool, step, *SPAN)

        @block.vector
        def _(dve):
            after, restart = in_order(dve, dve_order)
            V = nc.vector
            dve.wait_ge(consts_ready, 6)
            dve.wait_ge(weights_in[3], 48)

            def normalise(out, src, var, done, t):
                after(V.bn_stats(stat6[:], src))
                after(V.bn_aggr(mean_var[:], stat6[:]))
                after(V.tensor_scalar(var_eps[:], mean_var[:, 1:2], LN_EPS, None, ALU.add))
                dve.sem_inc(var, 1)
                dve.wait_ge(done, t.n + 1)
                dve.sem_inc(pace, 1)
                after(V.tensor_scalar(out, src, mean_var[:, 0:1], rstd[:], ALU.subtract, ALU.mult))

            def first_norm(t):
                dve.wait_ge(x_loaded[t.parity], t.half * 16 + 16)
                wait(dve, xnT_done, t.n)
                dve.sem_inc(pace, 1)
                normalise(xn[:], x_in[:, t.parity, :], var1, rstd1, t)
                dve.sem_inc(xn_ready, 1)

            def residual(t):
                dve.wait_ge(down_done, t.n + 1)
                dve.sem_inc(pace, 1)
                normalise(normed[:], down_bank[:, 0:H], var_down, rstd_down, t)
                dve.sem_inc(down_read, 1)
                dve.wait_ge(res_loaded[t.parity], t.half * 16 + 16)
                after(V.tensor_tensor(x_mid[:], normed[:], x_res[:, t.parity, :], ALU.add))
                dve.sem_inc(x_mid_ready, 1)
                normalise(xn2[:], x_mid[:], var2, rstd2, t)
                dve.sem_inc(xn2_ready, 1)

            def search(t):
                m = mag[:, t.parity, :]
                target = DROP + 3.5
                dve.wait_ge(mag_ready, t.n + 1)
                after(V.memset(lo[:], 0.0))
                after(V.memset(hi[:], float(I)))
                after(V.tensor_scalar(at[:, 0:1], mag_sum[:, t.parity, :], GUESS / I, None, ALU.mult))
                after(V.tensor_scalar(hi[:, 0:1], mag_sum[:, t.parity, :], FAR / I, None, ALU.mult))
                after(V.tensor_scalar(slope[:], mag_sum[:, t.parity, :], 1.0 / (I * AROUND), None, ALU.mult))
                for move in SEARCH:
                    after(V.tensor_scalar(work[:], m, at[:, 0:1], 0.0, ALU.is_le, ALU.add, accum_out=at[:, 1:2]))
                    after(V.tensor_scalar(low[:], at[:, 1:2], float(DROP), None, ALU.is_lt))
                    after(V.tensor_scalar(far[:], low[:], 1e30, None, ALU.mult))
                    if move:
                        after(V.scalar_tensor_tensor(lo[:], at[:], low[:], lo[:], ALU.mult, ALU.max))
                    after(V.scalar_tensor_tensor(hi[:], at[:], far[:], hi[:], ALU.add, ALU.min))
                    if move == "slope":
                        after(V.tensor_scalar(short[:], at[:, 1:2], -1.0, target, ALU.mult, ALU.add))
                        after(V.scalar_tensor_tensor(at[:, 0:1], short[:], slope[:], at[:, 0:1], ALU.mult, ALU.add))
                        after(V.tensor_scalar(at[:, 0:1], at[:, 0:1], lo[:, 0:1], hi[:, 0:1], ALU.max, ALU.min))
                    elif move == "secant":
                        after(V.tensor_tensor(gap[:], hi[:], lo[:], ALU.subtract))
                        after(V.reciprocal(gap[:, 1:2], gap[:, 1:2]))
                        after(V.tensor_scalar(short[:], lo[:, 1:2], -1.0, target, ALU.mult, ALU.add))
                        after(V.scalar_tensor_tensor(short[:], short[:], gap[:, 1:2], gap[:, 0:1], ALU.mult, ALU.mult))
                        after(V.scalar_tensor_tensor(at[:, 0:1], short[:], lo[:, 0:1], hi[:, 0:1], ALU.add, ALU.min))
                after(V.scalar_tensor_tensor(work[:], m, hi[:, 0:1], m, ALU.is_le, ALU.mult))
                after(V.max(top8[:], work[:]))
                after(V.tensor_scalar(rank[:], hi[:, 1:2], float(DROP), None, ALU.subtract))
                after(V.tensor_scalar(few[:], rank[:], float(TOP - 1), None, ALU.is_le))
                after(V.scalar_tensor_tensor(logit8[:], iota8[:], rank[:], top8[:], ALU.is_equal, ALU.mult,
                                             accum_out=cut[:]))
                after(V.tensor_scalar(logit8[:], top8[:], cut[:], 0.0, ALU.is_gt, ALU.add, accum_out=above[:]))
                after(V.scalar_tensor_tensor(open_row[:], above[:], rank[:], few[:], ALU.is_equal, ALU.mult))
                after(V.tensor_scalar(open_row[:], open_row[:], -1.0, 1.0, ALU.mult, ALU.add))
                dve.sem_inc(open_ready, 1)
                after(V.scalar_tensor_tensor(work[:], m, cut[:], gate[:, t.parity, :], ALU.is_gt, ALU.mult))

            def bitwise_search(t):
                m, g = mag[:, t.parity, :], gate[:, t.parity, :]

                def done(instruction):
                    dve.drain()

                done(V.memset(found[:], 0))
                done(V.memset(bit[:], 1 << 30))
                with dve.Fori(0, 31) as _:
                    done(V.tensor_tensor(trial[:], found[:], bit[:], ALU.bitwise_or))
                    done(V.tensor_scalar(work[:], m, trial[:].bitcast(F32), 0.0, ALU.is_lt, ALU.add,
                                         accum_out=above[:]))
                    done(V.tensor_scalar(take[:], above[:], float(DROP), None, ALU.is_lt))
                    done(V.copy_predicated(found[:], take[:], trial[:]))
                    done(V.tensor_scalar(bit[:], bit[:], 1, None, ALU.logical_shift_right))
                cut_bits = found[:].bitcast(F32)
                done(V.tensor_scalar(work[:], m, cut_bits, 0.0, ALU.is_lt, ALU.add, accum_out=above[:]))
                done(V.tensor_scalar(rank[:], above[:], -1.0, float(DROP), ALU.mult, ALU.add))
                done(V.tensor_scalar(work[:], m, cut_bits, None, ALU.is_equal))
                done(V.tensor_tensor_scan(act[:, 0:I], work[:], work[:], 0.0, ALU.add, ALU.bypass))
                done(V.scalar_tensor_tensor(work[:], act[:, 0:I], rank[:], work[:], ALU.is_gt, ALU.mult))
                done(V.scalar_tensor_tensor(work[:], m, cut_bits, work[:], ALU.is_gt, ALU.add))
                done(V.tensor_tensor(work[:], work[:], g, ALU.mult))

            def activate(t):
                dve.wait_ge(open_known, t.n + 1)
                wait(dve, actT_done, t.n * NR)
                dve.wait_ge(mm_moved, t.n * (2 * NC) + 2 * NC)
                dve.sem_inc(pace, 1)
                rows_open = V.value_load(any_open_int[0:1, 0:1])
                with dve.If(rows_open > 0):
                    bitwise_search(t)
                after(V.tensor_tensor(act[:, 0:I], work[:], up[:, t.parity, :], ALU.mult))
                dve.sem_inc(act_ready, 1)

            def shift_logits(t):
                dve.wait_ge(logits_done, t.n + 1)
                after(V.tensor_tensor(logits[:], route_bank[:, 0:E], router_b[:], ALU.add))
                after(V.max(logit8[:], logits[:]))
                after(V.tensor_scalar(neg_max[:], logit8[:, 0:1], -1.0, None, ALU.mult))
                dve.sem_inc(logits_ready, 1)

            def choose(t):
                dve.wait_ge(probs_ready, t.n + 1)
                dve.sem_inc(pace, 1)
                after(V.max(prob8[:], probs[:]))
                after(V.match_replace(dense[:], prob8[:], probs[:], 0.0))
                after(V.tensor_tensor(dense[:], probs[:], dense[:], ALU.subtract))
                dve.sem_inc(dense_ready, 1)
                after(V.reduce_sum(prob8_sum[:], prob8[:], AX_X))
                after(V.reciprocal(prob_sum[:], prob_sum[:]))

            def combine(t):
                dve.wait_ge(mix_done, t.n + 1)
                after(V.scalar_tensor_tensor(mix[:], xn2[:], prob8_sum[:], route_bank[:, 0:H], ALU.mult, ALU.add))
                dve.sem_inc(mix_read, 1)
                after(V.tensor_scalar(mix[:], mix[:], prob_sum[:], None, ALU.mult))
                normalise(normed[:], mix[:], var_mix, rstd_mix, t)
                wait(dve, stored[t.parity], t.half * 16)
                after(V.tensor_tensor(x_out[:, t.parity, :], x_mid[:], normed[:], ALU.add))
                dve.sem_inc(x_ready, 1)

            def step(tile):
                new, now, old = tile(2), tile(0), tile(-1)
                if old.below(TILES):
                    residual(old)
                if now.below(TILES):
                    search(now)
                if old.below(TILES):
                    shift_logits(old)
                if now.below(TILES):
                    activate(now)
                if old.below(TILES):
                    choose(old)
                if new.below(TILES):
                    first_norm(new)
                if old.below(TILES):
                    combine(old)
                restart()

            steps(dve, step, *SPAN)

        @block.scalar
        def _(act_eng):
            A = nc.scalar

            def move_xnT(t):
                if t.below(TILES):
                    act_eng.wait_ge(xnT_done, t.n + 1)
                    A.copy(xnT[:, t.parity, :, :], xt_bank[:, 0:H].rearrange("p (c n) -> p c n", c=HC))\
                        .then_inc(xnT_copied, 1)

            def gate_part(t):
                if not t.below(TILES):
                    return
                wait(act_eng, act_ready, t.n - 1)
                for j, (a, b) in enumerate(CH):
                    act_eng.wait_ge(mm_done, t.n * (2 * NC) + j + 1)
                    A.activation(gate[:, t.parity, a:b], mm[j][:, 0:b - a], ACT.Silu).then_inc(mm_moved, 1)
                act_eng.wait_ge(mm_moved, t.n * (2 * NC) + NC)
                A.activation(mag[:, t.parity, :], gate[:, t.parity, :], ACT.Abs,
                             accum_out=mag_sum[:, t.parity, :]).then_inc(mag_ready, 1)

            def up_part(t):
                if not t.below(TILES):
                    return
                for j, (a, b) in enumerate(CH):
                    act_eng.wait_ge(mm_done, t.n * (2 * NC) + NC + j + 1)
                    A.copy(up[:, t.parity, a:b], mm[j][:, 0:b - a]).then_inc(mm_moved, 1)

            def move_xn2T(t):
                if t.below(TILES):
                    act_eng.wait_ge(xn2T_done, t.n + 1)
                    A.copy(xn2T[:], xt_bank[:, 0:H].rearrange("p (c n) -> p c n", c=HC)).then_inc(xn2T_copied, 1)

            def exponentials(t):
                if t.below(TILES):
                    act_eng.wait_ge(logits_ready, t.n + 1)
                    A.activation(probs[:], logits[:], ACT.Exp, bias=neg_max[:], accum_out=prob_sum[:])\
                        .then_inc(probs_ready, 1)

            def move_actT(t):
                if t.below(TILES):
                    wait(act_eng, down_done, t.n)
                    for r, blocks in enumerate(ROUNDS):
                        act_eng.wait_ge(actT_done, t.n * NR + r + 1)
                        src = tp[(t.parity * NR + r) % 2][:, 0:len(blocks) * P]
                        A.copy(actT[:, blocks[0]:blocks[-1] + 1, :], src.rearrange("p (c n) -> p c n", n=P))\
                            .then_inc(actT_copied, 1)

            def move_denseT(t):
                if t.below(TILES):
                    act_eng.wait_ge(denseT_done, t.n + 1)
                    A.copy(denseT[:], route_bank[0:E, 0:P]).then_inc(denseT_copied, 1)

            def step(tile):
                gate_part(tile(1))
                move_xn2T(tile(-1))
                up_part(tile(1))
                exponentials(tile(-1))
                move_actT(tile(0))
                move_denseT(tile(-1))
                move_xnT(tile(2))

            steps(act_eng, step, *SPAN)

        @block.tensor
        def _(pe):
            T_ = nc.tensor
            pe.wait_ge(consts_ready, 6)

            def turn_x(t):
                if t.below(TILES):
                    pe.wait_ge(xn_ready, t.n + 1)
                    for c in range(HC):
                        last = T_.transpose(xt_bank[:, c * P:(c + 1) * P], xn[:, c * P:(c + 1) * P], ident[:])
                    last.then_inc(xnT_done, 1)

            def project(t, w, first):
                if not t.below(TILES):
                    return
                if first == 0:
                    pe.wait_ge(xnT_copied, t.n + 1)
                if not t.looped and t.n == 0:
                    pe.wait_ge(weights_in[0 if first == 0 else 1], 16)
                for j, (a, b) in enumerate(CH):
                    wait(pe, mm_moved, t.n * (2 * NC) + first + j + 1 - NC)
                    for c in range(HC):
                        last = T_.matmul(mm[j][:, 0:b - a], xnT[:, t.parity, c, :], w[:, c, a:b],
                                         start=(c == 0), stop=(c == HC - 1))
                    last.then_inc(mm_done, 1)

            def turn_x2(t):
                if t.below(TILES):
                    pe.wait_ge(xn2_ready, t.n + 1)
                    pe.wait_ge(xnT_copied, min(t.n + 3, TILES) if not t.looped else t.n + 3)
                    for c in range(HC):
                        last = T_.transpose(xt_bank[:, c * P:(c + 1) * P], xn2[:, c * P:(c + 1) * P], ident[:])
                    last.then_inc(xn2T_done, 1)

            def route(t):
                if t.below(TILES):
                    if not t.looped and t.n == 0:
                        pe.wait_ge(weights_in[3], 48)
                    pe.wait_ge(xn2T_copied, t.n + 1)
                    wait(pe, mix_read, t.n)
                    for c in range(HC):
                        last = T_.matmul(route_bank[:, 0:E], xn2T[:, c, :], router_w[:, c, :],
                                         start=(c == 0), stop=(c == HC - 1))
                    last.then_inc(logits_done, 1)

            def turn_act(t):
                if t.below(TILES):
                    pe.wait_ge(act_ready, t.n + 1)
                    for r, blocks in enumerate(ROUNDS):
                        wait(pe, actT_copied, t.n * NR + r - 1)
                        for k, c in enumerate(blocks):
                            last = T_.transpose(tp[(t.parity * NR + r) % 2][:, k * P:(k + 1) * P],
                                                act[:, c * P:(c + 1) * P], ident[:])
                        last.then_inc(actT_done, 1)

            def down(t):
                if t.below(TILES):
                    if not t.looped and t.n == 0:
                        pe.wait_ge(weights_in[2], 32)
                    wait(pe, down_read, t.n)
                    for r, blocks in enumerate(ROUNDS):
                        pe.wait_ge(actT_copied, t.n * NR + r + 1)
                        for c in blocks:
                            last = T_.matmul(down_bank[:, 0:H], actT[:, c, :], w_down[:, c, :],
                                             start=(c == 0), stop=(c == IC - 1))
                    last.then_inc(down_done, 1)

            def turn_dense(t):
                if t.below(TILES):
                    pe.wait_ge(dense_ready, t.n + 1)
                    pe.sem_inc(pace, 1)
                    T_.transpose(route_bank[0:E, 0:P], dense[:], ident[:]).then_inc(denseT_done, 1)

            def mix_experts(t):
                if t.below(TILES):
                    pe.wait_ge(denseT_copied, t.n + 1)
                    T_.matmul(route_bank[:, 0:H], denseT[:], expert_b[:], start=True, stop=True)\
                        .then_inc(mix_done, 1)

            def step(tile):
                project(tile(1), w_gate, 0)
                turn_x2(tile(-1))
                project(tile(1), w_up, NC)
                route(tile(-1))
                turn_act(tile(0))
                down(tile(0))
                turn_dense(tile(-1))
                mix_experts(tile(-1))
                turn_x(tile(2))

            steps(pe, step, *SPAN)


def selective_scan(nc, io, x_in_dram, x_out_dram):
    BATCHES, L, H = x_in_dram.shape
    D = io["in_proj"].shape[1] // 2
    N = io["A_log"].shape[1]
    K = io["conv_w"].shape[1]
    R = io["dt_proj"].shape[0]
    RBC = R + 2 * N
    HC, DC, TC = H // P, D // P, L // P
    G = 4
    GN = N // G
    GL = GN * L
    RMS_EPS = 1e-6
    PLAN = {
        (0, 0): [("dt", 1)], (0, 1): [("y", -1), ("norm", 0)], (0, 2): [("turn", 0), ("turn", 1)],
        (0, 3): [("out", 0)],
        (1, 0): [("dt", 2)], (1, 1): [("y", 0)], (1, 2): [("out", 1)], (1, 3): [("x", 0)],
        (2, 0): [("dt", 3), ("x", 1)], (2, 1): [("y", 1), ("x", 2)], (2, 2): [("x", 3)], (2, 3): [],
        (3, 0): [("dt", 4), ("x", 4)], (3, 1): [("y", 2), ("x", 5)], (3, 2): [("x", 6)], (3, 3): [],
        (4, 0): [("dt", 5), ("x", 7)], (4, 1): [("y", 3), ("silu_x", 0)], (4, 2): [("ssm", 0)], (4, 3): [("z", 0)],
        (5, 0): [("dt", 6)], (5, 1): [("y", 4), ("turn_ssm", 0)], (5, 2): [("z", 1)], (5, 3): [("z", 2)],
        (6, 0): [("dt", 7)], (6, 1): [("y", 5), ("z", 3)], (6, 2): [("z", 4)], (6, 3): [("z", 5)],
        (7, 0): [("z", 6)], (7, 1): [("y", 6), ("z", 7)], (7, 2): [("silu_z", 0)], (7, 3): [("dt", 8)],
    }
    assert DC == 8 and TC == 2 and N % G == 0
    order = [task for j in range(DC) for g in range(G) for task in PLAN[j, g]]
    front = [task for task in order if task[0] in ("turn", "x", "z", "ssm", "turn_ssm")]
    FRONT = {task: n for n, task in enumerate(front)}
    NF = len(front)
    x_in_b = x_in_dram.rearrange("b (k p) h -> b p k h", p=P)
    x_out_b = x_out_dram.rearrange("b (k p) h -> b p k h", p=P)
    bc_dram = [nc.dram_tensor(f"bc_rows{j}", [2 * N, L], F32) for j in range(2)]

    with ExitStack() as ctx:
        def sb(name, shape, dt=F32):
            return ctx.enter_context(nc.sbuf_tensor("c_" + name, shape, dt))

        def sem(name):
            return ctx.enter_context(nc.semaphore("c_" + name))

        in_proj = sb("in_proj", [P, HC, 2 * D])
        out_proj = sb("out_proj", [P, DC, H])
        x_proj = sb("x_proj", [P, DC, RBC])
        dt_proj = sb("dt_proj", [R, D])
        A_neg = sb("A_neg", [P, DC, N])
        conv_w = sb("conv_w", [P, DC, K])
        conv_b = sb("conv_b", [P, DC])
        dt_bias = sb("dt_bias", [P, DC])
        D_skip = sb("D_skip", [P, DC])
        norm_w = sb("norm_w", [RBC, 1])
        ident = sb("ident", [P, P])
        minus_half = sb("minus_half", [P, TC * 4])
        x_in = sb("x_in", [P, TC, H])
        x_res = sb("x_res", [P, TC, H])
        x_out = sb("x_out", [P, TC, H])
        xn = sb("xn", [P, TC, H])
        xnT = sb("xnT", [P, HC, L])
        padded = sb("padded", [P, 2, K - 1 + L])
        xc = sb("xc", [P, 2, DC, L])
        z = sb("z", [P, 2, DC, L])
        rbcT = sb("rbcT", [RBC, 2, L])
        B_all = sb("B_all", [P, 2, N, L])
        C_all = sb("C_all", [P, 2, N, L])
        dt = sb("dt", [P, 2, L])
        dtx = sb("dtx", [P, 2, L])
        soft = sb("soft", [P, L])
        relu = sb("relu", [P, L])
        state = sb("state", [P, G, GL])
        ssm = sb("ssm", [P, TC, RBC])
        square = sb("square", [P, TC, RBC])
        rms = sb("rms", [P, TC, 4])
        rms_inv = sb("rms_inv", [P, TC, 4])
        stat6 = sb("stat6", [P, 6])
        mean_var = sb("mean_var", [P, TC, 2])
        var_eps = sb("var_eps", [P, TC])
        rstd = sb("rstd", [P, TC])
        out_mean_var = sb("out_mean_var", [P, 2])
        out_var_eps = sb("out_var_eps", [P, 1])
        out_rstd = sb("out_rstd", [P, 1])
        decay = [ctx.enter_context(nc.psum_tensor(f"c_decay{j}", [P, GN, L], F32)) for j in range(2)]
        y_bank = [ctx.enter_context(nc.psum_tensor(f"c_y{j}", [P, 512], F32)) for j in range(2)]
        front_bank = ctx.enter_context(nc.psum_tensor("c_front", [P, 512], F32))
        back_bank = ctx.enter_context(nc.psum_tensor("c_back", [P, 512], F32))

        in_proj_in, out_proj_in, small_in, A_in = sem("in_proj_in"), sem("out_proj_in"), sem("small_in"), sem("A_in")
        consts_ready = sem("consts_ready")
        x_loaded, res_loaded, stored = sem("x_loaded"), sem("res_loaded"), sem("stored")
        rows_stored = sem("rows_stored")
        B_loaded, C_loaded = sem("B_loaded"), sem("C_loaded")
        A_ready = sem("A_ready")
        var_x, rstd_x, xn_ready = sem("var_x"), sem("rstd_x"), sem("xn_ready")
        front_done, front_read = sem("front_done"), sem("front_read")
        conv_done, xc_ready = sem("conv_done"), sem("xc_ready")
        z_ready = sem("z_ready")
        ssm_squares, ssm_rms, ssm_ready = sem("ssm_squares"), sem("ssm_rms"), sem("ssm_ready")
        dt_done, dt_parts, dt_ready = sem("dt_done"), sem("dt_parts"), sem("dt_ready")
        dt_split = sem("dt_split")
        decay_ready, input_ready = sem("decay_ready"), sem("input_ready")
        scanned, weighed, summed = sem("scanned"), sem("weighed"), sem("summed")
        y_skip, y_ready = sem("y_skip"), sem("y_ready")
        out_done, out_read = sem("out_done"), sem("out_read")
        var_out, rstd_out = sem("var_out"), sem("rstd_out")
        x_ready = sem("x_ready")
        dve_order = sem("dve_order")
        pace = sem("pace")
        block = ctx.enter_context(nc.Block())

        def batches(eng, main, tasks):
            def one(at, parity, previous, itself, following):
                before, now, after = ((at(d), (parity + d) % 2) for d in (-1, 0, 1))
                for j in range(DC):
                    for g in range(G):
                        if itself:
                            main(now, j, g)
                        for name, n in PLAN[j, g]:
                            if name == "y" and n < 0:
                                if previous:
                                    tasks[name](before, DC - 1)
                            elif name == "y":
                                if itself:
                                    tasks[name](now, n)
                            elif name == "dt" and n == DC:
                                if following:
                                    tasks[name](after, 0)
                            elif name == "dt":
                                if itself:
                                    tasks[name](now, n)
                            elif name == "out":
                                if previous:
                                    tasks[name](before, n)
                            elif following:
                                tasks[name](after, n)
                if "end" in tasks:
                    tasks["end"]()

            one(lambda d: -1 + d, 1, False, False, True)
            one(lambda d: d, 0, False, True, True)
            with eng.Fori(0, (BATCHES - 2) // 2) as pair:
                for k in range(2):
                    one(lambda d: pair * 2 + (1 + k + d), (1 + k) % 2, True, True, True)
            one(lambda d: BATCHES - 1 + d, (BATCHES - 1) % 2, True, True, False)
            one(lambda d: BATCHES + d, BATCHES % 2, True, False, False)

        def nothing(t, n):
            pass

        @block.sync
        def _(sp):
            def of(dram, b):
                return dram[b:b + 1] if isinstance(b, int) else dram[bass.ds(sp.snap(b), 1)]

            sp.dma_start(in_proj[:], io["in_proj"].rearrange("(c p) d -> p c d", p=P)).then_inc(in_proj_in, 16)
            sp.dma_start(conv_w[:], io["conv_w"].rearrange("(j p) k -> p j k", p=P)).then_inc(small_in, 16)
            sp.dma_start(A_neg[:], io["A_log"].rearrange("(j p) n -> p j n", p=P)).then_inc(A_in, 16)
            for to, of_ in ((conv_b, "conv_b"), (dt_bias, "dt_bias"), (D_skip, "D_param")):
                sp.dma_start(to[:], io[of_]).then_inc(small_in, 16)
            for a, b, of_ in ((0, R, "dt_ln_w"), (R, R + N, "B_ln_w"), (R + N, RBC, "C_ln_w")):
                sp.dma_start(norm_w[a:b, :], io[of_].rearrange("(n o) -> n o", o=1)).then_inc(small_in, 16)
            sp.dma_start(x_proj[:], io["x_proj"].rearrange("(j p) e -> p j e", p=P)).then_inc(small_in, 16)
            sp.dma_start(dt_proj[:], io["dt_proj"]).then_inc(small_in, 16)
            sp.dma_start(out_proj[:], io["out_proj"].rearrange("(j p) h -> p j h", p=P)).then_inc(out_proj_in, 16)

            def norm(t, n):
                b, _ = t
                src = of(x_in_b, b)
                wait(sp, xn_ready, b)
                sp.sem_inc(pace, 1)
                sp.dma_start(x_in[:], src.rearrange("o p k h -> (o p) k h")).then_inc(x_loaded, 16)

            def turn_ssm(t, n):
                b, parity = t
                sp.wait_ge(front_read, b * NF + FRONT["turn_ssm", 0] + 1)
                sp.sem_inc(pace, 1)
                sp.dma_start(bc_dram[parity].ap(), rbcT[R:RBC, parity, :]).then_inc(rows_stored, 16)
                sp.wait_ge(rows_stored, b * 16 + 16)
                sp.sem_inc(pace, 1)
                wait(sp, weighed, (b - 1) * (DC * G))
                sp.sem_inc(pace, 1)
                for rows, to, loaded in ((0, B_all, B_loaded), (N, C_all, C_loaded)):
                    src = bc_dram[parity].ap()[rows:rows + N, :].rearrange("(o n) l -> o (n l)", o=1)
                    sp.dma_start(to[:, parity, :, :].rearrange("p n l -> p (n l)"), src.to_broadcast([P, N * L]))\
                        .then_inc(loaded, 16)

            def out(t, n):
                b, _ = t
                if n == 0:
                    src = of(x_in_b, b)
                    wait(sp, x_ready, b * TC)
                    sp.sem_inc(pace, 1)
                    sp.dma_start(x_res[:], src.rearrange("o p k h -> (o p) k h")).then_inc(res_loaded, 16)
                else:
                    dst = of(x_out_b, b)
                    sp.wait_ge(x_ready, b * TC + TC)
                    sp.sem_inc(pace, 1)
                    sp.dma_start(dst.rearrange("o p k h -> (o p) k h"), x_out[:]).then_inc(stored, 16)

            sp.sem_inc(stored, 16)
            batches(sp, lambda t, j, g: None, {
                "norm": norm, "turn": nothing, "x": nothing, "z": nothing, "silu_x": nothing, "silu_z": nothing,
                "ssm": nothing, "turn_ssm": turn_ssm, "dt": nothing, "y": nothing, "out": out})
            sp.wait_ge(stored, 16 * (BATCHES + 1))

        @block.gpsimd
        def _(pool):
            X = nc.gpsimd
            X.memset(ident[:], 0.0).then_inc(consts_ready, 1)
            X.memset(minus_half[:], -0.5).then_inc(consts_ready, 1)
            X.memset(padded[:, :, 0:K - 1], 0.0).then_inc(consts_ready, 1)
            pool.wait_ge(consts_ready, 3)
            X.affine_select(out=ident[:], in_=ident[:], compare_op=ALU.not_equal, fill=1.0, base=0,
                            pattern=[[-1, P]], channel_multiplier=1).then_inc(consts_ready, 1)

            def main(t, j, g):
                b, parity = t
                q = b * (DC * G) + (j * G + g)
                if j == 0 and g == 0:
                    pool.wait_ge(B_loaded, b * 16 + 16)
                if g == 0:
                    pool.wait_ge(dt_ready, (b * DC + j) * 2 + 2)
                wait(pool, summed, q - (G - 1))
                a = dtx[:, j % 2, :].rearrange("p (o l) -> p o l", o=1).to_broadcast([P, GN, L])
                X.tensor_tensor(state[:, g, :].rearrange("p (n l) -> p n l", n=GN), a,
                                B_all[:, parity, g * GN:(g + 1) * GN, :], ALU.mult).then_inc(input_ready, 1)

            def norm(t, n):
                b, _ = t
                pool.wait_ge(var_x, b + 1)
                X.tensor_tensor(rstd[:], var_eps[:], minus_half[:, 0:TC], ALU.pow).then_inc(rstd_x, 1)

            def ssm_norm(t, n):
                b, _ = t
                pool.wait_ge(ssm_squares, b + 1)
                X.tensor_tensor(rms_inv[:].rearrange("p k s -> p (k s)"), rms[:].rearrange("p k s -> p (k s)"),
                                minus_half[:], ALU.pow).then_inc(ssm_rms, 1)

            def make_dt(t, j):
                b, parity = t
                n = b * DC + j
                pool.wait_ge(dt_parts, n + 1)
                wait(pool, decay_ready, (n - 1) * G)
                X.tensor_tensor(dt[:, j % 2, :], relu[:], soft[:], ALU.add).then_inc(dt_ready, 1)
                pool.wait_ge(dt_ready, n * 2 + 1)
                X.tensor_tensor(dtx[:, j % 2, :], dt[:, j % 2, :], xc[:, parity, j, :], ALU.mult)\
                    .then_inc(dt_ready, 1)

            def gate_y(t, j):
                b, parity = t
                pool.wait_ge(y_skip, b * DC + j + 1)
                X.tensor_tensor(xc[:, parity, j, :], xc[:, parity, j, :], z[:, parity, j, :], ALU.mult)\
                    .then_inc(y_ready, 1)

            def out(t, n):
                b, _ = t
                pool.wait_ge(var_out, b * TC + n + 1)
                X.tensor_tensor(out_rstd[:], out_var_eps[:], minus_half[:, 0:1], ALU.pow).then_inc(rstd_out, 1)

            batches(pool, main, {
                "norm": norm, "turn": nothing, "x": nothing, "z": nothing, "silu_x": nothing, "silu_z": nothing,
                "ssm": ssm_norm, "turn_ssm": nothing, "dt": make_dt, "y": gate_y, "out": out})

        @block.scalar
        def _(act):
            A = nc.scalar
            act.wait_ge(A_in, 16)
            A.activation(A_neg[:], A_neg[:], ACT.Exp).then_inc(A_ready, 1)
            act.wait_ge(A_ready, 1)
            A.mul(A_neg[:], A_neg[:], -1.0).then_inc(A_ready, 1)
            act.wait_ge(A_ready, 2)
            act.wait_ge(small_in, 16 * 9)

            def main(t, j, g):
                b, _ = t
                q = b * (DC * G) + (j * G + g)
                if g == 0:
                    act.wait_ge(dt_ready, (b * DC + j) * 2 + 1)
                wait(act, scanned, q - 1)
                for n in range(GN):
                    last = A.activation(decay[g % 2][:, n, 1:L], dt[:, j % 2, 1:L], ACT.Exp,
                                        scale=A_neg[:, j, g * GN + n:g * GN + n + 1])
                last.then_inc(decay_ready, 1)

            def bank_full(b, task):
                act.wait_ge(front_done, b * NF + FRONT[task] + 1)

            def turn(t, k):
                b, _ = t
                bank_full(b, ("turn", k))
                A.copy(xnT[:, :, k * P:(k + 1) * P], front_bank[:, 0:H].rearrange("p (c n) -> p c n", c=HC))\
                    .then_inc(front_read, 1)

            def x_part(t, j):
                b, parity = t
                bank_full(b, ("x", j))
                if j == 0:
                    wait(act, out_done, (b - 1) * TC)
                wait(act, conv_done, b * DC + j - 1)
                A.activation(xc[:, parity, j, :], front_bank[:, 0:L], ACT.Identity,
                             bias=conv_b[:, j:j + 1], scale=conv_w[:, j, K - 1:K])
                A.copy(padded[:, j % 2, K - 1:], front_bank[:, 0:L]).then_inc(front_read, 1)

            def z_part(t, j):
                b, parity = t
                bank_full(b, ("z", j))
                A.copy(z[:, parity, j, :], front_bank[:, 0:L]).then_inc(front_read, 1)

            def silu_x(t, n):
                b, parity = t
                act.wait_ge(conv_done, b * DC + DC)
                A.activation(xc[:, parity, :, :], xc[:, parity, :, :], ACT.Silu).then_inc(xc_ready, 1)

            def silu_z(t, n):
                b, parity = t
                act.wait_ge(front_read, b * NF + NF)
                A.activation(z[:, parity, :, :], z[:, parity, :, :], ACT.Silu).then_inc(z_ready, 1)

            def turn_ssm(t, n):
                b, parity = t
                bank_full(b, ("turn_ssm", 0))
                A.activation(rbcT[:, parity, :], front_bank[0:RBC, 0:L], ACT.Copy, scale=norm_w[:])\
                    .then_inc(front_read, 1)

            def softplus(t, j):
                b, _ = t
                n = b * DC + j
                act.wait_ge(dt_done, n + 1)
                wait(act, dt_ready, n * 2)
                bias = dt_bias[:, j:j + 1]
                A.activation(relu[:], back_bank[:, 0:L], ACT.Relu, bias=bias)
                A.activation(soft[:], back_bank[:, 0:L], ACT.Abs, bias=bias).then_inc(dt_split, 1)
                act.wait_ge(dt_split, n * 3 + 1)
                A.activation(soft[:], soft[:], ACT.Exp, scale=-1.0).then_inc(dt_split, 1)
                act.wait_ge(dt_split, n * 3 + 2)
                A.activation(soft[:], soft[:], ACT.Ln, bias=1.0).then_inc(dt_split, 1)
                act.wait_ge(dt_split, n * 3 + 3)
                act.sem_inc(dt_parts, 1)

            batches(act, main, {
                "norm": nothing, "turn": turn, "x": x_part, "z": z_part, "silu_x": silu_x, "silu_z": silu_z,
                "ssm": nothing, "turn_ssm": turn_ssm, "dt": softplus, "y": nothing, "out": nothing})

        @block.vector
        def _(dve):
            V = nc.vector
            after, restart = in_order(dve, dve_order)
            for j in range(2):
                after(V.memset(decay[j][:, :, 0:1], 0.0))
            dve.wait_ge(small_in, 16 * 9)
            dve.wait_ge(consts_ready, 4)
            restart()

            def main(t, j, g):
                b, parity = t
                q = b * (DC * G) + (j * G + g)
                if j == 0 and g == 0:
                    dve.wait_ge(C_loaded, b * 16 + 16)
                dve.wait_ge(decay_ready, q + 1)
                dve.wait_ge(input_ready, q + 1)
                V.tensor_tensor_scan(state[:, g, :], decay[g % 2][:].rearrange("p n l -> p (n l)"), state[:, g, :],
                                     0.0, ALU.mult, ALU.add).then_inc(scanned, 1)
                dve.wait_ge(scanned, q + 1)
                V.tensor_tensor(state[:, g, :], state[:, g, :],
                                C_all[:, parity, g * GN:(g + 1) * GN, :].rearrange("p n l -> p (n l)"), ALU.mult)\
                    .then_inc(weighed, 1)

            def norm(t, n):
                b, _ = t
                dve.wait_ge(x_loaded, b * 16 + 16)
                wait(dve, front_done, (b - 1) * NF + TC)
                for k in range(TC):
                    after(V.bn_stats(stat6[:], x_in[:, k, :]))
                    after(V.bn_aggr(mean_var[:, k, :], stat6[:]))
                after(V.tensor_scalar(var_eps[:], mean_var[:, :, 1], LN_EPS, None, ALU.add))
                dve.sem_inc(var_x, 1)
                dve.wait_ge(rstd_x, b + 1)
                for k in range(TC):
                    after(V.tensor_scalar(xn[:, k, :], x_in[:, k, :], mean_var[:, k, 0:1], rstd[:, k:k + 1],
                                          ALU.subtract, ALU.mult))
                dve.sem_inc(xn_ready, 1)

            def x_part(t, j):
                b, parity = t
                dve.wait_ge(front_read, b * NF + FRONT["x", j] + 1)
                dve.sem_inc(pace, 1)
                for k in range(K - 1):
                    after(V.scalar_tensor_tensor(xc[:, parity, j, :], padded[:, j % 2, k:k + L], conv_w[:, j, k:k + 1],
                                                 xc[:, parity, j, :], ALU.mult, ALU.add))
                dve.sem_inc(conv_done, 1)

            def ssm_part(t, n):
                b, _ = t
                dve.wait_ge(front_done, b * NF + FRONT["ssm", 0] + 1)
                wait(dve, front_done, (b - 1) * NF + FRONT["turn_ssm", 0] + 1)
                after(V.tensor_copy(ssm[:], front_bank[:, 0:TC * RBC].rearrange("p (k e) -> p k e", k=TC)))
                dve.sem_inc(front_read, 1)
                after(V.tensor_tensor(square[:], ssm[:], ssm[:], ALU.mult))
                after(V.reduce_sum(rms[:], square[:].rearrange("p k (s n) -> p k s n", n=N), AX_X))
                after(V.tensor_tensor(rms[:, :, 0], rms[:, :, 0], rms[:, :, 1], ALU.add))
                after(V.tensor_scalar(rms[:, :, 0], rms[:, :, 0], N / R, None, ALU.mult))
                after(V.tensor_copy(rms[:, :, 1], rms[:, :, 0]))
                after(V.tensor_scalar(rms[:], rms[:], 1.0 / N, RMS_EPS, ALU.mult, ALU.add))
                dve.sem_inc(ssm_squares, 1)
                dve.wait_ge(ssm_rms, b + 1)
                dve.sem_inc(pace, 1)
                scale = rms_inv[:].rearrange("p k (s o) -> p k s o", o=1).to_broadcast([P, TC, 4, N])
                after(V.tensor_tensor(ssm[:].rearrange("p k (s n) -> p k s n", n=N),
                                      ssm[:].rearrange("p k (s n) -> p k s n", n=N), scale, ALU.mult))
                dve.sem_inc(ssm_ready, 1)

            def skip_y(t, j):
                b, parity = t
                dve.wait_ge(summed, b * (DC * G) + (j + 1) * G)
                V.scalar_tensor_tensor(xc[:, parity, j, :], xc[:, parity, j, :], D_skip[:, j:j + 1],
                                       y_bank[j % 2][:, 0:L], ALU.mult, ALU.add).then_inc(y_skip, 1)

            def out(t, k):
                b, _ = t
                dve.wait_ge(out_done, b * TC + k + 1)
                dve.sem_inc(pace, 1)
                after(V.bn_stats(stat6[:], back_bank[:, 0:H]))
                after(V.bn_aggr(out_mean_var[:], stat6[:]))
                after(V.tensor_scalar(out_var_eps[:], out_mean_var[:, 1:2], LN_EPS, None, ALU.add))
                dve.sem_inc(var_out, 1)
                if k == 0:
                    dve.wait_ge(stored, b * 16 + 16)
                dve.wait_ge(rstd_out, b * TC + k + 1)
                dve.sem_inc(pace, 1)
                after(V.tensor_scalar(x_out[:, k, :], back_bank[:, 0:H], out_mean_var[:, 0:1], out_rstd[:],
                                      ALU.subtract, ALU.mult))
                dve.sem_inc(out_read, 1)
                if k == 0:
                    dve.wait_ge(res_loaded, b * 16 + 16)
                after(V.tensor_tensor(x_out[:, k, :], x_out[:, k, :], x_res[:, k, :], ALU.add))
                dve.sem_inc(x_ready, 1)

            batches(dve, main, {
                "norm": norm, "turn": nothing, "x": x_part, "z": nothing, "silu_x": nothing, "silu_z": nothing,
                "ssm": ssm_part, "turn_ssm": nothing, "dt": nothing, "y": skip_y, "out": out, "end": restart})

        @block.tensor
        def _(pe):
            T_ = nc.tensor
            pe.wait_ge(consts_ready, 4)
            pe.wait_ge(small_in, 16 * 9)
            pe.wait_ge(in_proj_in, 16)
            pe.wait_ge(out_proj_in, 16)

            def main(t, j, g):
                b, _ = t
                q = b * (DC * G) + (j * G + g)
                if g == 0:
                    wait(pe, y_skip, b * DC + j - 1)
                pe.wait_ge(weighed, q + 1)
                for n in range(GN):
                    last = T_.matmul(y_bank[j % 2][:, 0:L], ident[:], state[:, g, n * L:(n + 1) * L],
                                     start=(g == 0 and n == 0), stop=(g == G - 1 and n == GN - 1))
                last.then_inc(summed, 1)

            def bank_free(b, task):
                wait(pe, front_read, b * NF + FRONT[task])

            def turn(t, k):
                b, _ = t
                pe.wait_ge(xn_ready, b + 1)
                bank_free(b, ("turn", k))
                for c in range(HC):
                    last = T_.transpose(front_bank[:, c * P:(c + 1) * P], xn[:, k, c * P:(c + 1) * P], ident[:])
                last.then_inc(front_done, 1)

            def project(name, t, j):
                b, _ = t
                bank_free(b, (name, j))
                col = (j if name == "x" else DC + j) * P
                for c in range(HC):
                    last = T_.matmul(front_bank[:, 0:L], in_proj[:, c, col:col + P], xnT[:, c, :],
                                     start=(c == 0), stop=(c == HC - 1))
                last.then_inc(front_done, 1)

            def ssm_part(t, n):
                b, parity = t
                pe.wait_ge(xc_ready, b + 1)
                bank_free(b, ("ssm", 0))
                for k in range(TC):
                    for j in range(DC):
                        last = T_.matmul(front_bank[:, k * RBC:(k + 1) * RBC], xc[:, parity, j, k * P:(k + 1) * P],
                                         x_proj[:, j, :], start=(j == 0), stop=(j == DC - 1))
                last.then_inc(front_done, 1)

            def turn_ssm(t, n):
                b, parity = t
                pe.wait_ge(ssm_ready, b + 1)
                bank_free(b, ("turn_ssm", 0))
                pe.sem_inc(pace, 1)
                for k in range(TC):
                    last = T_.transpose(front_bank[0:RBC, k * P:(k + 1) * P], ssm[:, k, :], ident[:])
                last.then_inc(front_done, 1)

            def dt_part(t, j):
                b, parity = t
                n = b * DC + j
                pe.wait_ge(front_read, b * NF + FRONT["turn_ssm", 0] + 1)
                wait(pe, dt_parts, n)
                if j in (2, 3):
                    wait(pe, out_read, (b - 1) * TC + j - 1)
                T_.matmul(back_bank[:, 0:L], dt_proj[:, j * P:(j + 1) * P], rbcT[0:R, parity, :],
                          start=True, stop=True).then_inc(dt_done, 1)

            def out(t, k):
                b, parity = t
                pe.wait_ge(y_ready, b * DC + DC)
                last_dt = (b + 1) * DC + 2 + k
                if not isinstance(b, int) or b < BATCHES - 1:
                    pe.wait_ge(dt_parts, last_dt)
                else:
                    wait(pe, out_read, b * TC + k)
                for j in range(DC):
                    last = T_.matmul(back_bank[:, 0:H], xc[:, parity, j, k * P:(k + 1) * P], out_proj[:, j, :],
                                     start=(j == 0), stop=(j == DC - 1))
                last.then_inc(out_done, 1)

            batches(pe, main, {
                "norm": nothing, "turn": turn, "x": lambda t, j: project("x", t, j),
                "z": lambda t, j: project("z", t, j), "silu_x": nothing, "silu_z": nothing,
                "ssm": ssm_part, "turn_ssm": turn_ssm, "dt": dt_part, "y": nothing, "out": out})


def gated_lora(nc, io, x_in_dram, x_out_dram):
    tokens, H = x_in_dram.shape
    OUT = io["ffn_w"].shape[1]
    HID, E = io["gw2"].shape
    ER = io["lora_B"].shape[0]
    R = ER // E
    TILES = tokens // P
    HC = H // P
    SIDE = HID + ER
    CAPACITY = int(3.0 * tokens / E)
    ALPHA = 1.0 / R
    LOADS = 4
    PER = 512 // P
    x_in_t = x_in_dram.rearrange("(t p) h -> p t h", p=P)
    x_out_t = x_out_dram.rearrange("(t p) h -> t p h", p=P)
    assert TILES % 2 == 0 and TILES * E * 2 <= 512

    with ExitStack() as ctx:
        def sb(name, shape, dt=F32):
            return ctx.enter_context(nc.sbuf_tensor("d_" + name, shape, dt))

        def bank(name):
            return ctx.enter_context(nc.psum_tensor("d_" + name, [P, 512], F32))

        def sem(name):
            return ctx.enter_context(nc.semaphore("d_" + name))

        ffn_w = sb("ffn_w", [P, HC, OUT])
        side_w = sb("side_w", [P, HC, SIDE])
        lora_B = sb("lora_B", [ER, OUT])
        gw2 = sb("gw2", [HID, E])
        rows = {name: sb(name, [P, n]) for name, n in
                (("gb1", HID), ("ln_gamma", HID), ("ln_beta", HID), ("gb2", E))}
        ident = sb("ident", [P, P])
        ones = sb("ones", [P, P])
        minus_half = sb("minus_half", [P, TILES])
        iota_e = sb("iota_e", [P, TILES, E])
        x_all = sb("x_all", [P, TILES, H])
        main_all = sb("main_all", [P, TILES, OUT])
        side_all = sb("side_all", [P, TILES, SIDE])
        xn = sb("xn", [P, 2, H])
        xnT = sb("xnT", [P, 2, HC, P])
        stat6 = sb("stat6", [P, 6])
        mean_var = sb("mean_var", [P, TILES, 2])
        one_mean_var = sb("one_mean_var", [P, 2])
        var_eps = sb("var_eps", [P, TILES])
        rstd = sb("rstd", [P, TILES])
        hid = sb("hid", [P, TILES, HID])
        hid2 = sb("hid2", [P, TILES, HID])
        hidT = sb("hidT", [HID, TILES, P])
        scores = sb("scores", [P, TILES, E])
        key = sb("key", [P, TILES, E])
        equal = sb("equal", [P, TILES, E])
        best = sb("best", [P, 2, TILES])
        first = sb("first", [P, TILES])
        chosen = sb("chosen", [P, 2, TILES, E])
        share = sb("share", [P, 2, TILES])
        odds = sb("odds", [P, TILES])
        counts = sb("counts", [P, 2, E])
        weight = sb("weight", [P, TILES, E])
        tmp = sb("tmp", [P, 2, ER])
        tmpT = sb("tmpT", [ER, 2, P])

        turn_bank = [bank(f"turn{j}") for j in range(2)]
        main_bank = [bank(f"main{j}") for j in range(2)]
        side_bank = [bank(f"side{j}") for j in range(2)]
        gate_bank = bank("gate")
        count_bank = bank("count")

        x_loaded = [sem(f"x_loaded{j}") for j in range(LOADS)]
        weights_in, rows_in = sem("weights_in"), sem("rows_in")
        consts_ready = sem("consts_ready")
        var_ready, rstd_ready = sem("var_ready"), sem("rstd_ready")
        xn_ready, turned, xnT_ready = sem("xn_ready"), sem("turned"), sem("xnT_ready")
        main_done, main_moved = sem("main_done"), sem("main_moved")
        side_done, side_moved = sem("side_done"), sem("side_moved")
        hid_ready, hid_turned, hidT_ready = sem("hid_ready"), sem("hid_turned"), sem("hidT_ready")
        scores_done, gap_ready, odds_ready = sem("scores_done"), sem("gap_ready"), sem("odds_ready")
        chosen_ready, counted = sem("chosen_ready"), sem("counted")
        weight_ready, tmp_ready = sem("weight_ready"), sem("tmp_ready")
        tmp_turned, tmpT_ready, lora_done, lora_read = (sem("tmp_turned"), sem("tmpT_ready"), sem("lora_done"),
                                                        sem("lora_read"))
        x_ready, stored = sem("x_ready"), sem("stored")
        dve_order = sem("dve_order")
        pace = sem("pace")
        block = ctx.enter_context(nc.Block())

        def pairs(eng, body):
            for k in range(2):
                body(k, 0, k)
            with eng.Fori(1, TILES // 2) as pair:
                for k in range(2):
                    body(pair * 2 + k, pair, k)

        def at(t):
            return t if isinstance(t, int) else bass.ds(t, 1)

        def tile_of(tensor, t):
            return tensor[:, t, :] if isinstance(t, int) else \
                tensor[:, bass.ds(t, 1), :].rearrange("p o n -> p (o n)")

        @block.sync
        def _(sp):
            step = TILES // LOADS
            for j in range(LOADS):
                sp.dma_start(x_all[:, j * step:(j + 1) * step, :], x_in_t[:, j * step:(j + 1) * step, :])\
                    .then_inc(x_loaded[j], 16)
            sp.dma_start(ffn_w[:], io["ffn_w"].rearrange("(c p) o -> p c o", p=P)).then_inc(weights_in, 16)
            sp.dma_start(side_w[:, :, 0:HID], io["gw1"].rearrange("(c p) o -> p c o", p=P)).then_inc(weights_in, 16)
            sp.dma_start(side_w[:, :, HID:], io["lora_A"].rearrange("(c p) o -> p c o", p=P)).then_inc(weights_in, 16)
            sp.dma_start(lora_B[:], io["lora_B"]).then_inc(weights_in, 16)
            sp.dma_start(gw2[:], io["gw2"]).then_inc(weights_in, 16)
            for name, row in rows.items():
                n = row.shape[1]
                sp.dma_start(row[:], io[name].rearrange("(o n) -> o n", o=1).to_broadcast([P, n]))\
                    .then_inc(rows_in, 16)

            def store(t, pair, parity):
                dst = x_out_t[t:t + 1] if isinstance(t, int) else x_out_t[bass.ds(sp.snap(t), 1)]
                src = tile_of(x_all, t if isinstance(t, int) else sp.snap(t))
                sp.wait_ge(x_ready, t + 1)
                sp.sem_inc(pace, 1)
                sp.dma_start(dst.rearrange("o p h -> (o p) h"), src).then_inc(stored, 16)

            pairs(sp, store)
            sp.wait_ge(stored, 16 * TILES)

        @block.gpsimd
        def _(pool):
            X = nc.gpsimd
            X.memset(ident[:], 0.0).then_inc(consts_ready, 1)
            X.memset(minus_half[:], -0.5).then_inc(consts_ready, 1)
            X.memset(ones[:], 1.0).then_inc(consts_ready, 1)
            X.iota(iota_e[:], pattern=[[0, TILES], [1, E]], base=0, channel_multiplier=0,
                   allow_small_or_imprecise_dtypes=True).then_inc(consts_ready, 1)
            pool.wait_ge(consts_ready, 4)
            X.affine_select(out=ident[:], in_=ident[:], compare_op=ALU.not_equal, fill=1.0, base=0,
                            pattern=[[-1, P]], channel_multiplier=1).then_inc(consts_ready, 1)

            def scale(t, pair, parity):
                wait(pool, tmp_turned, t - 1)
                pool.sem_inc(pace, 1)
                w = tile_of(weight, t).rearrange("p (e o) -> p e o", o=1).to_broadcast([P, E, R])
                X.tensor_tensor(tmp[:, parity, :].rearrange("p (e r) -> p e r", e=E),
                                tile_of(side_all, t)[:, HID:].rearrange("p (e r) -> p e r", e=E), w, ALU.mult)\
                    .then_inc(tmp_ready, 1)

            for n in range(3):
                pool.wait_ge(var_ready, n + 1)
                X.tensor_tensor(rstd[:], var_eps[:], minus_half[:], ALU.pow).then_inc(rstd_ready, 1)
                if n == 1:
                    pool.wait_ge(weight_ready, 1)
                    pairs(pool, scale)

        @block.vector
        def _(dve):
            V = nc.vector
            after, restart = in_order(dve, dve_order)
            dve.wait_ge(consts_ready, 5)
            dve.wait_ge(rows_in, 64)
            for t in range(TILES):
                if t % (TILES // LOADS) == 0:
                    dve.wait_ge(x_loaded[t // (TILES // LOADS)], 16)
                after(V.bn_stats(stat6[:], x_all[:, t, :]))
                after(V.bn_aggr(mean_var[:, t, :], stat6[:]))
            after(V.tensor_scalar(var_eps[:], mean_var[:, :, 1], LN_EPS, None, ALU.add))
            dve.sem_inc(var_ready, 1)
            dve.wait_ge(rstd_ready, 1)
            restart()

            def normalise(t, pair, parity):
                wait(dve, turned, t - 1)
                V.tensor_scalar(xn[:, parity, :], tile_of(x_all, t), tile_of(mean_var, t)[:, 0:1],
                                rstd[:, at(t)] if not isinstance(t, int) else rstd[:, t:t + 1],
                                ALU.subtract, ALU.mult).then_inc(xn_ready, 1)

            pairs(dve, normalise)

            def spread(a, n):
                return a.rearrange("p (t o) -> p t o", o=1).to_broadcast([P, TILES, n])

            def every(a, n):
                return a.rearrange("p (o n) -> p o n", o=1).to_broadcast([P, TILES, n])

            dve.wait_ge(side_moved, TILES)
            after(V.tensor_tensor(hid[:], side_all[:, :, 0:HID], every(rows["gb1"][:], HID), ALU.add))
            after(V.reduce_sum(first[:], hid[:], AX_X))
            after(V.tensor_scalar(first[:], first[:], 1.0 / HID, None, ALU.mult))
            after(V.tensor_tensor(hid[:], hid[:], spread(first[:], HID), ALU.subtract))
            after(V.tensor_tensor(hid2[:], hid[:], hid[:], ALU.mult))
            after(V.reduce_sum(first[:], hid2[:], AX_X))
            after(V.tensor_scalar(var_eps[:], first[:], 1.0 / HID, LN_EPS, ALU.mult, ALU.add))
            dve.sem_inc(var_ready, 1)
            dve.wait_ge(rstd_ready, 2)
            after(V.tensor_tensor(hid[:], hid[:], spread(rstd[:], HID), ALU.mult))
            after(V.tensor_tensor(hid[:], hid[:], every(rows["ln_gamma"][:], HID), ALU.mult))
            after(V.tensor_tensor(hid[:], hid[:], every(rows["ln_beta"][:], HID), ALU.add))
            after(V.tensor_scalar(hid[:], hid[:], 0.0, None, ALU.max))
            dve.sem_inc(hid_ready, 1)
            dve.wait_ge(scores_done, 1)
            after(V.tensor_tensor(scores[:], gate_bank[:, 0:TILES * E].rearrange("p (t e) -> p t e", e=E),
                                  every(rows["gb2"][:], E), ALU.add))
            for k in range(2):
                after(V.tensor_reduce(best[:, k, :], scores[:], AX_X, ALU.max))
                after(V.tensor_tensor(equal[:], scores[:], spread(best[:, k, :], E), ALU.is_equal))
                after(V.scalar_tensor_tensor(key[:], equal[:], -64.0, iota_e[:], ALU.mult, ALU.add))
                after(V.tensor_reduce(first[:], key[:], AX_X, ALU.min))
                after(V.tensor_tensor(chosen[:, k, :, :], key[:], spread(first[:], E), ALU.is_equal))
                if k == 0:
                    after(V.scalar_tensor_tensor(scores[:], chosen[:, 0, :, :], -3e38, scores[:],
                                                 ALU.mult, ALU.add))
            dve.sem_inc(chosen_ready, 1)
            after(V.tensor_tensor(odds[:], best[:, 1, :], best[:, 0, :], ALU.subtract))
            dve.sem_inc(gap_ready, 1)
            dve.wait_ge(odds_ready, 1)
            after(V.tensor_scalar(share[:, 0, :], odds[:], 1.0, None, ALU.add))
            after(V.reciprocal(share[:, 0, :], share[:, 0, :]))
            after(V.tensor_tensor(share[:, 1, :], odds[:], share[:, 0, :], ALU.mult))
            dve.wait_ge(counted, 1)
            after(V.reduce_sum(counts[:], count_bank[:, 0:2 * TILES * E]
                               .rearrange("p (k t e) -> p k e t", k=2, e=E), AX_X))
            after(V.tensor_scalar(counts[:], counts[:], float(CAPACITY), ALPHA, ALU.is_le, ALU.mult))
            for k in range(2):
                after(V.tensor_tensor(chosen[:, k, :, :], chosen[:, k, :, :], spread(share[:, k, :], E), ALU.mult))
                after(V.tensor_tensor(chosen[:, k, :, :], chosen[:, k, :, :], every(counts[:, k, :], E), ALU.mult))
            after(V.tensor_tensor(weight[:], chosen[:, 0, :, :], chosen[:, 1, :, :], ALU.add))
            dve.sem_inc(weight_ready, 1)
            restart()

            def add_lora(t, pair, parity):
                dve.wait_ge(lora_done, t + 1)
                after(V.tensor_tensor(tile_of(main_all, t), tile_of(main_all, t), main_bank[parity][:, 0:OUT],
                                      ALU.add))
                dve.sem_inc(lora_read, 1)
                after(V.bn_stats(stat6[:], tile_of(main_all, t)))
                after(V.bn_aggr(one_mean_var[:], stat6[:]))
                after(V.tensor_copy(tile_of(mean_var, t), one_mean_var[:]))
                restart()

            dve.wait_ge(main_moved, TILES)
            pairs(dve, add_lora)
            after(V.tensor_scalar(var_eps[:], mean_var[:, :, 1], LN_EPS, None, ALU.add))
            dve.sem_inc(var_ready, 1)
            dve.wait_ge(rstd_ready, 3)
            restart()

            def finish(t, pair, parity):
                after(V.tensor_scalar(tile_of(main_all, t), tile_of(main_all, t), tile_of(mean_var, t)[:, 0:1],
                                      rstd[:, at(t)] if not isinstance(t, int) else rstd[:, t:t + 1],
                                      ALU.subtract, ALU.mult))
                after(V.tensor_tensor(tile_of(x_all, t), tile_of(x_all, t), tile_of(main_all, t), ALU.add))
                dve.sem_inc(x_ready, 1)
                restart()

            pairs(dve, finish)

        @block.scalar
        def _(act):
            A = nc.scalar

            def move(t, pair, parity):
                act.wait_ge(turned, t + 1)
                wait(act, side_done, t - 1)
                act.sem_inc(pace, 1)
                A.copy(xnT[:, parity, :, :], turn_bank[parity][:, 0:H].rearrange("p (c n) -> p c n", c=HC))\
                    .then_inc(xnT_ready, 1)
                act.wait_ge(main_done, t + 1)
                act.sem_inc(pace, 1)
                A.copy(tile_of(main_all, t), main_bank[parity][:, 0:OUT]).then_inc(main_moved, 1)
                act.wait_ge(side_done, t + 1)
                act.sem_inc(pace, 1)
                A.copy(tile_of(side_all, t), side_bank[parity][:, 0:SIDE]).then_inc(side_moved, 1)

            pairs(act, move)
            for r in range(TILES // PER):
                act.wait_ge(hid_turned, r + 1)
                A.copy(hidT[:, r * PER:(r + 1) * PER, :],
                       turn_bank[r % 2][0:HID, :].rearrange("p (t n) -> p t n", n=P)).then_inc(hidT_ready, 1)
            act.wait_ge(gap_ready, 1)
            A.activation(odds[:], odds[:], ACT.Exp).then_inc(odds_ready, 1)

            def move_tmp(t, pair, parity):
                act.wait_ge(tmp_turned, t + 1)
                wait(act, lora_done, t - 1)
                act.sem_inc(pace, 1)
                A.copy(tmpT[:, parity, :], turn_bank[parity][0:ER, 0:P]).then_inc(tmpT_ready, 1)

            pairs(act, move_tmp)

        @block.tensor
        def _(pe):
            T_ = nc.tensor
            pe.wait_ge(consts_ready, 5)
            pe.wait_ge(weights_in, 16 * 5)

            def products(t, pair, parity):
                pe.wait_ge(xn_ready, t + 1)
                wait(pe, xnT_ready, t - 1)
                for c in range(HC):
                    last = T_.transpose(turn_bank[parity][:, c * P:(c + 1) * P], xn[:, parity, c * P:(c + 1) * P],
                                        ident[:])
                last.then_inc(turned, 1)
                pe.wait_ge(xnT_ready, t + 1)
                wait(pe, main_moved, t - 1)
                for c in range(HC):
                    last = T_.matmul(main_bank[parity][:, 0:OUT], xnT[:, parity, c, :], ffn_w[:, c, :],
                                     start=(c == 0), stop=(c == HC - 1))
                last.then_inc(main_done, 1)
                wait(pe, side_moved, t - 1)
                for c in range(HC):
                    last = T_.matmul(side_bank[parity][:, 0:SIDE], xnT[:, parity, c, :], side_w[:, c, :],
                                     start=(c == 0), stop=(c == HC - 1))
                last.then_inc(side_done, 1)

            pairs(pe, products)
            pe.wait_ge(hid_ready, 1)
            for r in range(TILES // PER):
                if r >= 2:
                    pe.wait_ge(hidT_ready, r - 1)
                for k in range(PER):
                    last = T_.transpose(turn_bank[r % 2][0:HID, k * P:(k + 1) * P], hid[:, r * PER + k, :], ident[:])
                last.then_inc(hid_turned, 1)
            pe.wait_ge(hidT_ready, TILES // PER)
            for t in range(TILES):
                last = T_.matmul(gate_bank[:, t * E:(t + 1) * E], hidT[:, t, :], gw2[:], start=True, stop=True)
            last.then_inc(scores_done, 1)
            pe.wait_ge(chosen_ready, 1)
            T_.matmul(count_bank[:, 0:2 * TILES * E], ones[:], chosen[:].rearrange("p k t e -> p (k t e)"),
                      start=True, stop=True).then_inc(counted, 1)

            def lora(t, pair, parity):
                pe.wait_ge(tmp_ready, t + 1)
                wait(pe, tmpT_ready, t - 1)
                T_.transpose(turn_bank[parity][0:ER, 0:P], tmp[:, parity, :], ident[:]).then_inc(tmp_turned, 1)
                pe.wait_ge(tmpT_ready, t + 1)
                wait(pe, lora_read, t - 1)
                T_.matmul(main_bank[parity][:, 0:OUT], tmpT[:, parity, :], lora_B[:], start=True, stop=True)\
                    .then_inc(lora_done, 1)

            pairs(pe, lora)


def _program(nc, io, x, out):
    batches, length, H = x.shape
    after_mlp = nc.dram_tensor("x_after_router", [batches * length, H], F32).ap()
    after_scan = nc.dram_tensor("x_after_scan", [batches * length, H], F32).ap()
    mlp_and_router(nc, io, x.rearrange("b s h -> (b s) h"), after_mlp)
    selective_scan(nc, io, after_mlp.rearrange("(b s) h -> b s h", b=batches),
                   after_scan.rearrange("(b s) h -> b s h", b=batches))
    gated_lora(nc, io, after_scan, out.rearrange("b s h -> (b s) h"))


_AS_IS = {"router_bias": "L0_ffn_router_bias", "expert_bias": "L0_ffn_expert_bias",
          "conv_w": "L1_attn_conv_w", "A_log": "L1_attn_A_log",
          "dt_ln_w": "L1_attn_dt_ln_w", "B_ln_w": "L1_attn_B_ln_w", "C_ln_w": "L1_attn_C_ln_w",
          "in_proj": "L1_attn_in_proj_w",
          "gb1": "L1_ffn_gb1", "ln_gamma": "L1_ffn_ln_gamma", "ln_beta": "L1_ffn_ln_beta", "gb2": "L1_ffn_gb2"}
_COLUMNS = {"conv_b": "L1_attn_conv_b", "dt_bias": "L1_attn_dt_bias", "D_param": "L1_attn_D_param"}
_TURNED = {"w_gate": "L0_attn_w_gate", "w_up": "L0_attn_w_up", "w_down": "L0_attn_w_down",
           "router_w": "L0_ffn_router_weight",
           "x_proj": "L1_attn_x_proj_w", "dt_proj": "L1_attn_dt_proj_w", "out_proj": "L1_attn_out_proj_w",
           "ffn_w": "L1_ffn_weight", "gw1": "L1_ffn_gw1", "gw2": "L1_ffn_gw2"}
def kernel(**inputs):
    import numpy as _np
    import concourse.bacc as _bacc
    from concourse import mybir as _mybir
    from concourse.bass_utils import run_bass_kernel_spmd as _run

    nc = _bacc.Bacc("TRN2", target_bir_lowering=False, num_devices=1)
    arrays = {"x": _np.ascontiguousarray(inputs["L0_attn_x"])}
    for name, source in _AS_IS.items():
        arrays[name] = _np.ascontiguousarray(inputs[source])
    for name, source in _TURNED.items():
        arrays[name] = _np.ascontiguousarray(_np.asarray(inputs[source]).T)
    for name, source in _COLUMNS.items():
        arrays[name] = _np.ascontiguousarray(_np.asarray(inputs[source]).reshape(-1, 128).T)
    lora_a, lora_b = _np.asarray(inputs["L1_ffn_lora_A"]), _np.asarray(inputs["L1_ffn_lora_B"])
    arrays["lora_A"] = _np.ascontiguousarray(lora_a.transpose(1, 0, 2).reshape(lora_a.shape[1], -1))
    arrays["lora_B"] = _np.ascontiguousarray(lora_b.reshape(-1, lora_b.shape[2]))
    io = {name: nc.dram_tensor(name, a.shape, _mybir.dt.from_np(a.dtype), kind="ExternalInput").ap()
          for name, a in arrays.items()}
    x = io.pop("x")
    out = nc.dram_tensor("out", x.shape, _mybir.dt.float32, kind="ExternalOutput").ap()
    _program(nc, io, x, out)
    return _run(nc, [arrays], core_ids=[0]).results[0]["out"]
```

```python
from contextlib import ExitStack

import concourse.bass as bass
from concourse import mybir

P = 128
F32 = mybir.dt.float32
BF16 = mybir.dt.bfloat16
I32 = mybir.dt.int32
U32 = mybir.dt.uint32
ALU = mybir.AluOpType
ACT = mybir.ActivationFunctionType
AX_X = mybir.AxisListType.X
LN_EPS = 1e-5


class Tile:

    def __init__(self, pair, offset):
        self.parity = offset % 2
        self.real = pair is not None or 0 <= offset
        self.n = offset if pair is None else pair * 2 + offset
        self.half = offset // 2 if pair is None else pair + offset // 2
        self.offset = offset
        self.looped = pair is not None

    def below(self, count):
        return self.real and (self.looped or self.offset < count)


def wait(eng, sem, value):
    if not isinstance(value, int) or value > 0:
        eng.wait_ge(sem, value)


def in_order(eng, sem):
    count = [0]

    def along(instruction):
        count[0] += 1
        instruction.then_inc(sem, 1)

    def after(instruction):
        along(instruction)
        eng.wait_ge(sem, count[0])

    def restart():
        if count[0]:
            eng.sem_clear(sem)
        count[0] = 0

    return after, along, restart


def steps(eng, body, first, loop_from, loop_pairs, last):
    for s in range(first, loop_from):
        body(lambda d, s=s: Tile(None, s + d))
    with eng.Fori(0, loop_pairs) as pair:
        for k in range(2):
            body(lambda d, k=k: Tile(pair, loop_from + k + d))
    for s in range(loop_from + 2 * loop_pairs, last + 1):
        body(lambda d, s=s: Tile(None, s + d))


def mlp_and_router(nc, io, x_in_dram, x_out_dram):
    tokens, H = x_in_dram.shape
    I = io["w_gate"].shape[1]
    E = io["router_w"].shape[1]
    TILES = tokens // P
    HC = H // P
    IC = -(-I // P)
    DROP = I // 2
    TOP = 8
    MIX, DOWN, X, MID = range(4)
    CH = [(c, min(c + 512, I)) for c in range(0, I, 512)]
    NC = len(CH)
    ROUNDS = [range(r, min(r + 4, IC)) for r in range(0, IC, 4)]
    NR = len(ROUNDS)
    GUESS, AROUND, FAR = 0.81, 793.0, 4.0
    SEARCH = ["slope", "slope", "secant", "secant", None]
    x_in_t = x_in_dram.rearrange("(t p) h -> t p h", p=P)
    x_out_t = x_out_dram.rearrange("(t p) h -> t p h", p=P)

    with ExitStack() as ctx:
        def sb(name, shape, dt=F32):
            return ctx.enter_context(nc.sbuf_tensor("a_" + name, shape, dt))

        def bank(name):
            return ctx.enter_context(nc.psum_tensor("a_" + name, [P, 512], F32))

        def sem(name):
            return ctx.enter_context(nc.semaphore("a_" + name))

        w_gate = sb("w_gate", [P, HC, I])
        w_up = sb("w_up", [P, HC, I])
        w_down = sb("w_down", [P, IC, H])
        router_w = sb("router_w", [P, HC, E])
        router_b = sb("router_b", [P, E])
        expert_b = sb("expert_b", [E, H])
        ident = sb("ident", [P, P])
        minus_half = sb("minus_half", [P, 3])
        iota8 = sb("iota8", [P, TOP])
        x_in = sb("x_in", [P, 2, H])
        x_res = sb("x_res", [P, 2, H])
        x_out = sb("x_out", [P, 2, H])
        xn = sb("xn", [P, H])
        xnT = sb("xnT", [P, 2, HC, P])
        gate = sb("gate", [P, 2, I])
        mag = sb("mag", [P, 2, I])
        mag_sum = sb("mag_sum", [P, 2, 1])
        guess = sb("guess", [P, 2, 2])
        minus_guess = sb("minus_guess", [P, 1])
        signs = sb("signs", [P, I])
        sign_sum = sb("sign_sum", [P, 1])
        up = sb("up", [P, 2, I])
        work = sb("work", [P, I])
        act = sb("act", [P, IC * P])
        actT = sb("actT", [P, IC, P])
        mix_normed = sb("mix_normed", [P, H])
        normed = sb("normed", [P, H])
        x_mid = sb("x_mid", [P, 2, H])
        xn2 = sb("xn2", [P, 2, H])
        xn2T = sb("xn2T", [P, HC, P])
        mix = sb("mix", [P, H])
        logits = sb("logits", [P, E])
        logit8 = sb("logit8", [P, TOP])
        neg_max = sb("neg_max", [P, 1])
        probs = sb("probs", [P, E])
        prob_sum = sb("prob_sum", [P, 1])
        prob8 = sb("prob8", [P, TOP])
        prob8_sum = sb("prob8_sum", [P, 1])
        dense = sb("dense", [P, E])
        denseT = sb("denseT", [E, P])
        stat6 = sb("stat6", [P, 6])
        mean_var = sb("mean_var", [P, 4, 2])
        var_eps = sb("var_eps", [P, 4])
        rstd = sb("rstd", [P, 4])
        place = [sb(f"place{j}", [P, 2]) for j in range(2)]
        lo = sb("lo", [P, 2])
        hi = sb("hi", [P, 2])
        gap = sb("gap", [P, 2])
        slope = sb("slope", [P, 1])
        low = sb("low", [P, 1])
        far = sb("far", [P, 1])
        short = sb("short", [P, 1])
        top8 = sb("top8", [P, TOP])
        rank = sb("rank", [P, 1])
        cut = sb("cut", [P, 1])
        above = sb("above", [P, 1])
        few = sb("few", [P, 1])
        open_row = sb("open_row", [P, 1])
        any_open = sb("any_open", [P, 1])
        any_open_int = sb("any_open_int", [P, 1], I32)
        bit = sb("bit", [P, 1], I32)
        found = sb("found", [P, 1], I32)
        trial = sb("trial", [P, 1], I32)
        take = sb("take", [P, 1], I32)

        mm = [bank(f"mm{j}") for j in range(2)]
        tp = [bank(f"tp{j}") for j in range(2)]
        xt_bank = bank("xt_bank")
        down_bank = bank("down_bank")
        pick_bank = bank("pick_bank")
        mix_bank = bank("mix_bank")

        gate_in = [sem(f"gate_in{j}") for j in range(NC)]
        up_in, down_in, router_in = sem("up_in"), sem("down_in"), sem("router_in")
        consts_ready = sem("consts_ready")
        dve_consts = sem("dve_consts")
        x_loaded = [sem(f"x_loaded{j}") for j in range(2)]
        res_loaded = [sem(f"res_loaded{j}") for j in range(2)]
        stored = [sem(f"stored{j}") for j in range(2)]
        vars_ready, rstds_ready = sem("vars_ready"), sem("rstds_ready")
        mid_var, mid_rstd = sem("mid_var"), sem("mid_rstd")
        mix_normed_ready = sem("mix_normed_ready")
        xn_ready = sem("xn_ready")
        xnT_done, xnT_copied = sem("xnT_done"), sem("xnT_copied")
        mm_done, mm_moved = sem("mm_done"), sem("mm_moved")
        mag_ready, guess_parts, guess_ready = sem("mag_ready"), sem("guess_parts"), sem("guess_ready")
        product_ready = sem("product_ready")
        open_ready, open_known = sem("open_ready"), sem("open_known")
        act_ready = sem("act_ready")
        actT_done, actT_copied = sem("actT_done"), sem("actT_copied")
        down_done, down_read = sem("down_done"), sem("down_read")
        x_mid_ready = sem("x_mid_ready")
        xn2_ready = sem("xn2_ready")
        xn2T_done, xn2T_copied = sem("xn2T_done"), sem("xn2T_copied")
        logits_done, logits_ready, probs_ready = sem("logits_done"), sem("logits_ready"), sem("probs_ready")
        dense_ready, denseT_done, denseT_copied = sem("dense_ready"), sem("denseT_done"), sem("denseT_copied")
        mix_done, mix_read = sem("mix_done"), sem("mix_read")
        x_ready = sem("x_ready")
        dve_order, pool_order = sem("dve_order"), sem("pool_order")
        pace = sem("pace")
        block = ctx.enter_context(nc.Block())
        SPAN = (-2, 5, (TILES - 8) // 2, TILES + 2)
        assert TILES % 2 == 0 and TILES >= 10

        @block.sync
        def _(sp):
            def load_x(t):
                if t.below(TILES):
                    src = x_in_t[bass.ds(sp.snap(t.n), 1)] if t.looped else x_in_t[t.n:t.n + 1]
                    wait(sp, xn_ready, t.n - 1)
                    sp.sem_inc(pace, 1)
                    sp.dma_start(x_in[:, t.parity, :], src.rearrange("o p h -> (o p) h"))\
                        .then_inc(x_loaded[t.parity], 16)

            def load_res(t):
                if t.below(TILES):
                    src = x_in_t[bass.ds(sp.snap(t.n), 1)] if t.looped else x_in_t[t.n:t.n + 1]
                    wait(sp, x_mid_ready, t.n - 1)
                    sp.sem_inc(pace, 1)
                    sp.dma_start(x_res[:, t.parity, :], src.rearrange("o p h -> (o p) h"))\
                        .then_inc(res_loaded[t.parity], 16)

            def store_x(t):
                if t.below(TILES):
                    dst = x_out_t[bass.ds(sp.snap(t.n), 1)] if t.looped else x_out_t[t.n:t.n + 1]
                    sp.wait_ge(x_ready, t.n + 1)
                    sp.sem_inc(pace, 1)
                    sp.dma_start(dst.rearrange("o p h -> (o p) h"), x_out[:, t.parity, :])\
                        .then_inc(stored[t.parity], 16)

            load_x(Tile(None, 0))
            load_x(Tile(None, 1))
            for j, (a, b) in enumerate(CH):
                sp.dma_start(w_gate[:, :, a:b], io["w_gate"][:, a:b].rearrange("(c p) i -> p c i", p=P))\
                    .then_inc(gate_in[j], 16)
            sp.dma_start(w_up[:], io["w_up"].rearrange("(c p) i -> p c i", p=P)).then_inc(up_in, 16)
            sp.wait_ge(consts_ready, 4)
            whole = I // P * P
            sp.dma_start(w_down[:, 0:I // P, :], io["w_down"][0:whole, :].rearrange("(c p) h -> p c h", p=P))\
                .then_inc(down_in, 16)
            sp.dma_start(w_down[0:I - whole, IC - 1, :], io["w_down"][whole:I, :]).then_inc(down_in, 16)
            sp.dma_start(router_w[:], io["router_w"].rearrange("(c p) e -> p c e", p=P)).then_inc(router_in, 16)
            sp.dma_start(router_b[:], io["router_bias"].rearrange("(o e) -> o e", o=1).to_broadcast([P, E]))\
                .then_inc(router_in, 16)
            sp.dma_start(expert_b[:], io["expert_bias"]).then_inc(router_in, 16)

            def step(tile):
                if tile(3).looped or tile(3).n >= 2:
                    load_x(tile(3))
                load_res(tile(0))
                store_x(tile(-3))

            steps(sp, step, *SPAN)
            for parity in range(2):
                sp.wait_ge(stored[parity], 16 * (TILES // 2))

        @block.gpsimd
        def _(pool):
            nc.gpsimd.memset(ident[:], 0.0).then_inc(consts_ready, 1)
            nc.gpsimd.memset(minus_half[:], -0.5).then_inc(consts_ready, 1)
            nc.gpsimd.memset(w_down[:, IC - 1, :], 0.0).then_inc(consts_ready, 1)
            nc.gpsimd.memset(act[:, I:IC * P], 0.0).then_inc(consts_ready, 1)
            pool.wait_ge(consts_ready, 4)
            nc.gpsimd.affine_select(out=ident[:], in_=ident[:], compare_op=ALU.not_equal, fill=1.0, base=0,
                                    pattern=[[-1, P]], channel_multiplier=1).then_inc(consts_ready, 1)
            nc.gpsimd.iota(iota8[:], pattern=[[1, TOP]], base=0, channel_multiplier=0,
                           allow_small_or_imprecise_dtypes=True).then_inc(consts_ready, 1)
            pool.wait_ge(consts_ready, 6)

            def gate_up(t):
                if t.below(TILES):
                    pool.wait_ge(mm_moved, t.n * (2 * NC) + 2 * NC)
                    pool.sem_inc(pace, 1)
                    nc.gpsimd.tensor_tensor(up[:, t.parity, :], gate[:, t.parity, :], up[:, t.parity, :], ALU.mult)\
                        .then_inc(product_ready, 1)

            def inverse_roots(t):
                pool.wait_ge(vars_ready, t.n + 3)
                nc.gpsimd.tensor_tensor(rstd[:, 0:3], var_eps[:, 0:3], minus_half[:], ALU.pow)\
                    .then_inc(rstds_ready, 1)

            def inverse_root_mid(t):
                if t.below(TILES):
                    pool.wait_ge(mid_var, t.n + 1)
                    nc.gpsimd.tensor_tensor(rstd[:, MID:MID + 1], var_eps[:, MID:MID + 1], minus_half[:, 0:1],
                                            ALU.pow).then_inc(mid_rstd, 1)

            def add_mix(t):
                if t.below(TILES):
                    pool.wait_ge(mix_normed_ready, t.n + 1)
                    wait(pool, stored[t.parity], t.half * 16)
                    pool.sem_inc(pace, 1)
                    nc.gpsimd.tensor_tensor(x_out[:, t.parity, :], x_mid[:, t.parity, :], mix_normed[:], ALU.add)\
                        .then_inc(x_ready, 1)

            def any_row(t):
                if t.below(TILES):
                    pool.wait_ge(open_ready, t.n + 1)
                    pool.sem_inc(pace, 1)
                    nc.gpsimd.partition_all_reduce(any_open[:], open_row[:], P, bass.bass_isa.ReduceOp.max)\
                        .then_inc(pool_order, 1)
                    pool.wait_ge(pool_order, 1)
                    nc.gpsimd.tensor_copy(any_open_int[:], any_open[:]).then_inc(open_known, 1)
                    pool.sem_clear(pool_order)

            def step(tile):
                gate_up(tile(0))
                any_row(tile(0))
                inverse_roots(tile(0))
                add_mix(tile(-3))
                inverse_root_mid(tile(-1))

            steps(pool, step, *SPAN)

        @block.vector
        def _(dve):
            after, along, restart = in_order(dve, dve_order)
            V = nc.vector
            dve.wait_ge(consts_ready, 6)
            after(V.memset(mean_var[:], 0.0))
            restart()

            def statistics(src, which):
                after(V.bn_stats(stat6[:], src))
                after(V.bn_aggr(mean_var[:, which, :], stat6[:]))

            def apply(out, src, which):
                after(V.tensor_scalar(out, src, mean_var[:, which, 0:1], rstd[:, which:which + 1],
                                      ALU.subtract, ALU.mult))

            def mix_statistics(t):
                dve.wait_ge(mix_done, t.n + 1)
                after(V.scalar_tensor_tensor(mix[:], xn2[:, t.parity, :], prob8_sum[:], mix_bank[:, 0:H],
                                             ALU.mult, ALU.add))
                dve.sem_inc(mix_read, 1)
                statistics(mix[:], MIX)

            def down_statistics(t):
                dve.wait_ge(down_done, t.n + 1)
                dve.sem_inc(pace, 1)
                statistics(down_bank[:, 0:H], DOWN)

            def x_statistics(t):
                dve.wait_ge(x_loaded[t.parity], t.half * 16 + 16)
                wait(dve, xnT_done, t.n)
                dve.sem_inc(pace, 1)
                statistics(x_in[:, t.parity, :], X)

            def residual(t):
                apply(normed[:], down_bank[:, 0:H], DOWN)
                dve.sem_inc(down_read, 1)
                dve.wait_ge(res_loaded[t.parity], t.half * 16 + 16)
                after(V.tensor_tensor(x_mid[:, t.parity, :], normed[:], x_res[:, t.parity, :], ALU.add))
                dve.sem_inc(x_mid_ready, 1)
                statistics(x_mid[:, t.parity, :], MID)
                after(V.tensor_scalar(var_eps[:, MID:MID + 1], mean_var[:, MID, 1:2], LN_EPS, None, ALU.add))
                dve.sem_inc(mid_var, 1)

            def second_norm(t):
                dve.wait_ge(mid_rstd, t.n + 1)
                dve.sem_inc(pace, 1)
                apply(xn2[:, t.parity, :], x_mid[:, t.parity, :], MID)
                dve.sem_inc(xn2_ready, 1)

            def search(t):
                m = mag[:, t.parity, :]
                target = DROP + 3.5
                dve.wait_ge(guess_ready, t.n + 1)
                along(V.memset(lo[:], 0.0))
                along(V.memset(hi[:, 1:2], float(I)))
                along(V.tensor_scalar(hi[:, 0:1], mag_sum[:, t.parity, :], FAR / I, None, ALU.mult))
                after(V.tensor_scalar(slope[:], mag_sum[:, t.parity, :], 1.0 / (I * AROUND), None, ALU.mult))
                for n, move in enumerate(SEARCH):
                    at, to = place[n % 2], place[(n + 1) % 2]
                    if n == 0:
                        at = guess[:, t.parity, :]
                    else:
                        after(V.tensor_scalar(work[:], m, at[:, 0:1], 0.0, ALU.is_le, ALU.add,
                                              accum_out=at[:, 1:2]))
                    along(V.tensor_scalar(low[:], at[:, 1:2], float(DROP), None, ALU.is_lt))
                    if move == "slope":
                        along(V.tensor_scalar(short[:], at[:, 1:2], -1.0, target, ALU.mult, ALU.add))
                    after(V.tensor_scalar(far[:], at[:, 1:2], float(DROP), 1e30, ALU.is_lt, ALU.mult))
                    if move == "slope":
                        along(V.scalar_tensor_tensor(to[:, 0:1], short[:], slope[:], at[:, 0:1], ALU.mult, ALU.add))
                    if move:
                        along(V.scalar_tensor_tensor(lo[:], at[:, 0:2], low[:], lo[:], ALU.mult, ALU.max))
                    after(V.scalar_tensor_tensor(hi[:], at[:, 0:2], far[:], hi[:], ALU.add, ALU.min))
                    if move == "slope":
                        after(V.tensor_scalar(to[:, 0:1], to[:, 0:1], lo[:, 0:1], hi[:, 0:1], ALU.max, ALU.min))
                    elif move == "secant":
                        along(V.tensor_scalar(short[:], lo[:, 1:2], -1.0, target, ALU.mult, ALU.add))
                        after(V.tensor_tensor(gap[:], hi[:], lo[:], ALU.subtract))
                        after(V.reciprocal(slope[:], gap[:, 1:2]))
                        after(V.scalar_tensor_tensor(short[:], short[:], slope[:], gap[:, 0:1], ALU.mult, ALU.mult))
                        after(V.scalar_tensor_tensor(to[:, 0:1], short[:], lo[:, 0:1], hi[:, 0:1], ALU.add, ALU.min))
                along(V.tensor_scalar(rank[:], hi[:, 1:2], float(DROP), None, ALU.subtract))
                along(V.tensor_scalar(few[:], hi[:, 1:2], float(DROP + TOP - 1), None, ALU.is_le))
                after(V.scalar_tensor_tensor(work[:], m, hi[:, 0:1], m, ALU.is_le, ALU.mult))
                after(V.max(top8[:], work[:]))
                after(V.scalar_tensor_tensor(logit8[:], iota8[:], rank[:], top8[:], ALU.is_equal, ALU.mult,
                                             accum_out=cut[:]))
                after(V.tensor_scalar(logit8[:], top8[:], cut[:], 0.0, ALU.is_gt, ALU.add, accum_out=above[:]))
                after(V.scalar_tensor_tensor(open_row[:], above[:], rank[:], few[:], ALU.is_equal, ALU.mult))
                after(V.tensor_scalar(open_row[:], open_row[:], -1.0, 1.0, ALU.mult, ALU.add))
                dve.sem_inc(open_ready, 1)

            def bitwise_search(t):
                m = mag[:, t.parity, :]

                def done(instruction):
                    dve.drain()

                done(V.memset(found[:], 0))
                done(V.memset(bit[:], 1 << 30))
                with dve.Fori(0, 31) as _:
                    done(V.tensor_tensor(trial[:], found[:], bit[:], ALU.bitwise_or))
                    done(V.tensor_scalar(work[:], m, trial[:].bitcast(F32), 0.0, ALU.is_lt, ALU.add,
                                         accum_out=above[:]))
                    done(V.tensor_scalar(take[:], above[:], float(DROP), None, ALU.is_lt))
                    done(V.copy_predicated(found[:], take[:], trial[:]))
                    done(V.tensor_scalar(bit[:], bit[:], 1, None, ALU.logical_shift_right))
                cut_bits = found[:].bitcast(F32)
                done(V.tensor_scalar(work[:], m, cut_bits, 0.0, ALU.is_lt, ALU.add, accum_out=above[:]))
                done(V.tensor_scalar(rank[:], above[:], -1.0, float(DROP), ALU.mult, ALU.add))
                done(V.tensor_scalar(work[:], m, cut_bits, None, ALU.is_equal))
                done(V.tensor_tensor_scan(act[:, 0:I], work[:], work[:], 0.0, ALU.add, ALU.bypass))
                done(V.scalar_tensor_tensor(work[:], act[:, 0:I], rank[:], work[:], ALU.is_gt, ALU.mult))
                done(V.scalar_tensor_tensor(work[:], m, cut_bits, work[:], ALU.is_gt, ALU.add))
                done(V.tensor_tensor(act[:, 0:I], work[:], up[:, t.parity, :], ALU.mult))

            def activate(t):
                dve.wait_ge(open_known, t.n + 1)
                wait(dve, actT_done, t.n * NR)
                dve.wait_ge(product_ready, t.n + 1)
                dve.sem_inc(pace, 1)
                after(V.scalar_tensor_tensor(act[:, 0:I], mag[:, t.parity, :], cut[:], up[:, t.parity, :],
                                             ALU.is_gt, ALU.mult))
                rows_open = V.value_load(any_open_int[0:1, 0:1])
                with dve.If(rows_open > 0):
                    bitwise_search(t)
                dve.sem_inc(act_ready, 1)

            def shift_logits(t):
                if not t.looped and t.n == 0:
                    dve.wait_ge(router_in, 48)
                dve.wait_ge(logits_done, t.n + 1)
                after(V.tensor_tensor(logits[:], pick_bank[:, 0:E], router_b[:], ALU.add))
                after(V.max(logit8[:], logits[:]))
                after(V.tensor_scalar(neg_max[:], logit8[:, 0:1], -1.0, None, ALU.mult))
                dve.sem_inc(logits_ready, 1)

            def choose(t):
                dve.wait_ge(probs_ready, t.n + 1)
                dve.sem_inc(pace, 1)
                after(V.reciprocal(prob_sum[:], prob_sum[:]))
                after(V.tensor_scalar(probs[:], probs[:], prob_sum[:], None, ALU.mult))
                after(V.max(prob8[:], probs[:]))
                after(V.match_replace(dense[:], prob8[:], probs[:], 0.0))
                after(V.tensor_tensor(dense[:], probs[:], dense[:], ALU.subtract))
                dve.sem_inc(dense_ready, 1)
                after(V.reduce_sum(prob8_sum[:], prob8[:], AX_X))

            def step(tile):
                new, now, old, older, oldest = (tile(d) for d in (2, 0, -1, -2, -3))
                if now.below(TILES):
                    search(now)
                if oldest.below(TILES):
                    mix_statistics(oldest)
                if old.below(TILES):
                    down_statistics(old)
                if new.below(TILES):
                    x_statistics(new)
                after(V.tensor_scalar(var_eps[:, 0:3], mean_var[:, 0:3, 1], LN_EPS, None, ALU.add))
                dve.sem_inc(vars_ready, 1)
                if older.below(TILES):
                    shift_logits(older)
                dve.wait_ge(rstds_ready, now.n + 3)
                dve.sem_inc(pace, 1)
                if oldest.below(TILES):
                    wait(dve, x_ready, oldest.n)
                    dve.sem_inc(pace, 1)
                    apply(mix_normed[:], mix[:], MIX)
                    dve.sem_inc(mix_normed_ready, 1)
                if new.below(TILES):
                    apply(xn[:], x_in[:, new.parity, :], X)
                    dve.sem_inc(xn_ready, 1)
                if old.below(TILES):
                    wait(dve, x_ready, old.n - 1)
                    dve.sem_inc(pace, 1)
                    residual(old)
                if now.below(TILES):
                    activate(now)
                if old.below(TILES):
                    second_norm(old)
                if older.below(TILES):
                    choose(older)
                restart()

            steps(dve, step, *SPAN)

        @block.scalar
        def _(act_eng):
            A = nc.scalar

            def move_xnT(t):
                if t.below(TILES):
                    act_eng.wait_ge(xnT_done, t.n + 1)
                    A.copy(xnT[:, t.parity, :, :], xt_bank[:, 0:H].rearrange("p (c n) -> p c n", c=HC))\
                        .then_inc(xnT_copied, 1)

            def gate_part(t):
                if not t.below(TILES):
                    return
                wait(act_eng, act_ready, t.n - 1)
                for j, (a, b) in enumerate(CH):
                    act_eng.wait_ge(mm_done, t.n * (2 * NC) + j + 1)
                    A.activation(gate[:, t.parity, a:b], mm[j % 2][:, 0:b - a], ACT.Silu).then_inc(mm_moved, 1)
                act_eng.wait_ge(mm_moved, t.n * (2 * NC) + NC)
                A.activation(mag[:, t.parity, :], gate[:, t.parity, :], ACT.Abs,
                             accum_out=mag_sum[:, t.parity, :]).then_inc(mag_ready, 1)
                act_eng.wait_ge(mag_ready, t.n + 1)
                A.activation(guess[:, t.parity, 0:1], mag_sum[:, t.parity, :], ACT.Copy, scale=GUESS / I)
                A.activation(minus_guess[:], mag_sum[:, t.parity, :], ACT.Copy, scale=-GUESS / I)\
                    .then_inc(guess_parts, 1)
                act_eng.wait_ge(guess_parts, t.n * 2 + 1)
                A.activation(signs[:], mag[:, t.parity, :], ACT.Sign, bias=minus_guess[:], accum_out=sign_sum[:])\
                    .then_inc(guess_parts, 1)
                act_eng.wait_ge(guess_parts, t.n * 2 + 2)
                A.activation(guess[:, t.parity, 1:2], sign_sum[:], ACT.Copy, scale=-0.5, bias=I / 2 + 0.25)\
                    .then_inc(guess_ready, 1)

            def up_part(t, parts):
                if not t.below(TILES):
                    return
                for j in parts:
                    a, b = CH[j]
                    act_eng.wait_ge(mm_done, t.n * (2 * NC) + NC + j + 1)
                    A.copy(up[:, t.parity, a:b], mm[(NC + j) % 2][:, 0:b - a]).then_inc(mm_moved, 1)

            def move_xn2T(t):
                if t.below(TILES):
                    act_eng.wait_ge(xn2T_done, t.n + 1)
                    A.copy(xn2T[:], xt_bank[:, 0:H].rearrange("p (c n) -> p c n", c=HC)).then_inc(xn2T_copied, 1)

            def exponentials(t):
                if t.below(TILES):
                    act_eng.wait_ge(logits_ready, t.n + 1)
                    A.activation(probs[:], logits[:], ACT.Exp, bias=neg_max[:], accum_out=prob_sum[:])\
                        .then_inc(probs_ready, 1)

            def move_actT(t):
                if t.below(TILES):
                    wait(act_eng, down_done, t.n)
                    for r, blocks in enumerate(ROUNDS):
                        act_eng.wait_ge(actT_done, t.n * NR + r + 1)
                        src = tp[(t.parity * NR + r) % 2][:, 0:len(blocks) * P]
                        A.copy(actT[:, blocks[0]:blocks[-1] + 1, :], src.rearrange("p (c n) -> p c n", n=P))\
                            .then_inc(actT_copied, 1)

            def move_denseT(t):
                if t.below(TILES):
                    act_eng.wait_ge(denseT_done, t.n + 1)
                    A.copy(denseT[:], pick_bank[0:E, 0:P]).then_inc(denseT_copied, 1)

            def step(tile):
                move_xn2T(tile(-2))
                gate_part(tile(1))
                up_part(tile(1), range(0, 1))
                exponentials(tile(-2))
                up_part(tile(1), range(1, NC))
                move_actT(tile(0))
                move_denseT(tile(-2))
                move_xnT(tile(2))

            steps(act_eng, step, *SPAN)

        @block.tensor
        def _(pe):
            T_ = nc.tensor
            pe.wait_ge(consts_ready, 6)

            def turn_x(t):
                if t.below(TILES):
                    pe.wait_ge(xn_ready, t.n + 1)
                    for c in range(HC):
                        last = T_.transpose(xt_bank[:, c * P:(c + 1) * P], xn[:, c * P:(c + 1) * P], ident[:])
                    last.then_inc(xnT_done, 1)

            def project(t, w, first):
                if not t.below(TILES):
                    return
                if first == 0:
                    pe.wait_ge(xnT_copied, t.n + 1)
                for j, (a, b) in enumerate(CH):
                    if not t.looped and t.n == 0 and (first == 0 or j == 0):
                        pe.wait_ge(gate_in[j] if first == 0 else up_in, 16)
                    wait(pe, mm_moved, t.n * (2 * NC) + first + j - 1)
                    for c in range(HC):
                        last = T_.matmul(mm[(first + j) % 2][:, 0:b - a], xnT[:, t.parity, c, :], w[:, c, a:b],
                                         start=(c == 0), stop=(c == HC - 1))
                    last.then_inc(mm_done, 1)

            def turn_x2(t):
                if t.below(TILES):
                    pe.wait_ge(xn2_ready, t.n + 1)
                    pe.wait_ge(xnT_copied, min(t.n + 4, TILES) if not t.looped else t.n + 4)
                    for c in range(HC):
                        last = T_.transpose(xt_bank[:, c * P:(c + 1) * P], xn2[:, t.parity, c * P:(c + 1) * P], ident[:])
                    last.then_inc(xn2T_done, 1)

            def route(t):
                if t.below(TILES):
                    if not t.looped and t.n == 0:
                        pe.wait_ge(router_in, 48)
                    pe.wait_ge(xn2T_copied, t.n + 1)
                    wait(pe, denseT_copied, t.n)
                    for c in range(HC):
                        last = T_.matmul(pick_bank[:, 0:E], xn2T[:, c, :], router_w[:, c, :],
                                         start=(c == 0), stop=(c == HC - 1))
                    last.then_inc(logits_done, 1)

            def turn_act(t):
                if t.below(TILES):
                    pe.wait_ge(act_ready, t.n + 1)
                    for r, blocks in enumerate(ROUNDS):
                        wait(pe, actT_copied, t.n * NR + r - 1)
                        for k, c in enumerate(blocks):
                            last = T_.transpose(tp[(t.parity * NR + r) % 2][:, k * P:(k + 1) * P],
                                                act[:, c * P:(c + 1) * P], ident[:])
                        last.then_inc(actT_done, 1)

            def down(t):
                if t.below(TILES):
                    if not t.looped and t.n == 0:
                        pe.wait_ge(down_in, 32)
                    wait(pe, down_read, t.n)
                    for r, blocks in enumerate(ROUNDS):
                        pe.wait_ge(actT_copied, t.n * NR + r + 1)
                        for c in blocks:
                            last = T_.matmul(down_bank[:, 0:H], actT[:, c, :], w_down[:, c, :],
                                             start=(c == 0), stop=(c == IC - 1))
                    last.then_inc(down_done, 1)

            def turn_dense(t):
                if t.below(TILES):
                    pe.wait_ge(dense_ready, t.n + 1)
                    pe.sem_inc(pace, 1)
                    T_.transpose(pick_bank[0:E, 0:P], dense[:], ident[:]).then_inc(denseT_done, 1)

            def mix_experts(t):
                if t.below(TILES):
                    pe.wait_ge(denseT_copied, t.n + 1)
                    wait(pe, mix_read, t.n)
                    T_.matmul(mix_bank[:, 0:H], denseT[:], expert_b[:], start=True, stop=True)\
                        .then_inc(mix_done, 1)

            def step(tile):
                turn_x2(tile(-2))
                project(tile(1), w_gate, 0)
                route(tile(-2))
                project(tile(1), w_up, NC)
                turn_act(tile(0))
                down(tile(0))
                turn_dense(tile(-2))
                mix_experts(tile(-2))
                turn_x(tile(2))

            steps(pe, step, *SPAN)


def selective_scan(nc, io, x_in_dram, x_out_dram):
    BATCHES, L, H = x_in_dram.shape
    D = io["in_proj"].shape[1] // 2
    N = io["A_log"].shape[1]
    K = io["conv_w"].shape[1]
    R = io["dt_proj"].shape[0]
    RBC = R + 2 * N
    HC, DC, TC = H // P, D // P, L // P
    G = 4
    GN = N // G
    GL = GN * L
    RMS_EPS = 1e-6
    PLAN = {
        (0, 1): [("y", -1), ("norm", 0)], (0, 2): [("dt", 2)], (0, 3): [("out", 0)],
        (1, 0): [("turn", 0)], (1, 1): [("y", 0), ("turn", 1)], (1, 2): [("dt", 3)], (1, 3): [("out", 1)],
        (2, 0): [("x", 0)], (2, 1): [("y", 1)], (2, 2): [("dt", 4), ("x", 1)],
        (3, 0): [("x", 2)], (3, 1): [("y", 2)], (3, 2): [("dt", 5), ("x", 3)], (3, 3): [("z", 0)],
        (4, 1): [("y", 3), ("silu_x", 0)], (4, 2): [("dt", 6), ("z", 1)], (4, 3): [("ssm", 0)],
        (5, 1): [("y", 4)], (5, 2): [("dt", 7), ("turn_ssm", 0)], (5, 3): [("z", 2)],
        (6, 1): [("y", 5), ("z", 3)], (6, 2): [("dt", 8)], (6, 3): [("silu_z", 0)],
        (7, 1): [("y", 6)], (7, 2): [("dt", 9)],
    }
    SLOTS = DC * G
    AHEAD = {"pool": 3, "act": 2, "dve": 0, "pe": 0, "sp": 0}
    BEHIND = {"act": {"turn": 1, "x": 1, "z": 1, "turn_ssm": 1},
              "dve": {"x": 2, "ssm": 2, "out": 2},
              "pool": {"ssm": 2, "out": 2}, "pe": {}, "sp": {}}
    assert DC == 8 and TC == 2 and N % G == 0
    order = [task for slot in sorted(PLAN) for task in PLAN[slot]]
    TASKS = {engine: [[] for _ in range(SLOTS)] for engine in AHEAD}
    for engine, behind in BEHIND.items():
        for (j, g), planned in sorted(PLAN.items()):
            for name, n in planned:
                TASKS[engine][j * G + g + behind.get(name, 0)].append((name, n))
    front = [task for task in order if task[0] in ("turn", "x", "z", "ssm", "turn_ssm")]
    FRONT = {task: n for n, task in enumerate(front)}
    NF = len(front)
    x_in_b = x_in_dram.rearrange("b (k p) h -> b p k h", p=P)
    x_out_b = x_out_dram.rearrange("b (k p) h -> b p k h", p=P)
    bc_dram = [nc.dram_tensor(f"bc_rows{j}", [2 * N, L], F32) for j in range(2)]

    with ExitStack() as ctx:
        def sb(name, shape, dt=F32):
            return ctx.enter_context(nc.sbuf_tensor("c_" + name, shape, dt))

        def sem(name):
            return ctx.enter_context(nc.semaphore("c_" + name))

        in_proj = sb("in_proj", [P, HC, 2 * D])
        out_proj = sb("out_proj", [P, DC, H])
        x_proj = sb("x_proj", [P, DC, RBC])
        dt_proj = sb("dt_proj", [R, D])
        A_neg = sb("A_neg", [P, DC, N])
        conv_w = sb("conv_w", [P, DC, K])
        conv_b = sb("conv_b", [P, DC])
        dt_bias = sb("dt_bias", [P, DC])
        D_skip = sb("D_skip", [P, DC])
        norm_w = sb("norm_w", [RBC, 1])
        ident = sb("ident", [P, P])
        minus_half = sb("minus_half", [P, TC * 4])
        x_in = sb("x_in", [P, TC, H])
        x_res = sb("x_res", [P, TC, H])
        x_out = sb("x_out", [P, TC, H])
        xn = sb("xn", [P, TC, H])
        xnT = sb("xnT", [P, HC, L])
        padded = sb("padded", [P, 2, 2, K - 1 + L])
        xc = sb("xc", [P, 2, DC, L])
        z = sb("z", [P, 2, DC, L])
        rbcT = sb("rbcT", [RBC, 2, L])
        B_all = sb("B_all", [P, 2, N, L])
        C_all = sb("C_all", [P, 2, N, L])
        dt = sb("dt", [P, 2, L])
        dtx = sb("dtx", [P, 2, L])
        soft = sb("soft", [P, L])
        relu = sb("relu", [P, L])
        state = sb("state", [P, G, GL])
        ssm = sb("ssm", [P, TC, RBC])
        square = sb("square", [P, TC, RBC])
        rms = sb("rms", [P, TC, 4])
        rms_inv = sb("rms_inv", [P, TC, 4])
        stat6 = sb("stat6", [P, 6])
        mean_var = sb("mean_var", [P, TC, 2])
        var_eps = sb("var_eps", [P, TC])
        rstd = sb("rstd", [P, TC])
        out_mean_var = sb("out_mean_var", [P, 2])
        out_var_eps = sb("out_var_eps", [P, 1])
        out_rstd = sb("out_rstd", [P, 1])
        decay = [ctx.enter_context(nc.psum_tensor(f"c_decay{j}", [P, GN, L], F32)) for j in range(2)]
        y_bank = [ctx.enter_context(nc.psum_tensor(f"c_y{j}", [P, 512], F32)) for j in range(2)]
        front_bank = ctx.enter_context(nc.psum_tensor("c_front", [P, 512], F32))
        back_bank = ctx.enter_context(nc.psum_tensor("c_back", [P, 512], F32))

        in_proj_in, out_proj_in, small_in, A_in = sem("in_proj_in"), sem("out_proj_in"), sem("small_in"), sem("A_in")
        consts_ready = sem("consts_ready")
        x_loaded, res_loaded, stored = sem("x_loaded"), sem("res_loaded"), sem("stored")
        rows_stored = sem("rows_stored")
        B_loaded, C_loaded = sem("B_loaded"), sem("C_loaded")
        A_ready = sem("A_ready")
        var_x, rstd_x, xn_ready = sem("var_x"), sem("rstd_x"), sem("xn_ready")
        front_done, front_read = sem("front_done"), sem("front_read")
        conv_done, xc_ready = sem("conv_done"), sem("xc_ready")
        z_ready = sem("z_ready")
        ssm_squares, ssm_rms, ssm_ready = sem("ssm_squares"), sem("ssm_rms"), sem("ssm_ready")
        dt_done, dt_parts, dt_ready = sem("dt_done"), sem("dt_parts"), sem("dt_ready")
        dt_split = sem("dt_split")
        decay_ready, input_ready = sem("decay_ready"), sem("input_ready")
        scanned, weighed, summed = sem("scanned"), sem("weighed"), sem("summed")
        y_skip, y_ready = sem("y_skip"), sem("y_ready")
        out_done, out_read = sem("out_done"), sem("out_read")
        var_out, rstd_out = sem("var_out"), sem("rstd_out")
        x_ready = sem("x_ready")
        dve_order = sem("dve_order")
        pace = sem("pace")
        block = ctx.enter_context(nc.Block())

        def batches(name_of, eng, main, tasks):
            def one(at, parity, previous, itself, following):
                before, now, after = ((at(d), (parity + d) % 2) for d in (-1, 0, 1))
                for slot in range(SLOTS):
                    ahead = slot + AHEAD[name_of]
                    if itself if ahead < SLOTS else following:
                        main(now if ahead < SLOTS else after, ahead % SLOTS // G, ahead % G)
                    for name, n in TASKS[name_of][slot]:
                        if name == "out" or (name == "y" and n < 0):
                            batch, there = before, previous
                        elif name == "y" or (name == "dt" and n < DC):
                            batch, there = now, itself
                        else:
                            batch, there = after, following
                        if there:
                            tasks[name](batch, n % DC if name in ("y", "dt") else n)
                if "end" in tasks:
                    tasks["end"]()

            one(lambda d: -1 + d, 1, False, False, True)
            one(lambda d: d, 0, False, True, True)
            with eng.Fori(0, (BATCHES - 2) // 2) as pair:
                for k in range(2):
                    one(lambda d: pair * 2 + (1 + k + d), (1 + k) % 2, True, True, True)
            one(lambda d: BATCHES - 1 + d, (BATCHES - 1) % 2, True, True, False)
            one(lambda d: BATCHES + d, BATCHES % 2, True, False, False)

        def nothing(t, n):
            pass

        @block.sync
        def _(sp):
            def of(dram, b):
                return dram[b:b + 1] if isinstance(b, int) else dram[bass.ds(sp.snap(b), 1)]

            sp.dma_start(in_proj[:], io["in_proj"].rearrange("(c p) d -> p c d", p=P)).then_inc(in_proj_in, 16)
            sp.dma_start(conv_w[:], io["conv_w"].rearrange("(j p) k -> p j k", p=P)).then_inc(small_in, 16)
            sp.dma_start(A_neg[:], io["A_log"].rearrange("(j p) n -> p j n", p=P)).then_inc(A_in, 16)
            for to, of_ in ((conv_b, "conv_b"), (dt_bias, "dt_bias"), (D_skip, "D_param")):
                sp.dma_start(to[:], io[of_]).then_inc(small_in, 16)
            for a, b, of_ in ((0, R, "dt_ln_w"), (R, R + N, "B_ln_w"), (R + N, RBC, "C_ln_w")):
                sp.dma_start(norm_w[a:b, :], io[of_].rearrange("(n o) -> n o", o=1)).then_inc(small_in, 16)
            sp.dma_start(x_proj[:], io["x_proj"].rearrange("(j p) e -> p j e", p=P)).then_inc(small_in, 16)
            sp.dma_start(dt_proj[:], io["dt_proj"]).then_inc(small_in, 16)
            sp.dma_start(out_proj[:], io["out_proj"].rearrange("(j p) h -> p j h", p=P)).then_inc(out_proj_in, 16)

            def norm(t, n):
                b, _ = t
                src = of(x_in_b, b)
                wait(sp, xn_ready, b)
                sp.sem_inc(pace, 1)
                sp.dma_start(x_in[:], src.rearrange("o p k h -> (o p) k h")).then_inc(x_loaded, 16)

            def turn_ssm(t, n):
                b, parity = t
                sp.wait_ge(front_read, b * NF + FRONT["turn_ssm", 0] + 1)
                sp.sem_inc(pace, 1)
                sp.dma_start(bc_dram[parity].ap(), rbcT[R:RBC, parity, :]).then_inc(rows_stored, 16)
                sp.wait_ge(rows_stored, b * 16 + 16)
                sp.sem_inc(pace, 1)
                wait(sp, weighed, (b - 1) * (DC * G))
                sp.sem_inc(pace, 1)
                for rows, to, loaded in ((0, B_all, B_loaded), (N, C_all, C_loaded)):
                    src = bc_dram[parity].ap()[rows:rows + N, :].rearrange("(o n) l -> o (n l)", o=1)
                    sp.dma_start(to[:, parity, :, :].rearrange("p n l -> p (n l)"), src.to_broadcast([P, N * L]))\
                        .then_inc(loaded, 16)

            def out(t, n):
                b, _ = t
                if n == 0:
                    src = of(x_in_b, b)
                    wait(sp, x_ready, b * TC)
                    sp.sem_inc(pace, 1)
                    sp.dma_start(x_res[:], src.rearrange("o p k h -> (o p) k h")).then_inc(res_loaded, 16)
                else:
                    dst = of(x_out_b, b)
                    sp.wait_ge(x_ready, b * TC + TC)
                    sp.sem_inc(pace, 1)
                    sp.dma_start(dst.rearrange("o p k h -> (o p) k h"), x_out[:]).then_inc(stored, 16)

            sp.sem_inc(stored, 16)
            batches("sp", sp, lambda t, j, g: None, {
                "norm": norm, "turn": nothing, "x": nothing, "z": nothing, "silu_x": nothing, "silu_z": nothing,
                "ssm": nothing, "turn_ssm": turn_ssm, "dt": nothing, "y": nothing, "out": out})
            sp.wait_ge(stored, 16 * (BATCHES + 1))

        @block.gpsimd
        def _(pool):
            X = nc.gpsimd
            X.memset(ident[:], 0.0).then_inc(consts_ready, 1)
            X.memset(minus_half[:], -0.5).then_inc(consts_ready, 1)
            X.memset(padded[:, :, :, 0:K - 1], 0.0).then_inc(consts_ready, 1)
            pool.wait_ge(consts_ready, 3)
            X.affine_select(out=ident[:], in_=ident[:], compare_op=ALU.not_equal, fill=1.0, base=0,
                            pattern=[[-1, P]], channel_multiplier=1).then_inc(consts_ready, 1)

            def main(t, j, g):
                b, parity = t
                q = b * (DC * G) + (j * G + g)
                if j == 0 and g == 0:
                    pool.wait_ge(B_loaded, b * 16 + 16)
                if g == 0:
                    pool.wait_ge(dt_ready, (b * DC + j) * 2 + 2)
                wait(pool, summed, q - (G - 1))
                a = dtx[:, j % 2, :].rearrange("p (o l) -> p o l", o=1).to_broadcast([P, GN, L])
                X.tensor_tensor(state[:, g, :].rearrange("p (n l) -> p n l", n=GN), a,
                                B_all[:, parity, g * GN:(g + 1) * GN, :], ALU.mult).then_inc(input_ready, 1)

            def norm(t, n):
                b, _ = t
                pool.wait_ge(var_x, b + 1)
                X.tensor_tensor(rstd[:], var_eps[:], minus_half[:, 0:TC], ALU.pow).then_inc(rstd_x, 1)

            def ssm_norm(t, n):
                b, _ = t
                pool.wait_ge(ssm_squares, b + 1)
                X.tensor_tensor(rms_inv[:].rearrange("p k s -> p (k s)"), rms[:].rearrange("p k s -> p (k s)"),
                                minus_half[:], ALU.pow).then_inc(ssm_rms, 1)

            def make_dt(t, j):
                b, parity = t
                n = b * DC + j
                pool.wait_ge(dt_parts, n + 1)
                wait(pool, decay_ready, (n - 1) * G)
                X.tensor_tensor(dt[:, j % 2, :], relu[:], soft[:], ALU.add).then_inc(dt_ready, 1)
                pool.wait_ge(dt_ready, n * 2 + 1)
                X.tensor_tensor(dtx[:, j % 2, :], dt[:, j % 2, :], xc[:, parity, j, :], ALU.mult)\
                    .then_inc(dt_ready, 1)

            def gate_y(t, j):
                b, parity = t
                if j == 0:
                    pool.wait_ge(z_ready, b + 1)
                pool.wait_ge(y_skip, b * DC + j + 1)
                X.tensor_tensor(xc[:, parity, j, :], xc[:, parity, j, :], z[:, parity, j, :], ALU.mult)\
                    .then_inc(y_ready, 1)

            def out(t, n):
                b, _ = t
                pool.wait_ge(var_out, b * TC + n + 1)
                X.tensor_tensor(out_rstd[:], out_var_eps[:], minus_half[:, 0:1], ALU.pow).then_inc(rstd_out, 1)

            batches("pool", pool, main, {
                "norm": norm, "turn": nothing, "x": nothing, "z": nothing, "silu_x": nothing, "silu_z": nothing,
                "ssm": ssm_norm, "turn_ssm": nothing, "dt": make_dt, "y": gate_y, "out": out})

        @block.scalar
        def _(act):
            A = nc.scalar
            exp_and_ln = "natural_log_exp_and_others"
            A.preload_act_table_set(exp_and_ln)
            act.wait_ge(A_in, 16)
            A.activation(A_neg[:], A_neg[:], ACT.Exp).then_inc(A_ready, 1)
            act.wait_ge(A_ready, 1)
            A.mul(A_neg[:], A_neg[:], -1.0).then_inc(A_ready, 1)
            act.wait_ge(A_ready, 2)
            act.wait_ge(small_in, 16 * 9)

            def main(t, j, g):
                b, _ = t
                q = b * (DC * G) + (j * G + g)
                if g == 0:
                    act.wait_ge(dt_ready, (b * DC + j) * 2 + 1)
                wait(act, scanned, q - 1)
                for n in range(GN):
                    last = A.activation(decay[g % 2][:, n, 1:L], dt[:, j % 2, 1:L], ACT.Exp,
                                        scale=A_neg[:, j, g * GN + n:g * GN + n + 1])
                last.then_inc(decay_ready, 1)

            def bank_full(b, task):
                act.wait_ge(front_done, b * NF + FRONT[task] + 1)

            def turn(t, k):
                b, _ = t
                bank_full(b, ("turn", k))
                A.copy(xnT[:, :, k * P:(k + 1) * P], front_bank[:, 0:H].rearrange("p (c n) -> p c n", c=HC))\
                    .then_inc(front_read, 1)

            def x_part(t, i):
                b, parity = t
                bank_full(b, ("x", i))
                if i == 0:
                    wait(act, out_done, (b - 1) * TC)
                wait(act, conv_done, b * (DC // 2) + i - 1)
                for k in range(2):
                    j = 2 * i + k
                    A.activation(xc[:, parity, j, :], front_bank[:, k * L:(k + 1) * L], ACT.Identity,
                                 bias=conv_b[:, j:j + 1], scale=conv_w[:, j, K - 1:K])
                A.copy(padded[:, i % 2, :, K - 1:], front_bank[:, 0:2 * L].rearrange("p (k l) -> p k l", k=2))\
                    .then_inc(front_read, 1)

            def z_part(t, i):
                b, parity = t
                bank_full(b, ("z", i))
                A.copy(z[:, parity, 2 * i:2 * i + 2, :], front_bank[:, 0:2 * L].rearrange("p (k l) -> p k l", k=2))\
                    .then_inc(front_read, 1)

            def silu_x(t, n):
                b, parity = t
                act.wait_ge(conv_done, (b + 1) * (DC // 2))
                A.activation(xc[:, parity, :, :], xc[:, parity, :, :], ACT.Silu).then_inc(xc_ready, 1)
                A.preload_act_table_set(exp_and_ln)

            def silu_z(t, n):
                b, parity = t
                act.wait_ge(front_read, b * NF + NF)
                A.activation(z[:, parity, :, :], z[:, parity, :, :], ACT.Silu).then_inc(z_ready, 1)
                A.preload_act_table_set(exp_and_ln)

            def turn_ssm(t, n):
                b, parity = t
                bank_full(b, ("turn_ssm", 0))
                A.activation(rbcT[:, parity, :], front_bank[0:RBC, 0:L], ACT.Copy, scale=norm_w[:])\
                    .then_inc(front_read, 1)

            def softplus(t, j):
                b, _ = t
                n = b * DC + j
                act.wait_ge(dt_done, n + 1)
                wait(act, dt_ready, n * 2)
                bias = dt_bias[:, j:j + 1]
                A.activation(relu[:], back_bank[:, 0:L], ACT.Relu, bias=bias)
                A.activation(soft[:], back_bank[:, 0:L], ACT.Abs, bias=bias).then_inc(dt_split, 1)
                act.wait_ge(dt_split, n * 3 + 1)
                A.activation(soft[:], soft[:], ACT.Exp, scale=-1.0).then_inc(dt_split, 1)
                act.wait_ge(dt_split, n * 3 + 2)
                A.activation(soft[:], soft[:], ACT.Ln, bias=1.0).then_inc(dt_split, 1)
                act.wait_ge(dt_split, n * 3 + 3)
                act.sem_inc(dt_parts, 1)

            batches("act", act, main, {
                "norm": nothing, "turn": turn, "x": x_part, "z": z_part, "silu_x": silu_x, "silu_z": silu_z,
                "ssm": nothing, "turn_ssm": turn_ssm, "dt": softplus, "y": nothing, "out": nothing})

        @block.vector
        def _(dve):
            V = nc.vector
            after, along, restart = in_order(dve, dve_order)
            for j in range(2):
                after(V.memset(decay[j][:, :, 0:1], 0.0))
            dve.wait_ge(small_in, 16 * 9)
            dve.wait_ge(consts_ready, 4)
            restart()

            def main(t, j, g):
                b, parity = t
                q = b * (DC * G) + (j * G + g)
                if j == 0 and g == 0:
                    dve.wait_ge(C_loaded, b * 16 + 16)
                dve.wait_ge(decay_ready, q + 1)
                dve.wait_ge(input_ready, q + 1)
                V.tensor_tensor_scan(state[:, g, :], decay[g % 2][:].rearrange("p n l -> p (n l)"), state[:, g, :],
                                     0.0, ALU.mult, ALU.add).then_inc(scanned, 1)
                dve.wait_ge(scanned, q + 1)
                V.tensor_tensor(state[:, g, :], state[:, g, :],
                                C_all[:, parity, g * GN:(g + 1) * GN, :].rearrange("p n l -> p (n l)"), ALU.mult)\
                    .then_inc(weighed, 1)

            def norm(t, n):
                b, _ = t
                dve.wait_ge(x_loaded, b * 16 + 16)
                wait(dve, front_done, (b - 1) * NF + TC)
                for k in range(TC):
                    after(V.bn_stats(stat6[:], x_in[:, k, :]))
                    after(V.bn_aggr(mean_var[:, k, :], stat6[:]))
                after(V.tensor_scalar(var_eps[:], mean_var[:, :, 1], LN_EPS, None, ALU.add))
                dve.sem_inc(var_x, 1)
                dve.wait_ge(rstd_x, b + 1)
                for k in range(TC):
                    after(V.tensor_scalar(xn[:, k, :], x_in[:, k, :], mean_var[:, k, 0:1], rstd[:, k:k + 1],
                                          ALU.subtract, ALU.mult))
                dve.sem_inc(xn_ready, 1)

            def x_part(t, i):
                b, parity = t
                dve.wait_ge(front_read, b * NF + FRONT["x", i] + 1)
                dve.sem_inc(pace, 1)
                for k in range(K - 1):
                    for j in (2 * i, 2 * i + 1):
                        after(V.scalar_tensor_tensor(xc[:, parity, j, :], padded[:, i % 2, j % 2, k:k + L],
                                                     conv_w[:, j, k:k + 1], xc[:, parity, j, :], ALU.mult, ALU.add))
                dve.sem_inc(conv_done, 1)

            def ssm_part(t, n):
                b, _ = t
                dve.wait_ge(front_done, b * NF + FRONT["ssm", 0] + 1)
                wait(dve, front_done, (b - 1) * NF + FRONT["turn_ssm", 0] + 1)
                after(V.tensor_copy(ssm[:], front_bank[:, 0:TC * RBC].rearrange("p (k e) -> p k e", k=TC)))
                dve.sem_inc(front_read, 1)
                after(V.tensor_tensor(square[:], ssm[:], ssm[:], ALU.mult))
                after(V.reduce_sum(rms[:], square[:].rearrange("p k (s n) -> p k s n", n=N), AX_X))
                after(V.tensor_tensor(rms[:, :, 0], rms[:, :, 0], rms[:, :, 1], ALU.add))
                after(V.tensor_scalar(rms[:, :, 0], rms[:, :, 0], N / R, None, ALU.mult))
                after(V.tensor_copy(rms[:, :, 1], rms[:, :, 0]))
                after(V.tensor_scalar(rms[:], rms[:], 1.0 / N, RMS_EPS, ALU.mult, ALU.add))
                dve.sem_inc(ssm_squares, 1)
                dve.wait_ge(ssm_rms, b + 1)
                dve.sem_inc(pace, 1)
                scale = rms_inv[:].rearrange("p k (s o) -> p k s o", o=1).to_broadcast([P, TC, 4, N])
                after(V.tensor_tensor(ssm[:].rearrange("p k (s n) -> p k s n", n=N),
                                      ssm[:].rearrange("p k (s n) -> p k s n", n=N), scale, ALU.mult))
                dve.sem_inc(ssm_ready, 1)

            def skip_y(t, j):
                b, parity = t
                dve.wait_ge(summed, b * (DC * G) + (j + 1) * G)
                V.scalar_tensor_tensor(xc[:, parity, j, :], xc[:, parity, j, :], D_skip[:, j:j + 1],
                                       y_bank[j % 2][:, 0:L], ALU.mult, ALU.add).then_inc(y_skip, 1)

            def out(t, k):
                b, _ = t
                dve.wait_ge(out_done, b * TC + k + 1)
                dve.sem_inc(pace, 1)
                after(V.bn_stats(stat6[:], back_bank[:, 0:H]))
                after(V.bn_aggr(out_mean_var[:], stat6[:]))
                after(V.tensor_scalar(out_var_eps[:], out_mean_var[:, 1:2], LN_EPS, None, ALU.add))
                dve.sem_inc(var_out, 1)
                if k == 0:
                    dve.wait_ge(stored, b * 16 + 16)
                dve.wait_ge(rstd_out, b * TC + k + 1)
                dve.sem_inc(pace, 1)
                after(V.tensor_scalar(x_out[:, k, :], back_bank[:, 0:H], out_mean_var[:, 0:1], out_rstd[:],
                                      ALU.subtract, ALU.mult))
                dve.sem_inc(out_read, 1)
                if k == 0:
                    dve.wait_ge(res_loaded, b * 16 + 16)
                after(V.tensor_tensor(x_out[:, k, :], x_out[:, k, :], x_res[:, k, :], ALU.add))
                dve.sem_inc(x_ready, 1)

            batches("dve", dve, main, {
                "norm": norm, "turn": nothing, "x": x_part, "z": nothing, "silu_x": nothing, "silu_z": nothing,
                "ssm": ssm_part, "turn_ssm": nothing, "dt": nothing, "y": skip_y, "out": out, "end": restart})

        @block.tensor
        def _(pe):
            T_ = nc.tensor
            pe.wait_ge(consts_ready, 4)
            pe.wait_ge(small_in, 16 * 9)
            pe.wait_ge(in_proj_in, 16)
            pe.wait_ge(out_proj_in, 16)

            def main(t, j, g):
                b, _ = t
                q = b * (DC * G) + (j * G + g)
                if g == 0:
                    wait(pe, y_skip, b * DC + j - 1)
                pe.wait_ge(weighed, q + 1)
                for n in range(GN):
                    last = T_.matmul(y_bank[j % 2][:, 0:L], ident[:], state[:, g, n * L:(n + 1) * L],
                                     start=(g == 0 and n == 0), stop=(g == G - 1 and n == GN - 1))
                last.then_inc(summed, 1)

            def bank_free(b, task):
                wait(pe, front_read, b * NF + FRONT[task])

            def turn(t, k):
                b, _ = t
                pe.wait_ge(xn_ready, b + 1)
                bank_free(b, ("turn", k))
                for c in range(HC):
                    last = T_.transpose(front_bank[:, c * P:(c + 1) * P], xn[:, k, c * P:(c + 1) * P], ident[:])
                last.then_inc(front_done, 1)

            def project(name, t, i):
                b, _ = t
                bank_free(b, (name, i))
                for k in range(2):
                    col = (2 * i + k + (0 if name == "x" else DC)) * P
                    for c in range(HC):
                        last = T_.matmul(front_bank[:, k * L:(k + 1) * L], in_proj[:, c, col:col + P], xnT[:, c, :],
                                         start=(c == 0), stop=(c == HC - 1))
                last.then_inc(front_done, 1)

            def ssm_part(t, n):
                b, parity = t
                pe.wait_ge(xc_ready, b + 1)
                bank_free(b, ("ssm", 0))
                for k in range(TC):
                    for j in range(DC):
                        last = T_.matmul(front_bank[:, k * RBC:(k + 1) * RBC], xc[:, parity, j, k * P:(k + 1) * P],
                                         x_proj[:, j, :], start=(j == 0), stop=(j == DC - 1))
                last.then_inc(front_done, 1)

            def turn_ssm(t, n):
                b, parity = t
                pe.wait_ge(ssm_ready, b + 1)
                bank_free(b, ("turn_ssm", 0))
                pe.sem_inc(pace, 1)
                for k in range(TC):
                    last = T_.transpose(front_bank[0:RBC, k * P:(k + 1) * P], ssm[:, k, :], ident[:])
                last.then_inc(front_done, 1)

            def dt_part(t, j):
                b, parity = t
                n = b * DC + j
                pe.wait_ge(front_read, b * NF + FRONT["turn_ssm", 0] + 1)
                wait(pe, dt_parts, n)
                if j in (3, 4):
                    wait(pe, out_read, (b - 1) * TC + j - 2)
                T_.matmul(back_bank[:, 0:L], dt_proj[:, j * P:(j + 1) * P], rbcT[0:R, parity, :],
                          start=True, stop=True).then_inc(dt_done, 1)

            def out(t, k):
                b, parity = t
                pe.wait_ge(y_ready, b * DC + DC)
                last_dt = (b + 1) * DC + 3 + k
                if not isinstance(b, int) or b < BATCHES - 1:
                    pe.wait_ge(dt_parts, last_dt)
                else:
                    wait(pe, out_read, b * TC + k)
                for j in range(DC):
                    last = T_.matmul(back_bank[:, 0:H], xc[:, parity, j, k * P:(k + 1) * P], out_proj[:, j, :],
                                     start=(j == 0), stop=(j == DC - 1))
                last.then_inc(out_done, 1)

            batches("pe", pe, main, {
                "norm": nothing, "turn": turn, "x": lambda t, j: project("x", t, j),
                "z": lambda t, j: project("z", t, j), "silu_x": nothing, "silu_z": nothing,
                "ssm": ssm_part, "turn_ssm": turn_ssm, "dt": dt_part, "y": nothing, "out": out})


def gated_lora(nc, io, x_in_dram, x_out_dram):
    tokens, H = x_in_dram.shape
    OUT = io["ffn_w"].shape[1]
    HID, E = io["gw2"].shape
    ER = io["lora_B"].shape[0]
    R = ER // E
    TILES = tokens // P
    HC = H // P
    SIDE = HID + ER
    CAPACITY = int(3.0 * tokens / E)
    ALPHA = 1.0 / R
    LOADS = 4
    PER = 512 // P
    x_in_t = x_in_dram.rearrange("(t p) h -> p t h", p=P)
    x_out_t = x_out_dram.rearrange("(t p) h -> t p h", p=P)
    assert TILES % 2 == 0 and TILES * E * 2 <= 512

    with ExitStack() as ctx:
        def sb(name, shape, dt=F32):
            return ctx.enter_context(nc.sbuf_tensor("d_" + name, shape, dt))

        def bank(name):
            return ctx.enter_context(nc.psum_tensor("d_" + name, [P, 512], F32))

        def sem(name):
            return ctx.enter_context(nc.semaphore("d_" + name))

        ffn_w = sb("ffn_w", [P, HC, OUT])
        side_w = sb("side_w", [P, HC, SIDE])
        lora_B = sb("lora_B", [ER, OUT])
        gw2 = sb("gw2", [HID, E])
        rows = {name: sb(name, [P, n]) for name, n in
                (("gb1", HID), ("ln_gamma", HID), ("ln_beta", HID), ("gb2", E))}
        ident = sb("ident", [P, P])
        ones = sb("ones", [P, P])
        minus_half = sb("minus_half", [P, TILES])
        iota_e = sb("iota_e", [P, TILES, E])
        x_all = sb("x_all", [P, TILES, H])
        main_all = sb("main_all", [P, TILES, OUT])
        side_all = sb("side_all", [P, TILES, SIDE])
        xn = sb("xn", [P, 2, H])
        xnT = sb("xnT", [P, 2, HC, P])
        stat6 = sb("stat6", [P, 6])
        mean_var = sb("mean_var", [P, TILES, 2])
        one_mean_var = sb("one_mean_var", [P, 2])
        var_eps = sb("var_eps", [P, TILES])
        rstd = sb("rstd", [P, TILES])
        hid = sb("hid", [P, TILES, HID])
        hid2 = sb("hid2", [P, TILES, HID])
        hidT = sb("hidT", [HID, TILES, P])
        scores = sb("scores", [P, TILES, E])
        key = sb("key", [P, TILES, E])
        equal = sb("equal", [P, TILES, E])
        best = sb("best", [P, 2, TILES])
        first = sb("first", [P, TILES])
        chosen = sb("chosen", [P, 2, TILES, E])
        share = sb("share", [P, 2, TILES])
        odds = sb("odds", [P, TILES])
        counts = sb("counts", [P, 2, E])
        weight = sb("weight", [P, TILES, E])
        tmp = sb("tmp", [P, 2, ER])
        tmpT = sb("tmpT", [ER, 2, P])

        turn_bank = [bank(f"turn{j}") for j in range(2)]
        main_bank = [bank(f"main{j}") for j in range(2)]
        side_bank = [bank(f"side{j}") for j in range(2)]
        gate_bank = bank("gate")
        count_bank = bank("count")

        x_loaded = [sem(f"x_loaded{j}") for j in range(LOADS)]
        weights_in, rows_in = sem("weights_in"), sem("rows_in")
        consts_ready = sem("consts_ready")
        var_ready, rstd_ready = sem("var_ready"), sem("rstd_ready")
        xn_ready, turned, xnT_ready = sem("xn_ready"), sem("turned"), sem("xnT_ready")
        main_done, main_moved = sem("main_done"), sem("main_moved")
        side_done, side_moved = sem("side_done"), sem("side_moved")
        hid_ready, hid_turned, hidT_ready = sem("hid_ready"), sem("hid_turned"), sem("hidT_ready")
        scores_done, gap_ready, odds_ready = sem("scores_done"), sem("gap_ready"), sem("odds_ready")
        chosen_ready, counted = sem("chosen_ready"), sem("counted")
        weight_ready, tmp_ready = sem("weight_ready"), sem("tmp_ready")
        tmp_turned, tmpT_ready, lora_done, lora_read = (sem("tmp_turned"), sem("tmpT_ready"), sem("lora_done"),
                                                        sem("lora_read"))
        x_ready, stored = sem("x_ready"), sem("stored")
        dve_order = sem("dve_order")
        pace = sem("pace")
        block = ctx.enter_context(nc.Block())

        def pairs(eng, body):
            for k in range(2):
                body(k, 0, k)
            with eng.Fori(1, TILES // 2) as pair:
                for k in range(2):
                    body(pair * 2 + k, pair, k)

        def at(t):
            return t if isinstance(t, int) else bass.ds(t, 1)

        def tile_of(tensor, t):
            return tensor[:, t, :] if isinstance(t, int) else \
                tensor[:, bass.ds(t, 1), :].rearrange("p o n -> p (o n)")

        @block.sync
        def _(sp):
            step = TILES // LOADS
            for j in range(LOADS):
                sp.dma_start(x_all[:, j * step:(j + 1) * step, :], x_in_t[:, j * step:(j + 1) * step, :])\
                    .then_inc(x_loaded[j], 16)
            sp.dma_start(ffn_w[:], io["ffn_w"].rearrange("(c p) o -> p c o", p=P)).then_inc(weights_in, 16)
            sp.dma_start(side_w[:, :, 0:HID], io["gw1"].rearrange("(c p) o -> p c o", p=P)).then_inc(weights_in, 16)
            sp.dma_start(side_w[:, :, HID:], io["lora_A"].rearrange("(c p) o -> p c o", p=P)).then_inc(weights_in, 16)
            sp.dma_start(lora_B[:], io["lora_B"]).then_inc(weights_in, 16)
            sp.dma_start(gw2[:], io["gw2"]).then_inc(weights_in, 16)
            for name, row in rows.items():
                n = row.shape[1]
                sp.dma_start(row[:], io[name].rearrange("(o n) -> o n", o=1).to_broadcast([P, n]))\
                    .then_inc(rows_in, 16)

            def store(t, pair, parity):
                dst = x_out_t[t:t + 1] if isinstance(t, int) else x_out_t[bass.ds(sp.snap(t), 1)]
                src = tile_of(x_all, t if isinstance(t, int) else sp.snap(t))
                sp.wait_ge(x_ready, t + 1)
                sp.sem_inc(pace, 1)
                sp.dma_start(dst.rearrange("o p h -> (o p) h"), src).then_inc(stored, 16)

            pairs(sp, store)
            sp.wait_ge(stored, 16 * TILES)

        @block.gpsimd
        def _(pool):
            X = nc.gpsimd
            X.memset(ident[:], 0.0).then_inc(consts_ready, 1)
            X.memset(minus_half[:], -0.5).then_inc(consts_ready, 1)
            X.memset(ones[:], 1.0).then_inc(consts_ready, 1)
            X.iota(iota_e[:], pattern=[[0, TILES], [1, E]], base=0, channel_multiplier=0,
                   allow_small_or_imprecise_dtypes=True).then_inc(consts_ready, 1)
            pool.wait_ge(consts_ready, 4)
            X.affine_select(out=ident[:], in_=ident[:], compare_op=ALU.not_equal, fill=1.0, base=0,
                            pattern=[[-1, P]], channel_multiplier=1).then_inc(consts_ready, 1)

            def scale(t, pair, parity):
                wait(pool, tmp_turned, t - 1)
                pool.sem_inc(pace, 1)
                w = tile_of(weight, t).rearrange("p (e o) -> p e o", o=1).to_broadcast([P, E, R])
                X.tensor_tensor(tmp[:, parity, :].rearrange("p (e r) -> p e r", e=E),
                                tile_of(side_all, t)[:, HID:].rearrange("p (e r) -> p e r", e=E), w, ALU.mult)\
                    .then_inc(tmp_ready, 1)

            for n in range(3):
                pool.wait_ge(var_ready, n + 1)
                X.tensor_tensor(rstd[:], var_eps[:], minus_half[:], ALU.pow).then_inc(rstd_ready, 1)
                if n == 1:
                    pool.wait_ge(weight_ready, 1)
                    pairs(pool, scale)

        @block.vector
        def _(dve):
            V = nc.vector
            after, along, restart = in_order(dve, dve_order)
            dve.wait_ge(consts_ready, 5)
            dve.wait_ge(rows_in, 64)
            for t in range(TILES):
                if t % (TILES // LOADS) == 0:
                    dve.wait_ge(x_loaded[t // (TILES // LOADS)], 16)
                after(V.bn_stats(stat6[:], x_all[:, t, :]))
                after(V.bn_aggr(mean_var[:, t, :], stat6[:]))
            after(V.tensor_scalar(var_eps[:], mean_var[:, :, 1], LN_EPS, None, ALU.add))
            dve.sem_inc(var_ready, 1)
            dve.wait_ge(rstd_ready, 1)
            restart()

            def normalise(t, pair, parity):
                wait(dve, turned, t - 1)
                V.tensor_scalar(xn[:, parity, :], tile_of(x_all, t), tile_of(mean_var, t)[:, 0:1],
                                rstd[:, at(t)] if not isinstance(t, int) else rstd[:, t:t + 1],
                                ALU.subtract, ALU.mult).then_inc(xn_ready, 1)

            pairs(dve, normalise)

            def spread(a, n):
                return a.rearrange("p (t o) -> p t o", o=1).to_broadcast([P, TILES, n])

            def every(a, n):
                return a.rearrange("p (o n) -> p o n", o=1).to_broadcast([P, TILES, n])

            dve.wait_ge(side_moved, TILES)
            after(V.tensor_tensor(hid[:], side_all[:, :, 0:HID], every(rows["gb1"][:], HID), ALU.add))
            after(V.reduce_sum(first[:], hid[:], AX_X))
            after(V.tensor_scalar(first[:], first[:], 1.0 / HID, None, ALU.mult))
            after(V.tensor_tensor(hid[:], hid[:], spread(first[:], HID), ALU.subtract))
            after(V.tensor_tensor(hid2[:], hid[:], hid[:], ALU.mult))
            after(V.reduce_sum(first[:], hid2[:], AX_X))
            after(V.tensor_scalar(var_eps[:], first[:], 1.0 / HID, LN_EPS, ALU.mult, ALU.add))
            dve.sem_inc(var_ready, 1)
            dve.wait_ge(rstd_ready, 2)
            after(V.tensor_tensor(hid[:], hid[:], spread(rstd[:], HID), ALU.mult))
            after(V.tensor_tensor(hid[:], hid[:], every(rows["ln_gamma"][:], HID), ALU.mult))
            after(V.tensor_tensor(hid[:], hid[:], every(rows["ln_beta"][:], HID), ALU.add))
            after(V.tensor_scalar(hid[:], hid[:], 0.0, None, ALU.max))
            dve.sem_inc(hid_ready, 1)
            dve.wait_ge(scores_done, 1)
            after(V.tensor_tensor(scores[:], gate_bank[:, 0:TILES * E].rearrange("p (t e) -> p t e", e=E),
                                  every(rows["gb2"][:], E), ALU.add))
            for k in range(2):
                after(V.tensor_reduce(best[:, k, :], scores[:], AX_X, ALU.max))
                after(V.tensor_tensor(equal[:], scores[:], spread(best[:, k, :], E), ALU.is_equal))
                after(V.scalar_tensor_tensor(key[:], equal[:], -64.0, iota_e[:], ALU.mult, ALU.add))
                after(V.tensor_reduce(first[:], key[:], AX_X, ALU.min))
                after(V.tensor_tensor(chosen[:, k, :, :], key[:], spread(first[:], E), ALU.is_equal))
                if k == 0:
                    after(V.scalar_tensor_tensor(scores[:], chosen[:, 0, :, :], -3e38, scores[:],
                                                 ALU.mult, ALU.add))
            dve.sem_inc(chosen_ready, 1)
            after(V.tensor_tensor(odds[:], best[:, 1, :], best[:, 0, :], ALU.subtract))
            dve.sem_inc(gap_ready, 1)
            dve.wait_ge(odds_ready, 1)
            after(V.tensor_scalar(share[:, 0, :], odds[:], 1.0, None, ALU.add))
            after(V.reciprocal(share[:, 0, :], share[:, 0, :]))
            after(V.tensor_tensor(share[:, 1, :], odds[:], share[:, 0, :], ALU.mult))
            dve.wait_ge(counted, 1)
            after(V.reduce_sum(counts[:], count_bank[:, 0:2 * TILES * E]
                               .rearrange("p (k t e) -> p k e t", k=2, e=E), AX_X))
            after(V.tensor_scalar(counts[:], counts[:], float(CAPACITY), ALPHA, ALU.is_le, ALU.mult))
            for k in range(2):
                after(V.tensor_tensor(chosen[:, k, :, :], chosen[:, k, :, :], spread(share[:, k, :], E), ALU.mult))
                after(V.tensor_tensor(chosen[:, k, :, :], chosen[:, k, :, :], every(counts[:, k, :], E), ALU.mult))
            after(V.tensor_tensor(weight[:], chosen[:, 0, :, :], chosen[:, 1, :, :], ALU.add))
            dve.sem_inc(weight_ready, 1)
            restart()

            def add_lora(t, pair, parity):
                dve.wait_ge(lora_done, t + 1)
                after(V.tensor_tensor(tile_of(main_all, t), tile_of(main_all, t), main_bank[parity][:, 0:OUT],
                                      ALU.add))
                dve.sem_inc(lora_read, 1)
                after(V.bn_stats(stat6[:], tile_of(main_all, t)))
                after(V.bn_aggr(one_mean_var[:], stat6[:]))
                after(V.tensor_copy(tile_of(mean_var, t), one_mean_var[:]))
                restart()

            dve.wait_ge(main_moved, TILES)
            pairs(dve, add_lora)
            after(V.tensor_scalar(var_eps[:], mean_var[:, :, 1], LN_EPS, None, ALU.add))
            dve.sem_inc(var_ready, 1)
            dve.wait_ge(rstd_ready, 3)
            restart()

            def finish(t, pair, parity):
                after(V.tensor_scalar(tile_of(main_all, t), tile_of(main_all, t), tile_of(mean_var, t)[:, 0:1],
                                      rstd[:, at(t)] if not isinstance(t, int) else rstd[:, t:t + 1],
                                      ALU.subtract, ALU.mult))
                after(V.tensor_tensor(tile_of(x_all, t), tile_of(x_all, t), tile_of(main_all, t), ALU.add))
                dve.sem_inc(x_ready, 1)
                restart()

            pairs(dve, finish)

        @block.scalar
        def _(act):
            A = nc.scalar

            def move(t, pair, parity):
                act.wait_ge(turned, t + 1)
                wait(act, side_done, t - 1)
                act.sem_inc(pace, 1)
                A.copy(xnT[:, parity, :, :], turn_bank[parity][:, 0:H].rearrange("p (c n) -> p c n", c=HC))\
                    .then_inc(xnT_ready, 1)
                act.wait_ge(main_done, t + 1)
                act.sem_inc(pace, 1)
                A.copy(tile_of(main_all, t), main_bank[parity][:, 0:OUT]).then_inc(main_moved, 1)
                act.wait_ge(side_done, t + 1)
                act.sem_inc(pace, 1)
                A.copy(tile_of(side_all, t), side_bank[parity][:, 0:SIDE]).then_inc(side_moved, 1)

            pairs(act, move)
            for r in range(TILES // PER):
                act.wait_ge(hid_turned, r + 1)
                A.copy(hidT[:, r * PER:(r + 1) * PER, :],
                       turn_bank[r % 2][0:HID, :].rearrange("p (t n) -> p t n", n=P)).then_inc(hidT_ready, 1)
            act.wait_ge(gap_ready, 1)
            A.activation(odds[:], odds[:], ACT.Exp).then_inc(odds_ready, 1)

            def move_tmp(t, pair, parity):
                act.wait_ge(tmp_turned, t + 1)
                wait(act, lora_done, t - 1)
                act.sem_inc(pace, 1)
                A.copy(tmpT[:, parity, :], turn_bank[parity][0:ER, 0:P]).then_inc(tmpT_ready, 1)

            pairs(act, move_tmp)

        @block.tensor
        def _(pe):
            T_ = nc.tensor
            pe.wait_ge(consts_ready, 5)
            pe.wait_ge(weights_in, 16 * 5)

            def products(t, pair, parity):
                pe.wait_ge(xn_ready, t + 1)
                wait(pe, xnT_ready, t - 1)
                for c in range(HC):
                    last = T_.transpose(turn_bank[parity][:, c * P:(c + 1) * P], xn[:, parity, c * P:(c + 1) * P],
                                        ident[:])
                last.then_inc(turned, 1)
                pe.wait_ge(xnT_ready, t + 1)
                wait(pe, main_moved, t - 1)
                for c in range(HC):
                    last = T_.matmul(main_bank[parity][:, 0:OUT], xnT[:, parity, c, :], ffn_w[:, c, :],
                                     start=(c == 0), stop=(c == HC - 1))
                last.then_inc(main_done, 1)
                wait(pe, side_moved, t - 1)
                for c in range(HC):
                    last = T_.matmul(side_bank[parity][:, 0:SIDE], xnT[:, parity, c, :], side_w[:, c, :],
                                     start=(c == 0), stop=(c == HC - 1))
                last.then_inc(side_done, 1)

            pairs(pe, products)
            pe.wait_ge(hid_ready, 1)
            for r in range(TILES // PER):
                if r >= 2:
                    pe.wait_ge(hidT_ready, r - 1)
                for k in range(PER):
                    last = T_.transpose(turn_bank[r % 2][0:HID, k * P:(k + 1) * P], hid[:, r * PER + k, :], ident[:])
                last.then_inc(hid_turned, 1)
            pe.wait_ge(hidT_ready, TILES // PER)
            for t in range(TILES):
                last = T_.matmul(gate_bank[:, t * E:(t + 1) * E], hidT[:, t, :], gw2[:], start=True, stop=True)
            last.then_inc(scores_done, 1)
            pe.wait_ge(chosen_ready, 1)
            T_.matmul(count_bank[:, 0:2 * TILES * E], ones[:], chosen[:].rearrange("p k t e -> p (k t e)"),
                      start=True, stop=True).then_inc(counted, 1)

            def lora(t, pair, parity):
                pe.wait_ge(tmp_ready, t + 1)
                wait(pe, tmpT_ready, t - 1)
                T_.transpose(turn_bank[parity][0:ER, 0:P], tmp[:, parity, :], ident[:]).then_inc(tmp_turned, 1)
                pe.wait_ge(tmpT_ready, t + 1)
                wait(pe, lora_read, t - 1)
                T_.matmul(main_bank[parity][:, 0:OUT], tmpT[:, parity, :], lora_B[:], start=True, stop=True)\
                    .then_inc(lora_done, 1)

            pairs(pe, lora)


def _program(nc, io, x, out):
    batches, length, H = x.shape
    after_mlp = nc.dram_tensor("x_after_router", [batches * length, H], F32).ap()
    after_scan = nc.dram_tensor("x_after_scan", [batches * length, H], F32).ap()
    mlp_and_router(nc, io, x.rearrange("b s h -> (b s) h"), after_mlp)
    selective_scan(nc, io, after_mlp.rearrange("(b s) h -> b s h", b=batches),
                   after_scan.rearrange("(b s) h -> b s h", b=batches))
    gated_lora(nc, io, after_scan, out.rearrange("b s h -> (b s) h"))


_AS_IS = {"router_bias": "L0_ffn_router_bias", "expert_bias": "L0_ffn_expert_bias",
          "conv_w": "L1_attn_conv_w", "A_log": "L1_attn_A_log",
          "dt_ln_w": "L1_attn_dt_ln_w", "B_ln_w": "L1_attn_B_ln_w", "C_ln_w": "L1_attn_C_ln_w",
          "in_proj": "L1_attn_in_proj_w",
          "gb1": "L1_ffn_gb1", "ln_gamma": "L1_ffn_ln_gamma", "ln_beta": "L1_ffn_ln_beta", "gb2": "L1_ffn_gb2"}
_COLUMNS = {"conv_b": "L1_attn_conv_b", "dt_bias": "L1_attn_dt_bias", "D_param": "L1_attn_D_param"}
_TURNED = {"w_gate": "L0_attn_w_gate", "w_up": "L0_attn_w_up", "w_down": "L0_attn_w_down",
           "router_w": "L0_ffn_router_weight",
           "x_proj": "L1_attn_x_proj_w", "dt_proj": "L1_attn_dt_proj_w", "out_proj": "L1_attn_out_proj_w",
           "ffn_w": "L1_ffn_weight", "gw1": "L1_ffn_gw1", "gw2": "L1_ffn_gw2"}
def kernel(**inputs):
    import numpy as _np
    import concourse.bacc as _bacc
    from concourse import mybir as _mybir
    from concourse.bass_utils import run_bass_kernel_spmd as _run

    nc = _bacc.Bacc("TRN2", target_bir_lowering=False, num_devices=1)
    arrays = {"x": _np.ascontiguousarray(inputs["L0_attn_x"])}
    for name, source in _AS_IS.items():
        arrays[name] = _np.ascontiguousarray(inputs[source])
    for name, source in _TURNED.items():
        arrays[name] = _np.ascontiguousarray(_np.asarray(inputs[source]).T)
    for name, source in _COLUMNS.items():
        arrays[name] = _np.ascontiguousarray(_np.asarray(inputs[source]).reshape(-1, 128).T)
    lora_a, lora_b = _np.asarray(inputs["L1_ffn_lora_A"]), _np.asarray(inputs["L1_ffn_lora_B"])
    arrays["lora_A"] = _np.ascontiguousarray(lora_a.transpose(1, 0, 2).reshape(lora_a.shape[1], -1))
    arrays["lora_B"] = _np.ascontiguousarray(lora_b.reshape(-1, lora_b.shape[2]))
    io = {name: nc.dram_tensor(name, a.shape, _mybir.dt.from_np(a.dtype), kind="ExternalInput").ap()
          for name, a in arrays.items()}
    x = io.pop("x")
    out = nc.dram_tensor("out", x.shape, _mybir.dt.float32, kind="ExternalOutput").ap()
    _program(nc, io, x, out)
    return _run(nc, [arrays], core_ids=[0]).results[0]["out"]
```

```python
from contextlib import ExitStack

import concourse.bass as bass
from concourse import mybir

P = 128
F32 = mybir.dt.float32
I32 = mybir.dt.int32
ALU = mybir.AluOpType
ACT = mybir.ActivationFunctionType
AX_X = mybir.AxisListType.X
LN_EPS = 1e-5


class Tile:

    def __init__(self, pair, offset):
        self.parity = offset % 2
        self.real = pair is not None or 0 <= offset
        self.n = offset if pair is None else pair * 2 + offset
        self.half = offset // 2 if pair is None else pair + offset // 2
        self.offset = offset
        self.looped = pair is not None

    def below(self, count):
        return self.real and (self.looped or self.offset < count)


def wait(eng, sem, value):
    if not isinstance(value, int) or value > 0:
        eng.wait_ge(sem, value)


def in_order(eng, sem):
    count = [0]

    def along(instruction):
        count[0] += 1
        instruction.then_inc(sem, 1)

    def settle():
        eng.wait_ge(sem, count[0])

    def after(instruction):
        along(instruction)
        settle()

    def restart():
        if count[0]:
            eng.sem_clear(sem)
        count[0] = 0

    return after, along, settle, restart


def steps(eng, body, first, loop_from, loop_pairs, last):
    for s in range(first, loop_from):
        body(lambda d, s=s: Tile(None, s + d))
    with eng.Fori(0, loop_pairs) as pair:
        for k in range(2):
            body(lambda d, k=k: Tile(pair, loop_from + k + d))
    for s in range(loop_from + 2 * loop_pairs, last + 1):
        body(lambda d, s=s: Tile(None, s + d))


def mlp_and_router(nc, io, next_weights, x_in_dram, x_out_dram):
    tokens, H = x_in_dram.shape
    I = io["w_gate"].shape[1]
    E = io["router_w"].shape[1]
    TILES = tokens // P
    HC = H // P
    IC = -(-I // P)
    DROP = I // 2
    TOP = 8
    MIX, DOWN, X, MID = range(4)
    CH = [(c, min(c + 512, I)) for c in range(0, I, 512)]
    NC = len(CH)
    ROUNDS = [range(r, min(r + 4, IC)) for r in range(0, IC, 4)]
    NR = len(ROUNDS)
    GUESS, AROUND, FAR = 0.81, 793.0, 4.0
    SEARCH = ["slope", "slope", "secant", "secant", None]
    x_in_t = x_in_dram.rearrange("(t p) h -> t p h", p=P)
    x_out_t = x_out_dram.rearrange("(t p) h -> t p h", p=P)

    with ExitStack() as ctx:
        def sb(name, shape, dt=F32):
            return ctx.enter_context(nc.sbuf_tensor("a_" + name, shape, dt))

        def bank(name):
            return ctx.enter_context(nc.psum_tensor("a_" + name, [P, 512], F32))

        def sem(name):
            return ctx.enter_context(nc.semaphore("a_" + name))

        w_gate = sb("w_gate", [P, HC, I])
        w_up = sb("w_up", [P, HC, I])
        w_down = sb("w_down", [P, IC, H])
        router_w = sb("router_w", [P, HC, E])
        router_b = sb("router_b", [P, E])
        expert_b = sb("expert_b", [E, H])
        ident = sb("ident", [P, P])
        minus_half = sb("minus_half", [P, 3])
        iota8 = sb("iota8", [P, TOP])
        x_in = sb("x_in", [P, 2, H])
        x_res = sb("x_res", [P, 2, H])
        x_out = sb("x_out", [P, 2, H])
        xn = sb("xn", [P, H])
        xnT = sb("xnT", [P, 2, HC, P])
        gate = sb("gate", [P, 2, I])
        mag = sb("mag", [P, 2, I])
        mag_sum = sb("mag_sum", [P, 2, 1])
        guess = sb("guess", [P, 2, 2])
        minus_guess = sb("minus_guess", [P, 1])
        signs = sb("signs", [P, I])
        sign_sum = sb("sign_sum", [P, 1])
        up = sb("up", [P, 2, I])
        work = sb("work", [P, I])
        act = sb("act", [P, IC * P])
        actT = sb("actT", [P, IC, P])
        mix_normed = sb("mix_normed", [P, H])
        normed = sb("normed", [P, H])
        x_mid = sb("x_mid", [P, 2, H])
        xn2 = sb("xn2", [P, 2, H])
        xn2T = sb("xn2T", [P, HC, P])
        mix = sb("mix", [P, H])
        logits = sb("logits", [P, E])
        logit8 = sb("logit8", [P, TOP])
        neg_max = sb("neg_max", [P, 1])
        probs = sb("probs", [P, E])
        prob_sum = sb("prob_sum", [P, 1])
        prob8 = sb("prob8", [P, TOP])
        prob8_sum = sb("prob8_sum", [P, 1])
        dense = sb("dense", [P, E])
        denseT = sb("denseT", [E, P])
        stat6 = sb("stat6", [P, 4, 6])
        mean_var = sb("mean_var", [P, 4, 2])
        var_eps = sb("var_eps", [P, 4])
        rstd = sb("rstd", [P, 4])
        place = [sb(f"place{j}", [P, 2]) for j in range(2)]
        lo = sb("lo", [P, 2])
        hi = sb("hi", [P, 2])
        gap = sb("gap", [P, 2])
        slope = sb("slope", [P, 1])
        low = sb("low", [P, 1])
        far = sb("far", [P, 1])
        short = sb("short", [P, 1])
        top8 = sb("top8", [P, TOP])
        rank = sb("rank", [P, 1])
        cut = sb("cut", [P, 1])
        above = sb("above", [P, 1])
        many = sb("many", [P, 1])
        open_row = sb("open_row", [P, 1])
        any_open = sb("any_open", [P, 1])
        any_open_int = sb("any_open_int", [P, 1], I32)
        bit = sb("bit", [P, 1], I32)
        found = sb("found", [P, 1], I32)
        trial = sb("trial", [P, 1], I32)
        take = sb("take", [P, 1], I32)

        mm = [bank(f"mm{j}") for j in range(2)]
        tp = [bank(f"tp{j}") for j in range(2)]
        xt_bank = bank("xt_bank")
        down_bank = bank("down_bank")
        pick_bank = bank("pick_bank")
        mix_bank = bank("mix_bank")

        gate_in = [sem(f"gate_in{j}") for j in range(NC)]
        up_in, down_in, router_in = sem("up_in"), sem("down_in"), sem("router_in")
        consts_ready = sem("consts_ready")
        x_loaded = [sem(f"x_loaded{j}") for j in range(2)]
        res_loaded = [sem(f"res_loaded{j}") for j in range(2)]
        stored = [sem(f"stored{j}") for j in range(2)]
        vars_ready, rstds_ready = sem("vars_ready"), sem("rstds_ready")
        mid_var, mid_rstd = sem("mid_var"), sem("mid_rstd")
        mix_normed_ready = sem("mix_normed_ready")
        xn_ready = sem("xn_ready")
        xnT_done, xnT_copied = sem("xnT_done"), sem("xnT_copied")
        mm_done, mm_moved = sem("mm_done"), sem("mm_moved")
        mag_ready, guess_parts, guess_ready = sem("mag_ready"), sem("guess_parts"), sem("guess_ready")
        product_ready = sem("product_ready")
        open_ready, open_known = sem("open_ready"), sem("open_known")
        act_ready = sem("act_ready")
        actT_done, actT_copied = sem("actT_done"), sem("actT_copied")
        down_done, down_read = sem("down_done"), sem("down_read")
        x_mid_ready = sem("x_mid_ready")
        xn2_ready = sem("xn2_ready")
        xn2T_done, xn2T_copied = sem("xn2T_done"), sem("xn2T_copied")
        logits_done, logits_ready, probs_ready = sem("logits_done"), sem("logits_ready"), sem("probs_ready")
        dense_ready, denseT_done, denseT_copied = sem("dense_ready"), sem("denseT_done"), sem("denseT_copied")
        mix_done, mix_read = sem("mix_done"), sem("mix_read")
        x_ready = sem("x_ready")
        dve_order, pool_order = sem("dve_order"), sem("pool_order")
        pace = sem("pace")
        block = ctx.enter_context(nc.Block())
        SPAN = (-2, 5, (TILES - 8) // 2, TILES + 2)
        assert TILES % 2 == 0 and TILES >= 10

        @block.sync
        def _(sp):
            def load_x(t):
                if t.below(TILES):
                    src = x_in_t[bass.ds(sp.snap(t.n), 1)] if t.looped else x_in_t[t.n:t.n + 1]
                    wait(sp, xn_ready, t.n - 1)
                    sp.sem_inc(pace, 1)
                    sp.dma_start(x_in[:, t.parity, :], src.rearrange("o p h -> (o p) h"))\
                        .then_inc(x_loaded[t.parity], 16)

            def load_res(t):
                if t.below(TILES):
                    src = x_in_t[bass.ds(sp.snap(t.n), 1)] if t.looped else x_in_t[t.n:t.n + 1]
                    wait(sp, x_mid_ready, t.n - 1)
                    sp.sem_inc(pace, 1)
                    sp.dma_start(x_res[:, t.parity, :], src.rearrange("o p h -> (o p) h"))\
                        .then_inc(res_loaded[t.parity], 16)

            def store_x(t):
                if t.below(TILES):
                    dst = x_out_t[bass.ds(sp.snap(t.n), 1)] if t.looped else x_out_t[t.n:t.n + 1]
                    sp.wait_ge(x_ready, t.n + 1)
                    sp.sem_inc(pace, 1)
                    sp.dma_start(dst.rearrange("o p h -> (o p) h"), x_out[:, t.parity, :])\
                        .then_inc(stored[t.parity], 16)

            load_x(Tile(None, 0))
            load_x(Tile(None, 1))
            for j, (a, b) in enumerate(CH):
                sp.dma_start(w_gate[:, :, a:b], io["w_gate"][:, a:b].rearrange("(c p) i -> p c i", p=P))\
                    .then_inc(gate_in[j], 16)
            sp.dma_start(w_up[:], io["w_up"].rearrange("(c p) i -> p c i", p=P)).then_inc(up_in, 16)
            sp.wait_ge(consts_ready, 4)
            whole = I // P * P
            sp.dma_start(w_down[:, 0:I // P, :], io["w_down"][0:whole, :].rearrange("(c p) h -> p c h", p=P))\
                .then_inc(down_in, 16)
            sp.dma_start(w_down[0:I - whole, IC - 1, :], io["w_down"][whole:I, :]).then_inc(down_in, 16)
            sp.dma_start(router_w[:], io["router_w"].rearrange("(c p) e -> p c e", p=P)).then_inc(router_in, 16)
            sp.dma_start(router_b[:], io["router_bias"].rearrange("(o e) -> o e", o=1).to_broadcast([P, E]))\
                .then_inc(router_in, 16)
            sp.dma_start(expert_b[:], io["expert_bias"]).then_inc(router_in, 16)
            next_weights.load(sp)

            def step(tile):
                if tile(3).looped or tile(3).n >= 2:
                    load_x(tile(3))
                load_res(tile(0))
                store_x(tile(-3))

            steps(sp, step, *SPAN)
            for parity in range(2):
                sp.wait_ge(stored[parity], 16 * (TILES // 2))

        @block.gpsimd
        def _(pool):
            nc.gpsimd.memset(ident[:], 0.0).then_inc(consts_ready, 1)
            nc.gpsimd.memset(minus_half[:], -0.5).then_inc(consts_ready, 1)
            nc.gpsimd.memset(w_down[:, IC - 1, :], 0.0).then_inc(consts_ready, 1)
            nc.gpsimd.memset(act[:, I:IC * P], 0.0).then_inc(consts_ready, 1)
            pool.wait_ge(consts_ready, 4)
            nc.gpsimd.affine_select(out=ident[:], in_=ident[:], compare_op=ALU.not_equal, fill=1.0, base=0,
                                    pattern=[[-1, P]], channel_multiplier=1).then_inc(consts_ready, 1)
            nc.gpsimd.iota(iota8[:], pattern=[[1, TOP]], base=0, channel_multiplier=0,
                           allow_small_or_imprecise_dtypes=True).then_inc(consts_ready, 1)
            pool.wait_ge(consts_ready, 6)

            def gate_up(t):
                if t.below(TILES):
                    pool.wait_ge(mm_moved, t.n * (2 * NC) + 2 * NC)
                    pool.sem_inc(pace, 1)
                    nc.gpsimd.tensor_tensor(up[:, t.parity, :], gate[:, t.parity, :], up[:, t.parity, :], ALU.mult)\
                        .then_inc(product_ready, 1)

            def inverse_roots(t):
                pool.wait_ge(vars_ready, t.n + 3)
                nc.gpsimd.tensor_tensor(rstd[:, 0:3], var_eps[:, 0:3], minus_half[:], ALU.pow)\
                    .then_inc(rstds_ready, 1)

            def inverse_root_mid(t):
                if t.below(TILES):
                    pool.wait_ge(mid_var, t.n + 1)
                    nc.gpsimd.tensor_tensor(rstd[:, MID:MID + 1], var_eps[:, MID:MID + 1], minus_half[:, 0:1],
                                            ALU.pow).then_inc(mid_rstd, 1)

            def add_mix(t):
                if t.below(TILES):
                    pool.wait_ge(mix_normed_ready, t.n + 1)
                    wait(pool, stored[t.parity], t.half * 16)
                    pool.sem_inc(pace, 1)
                    nc.gpsimd.tensor_tensor(x_out[:, t.parity, :], x_mid[:, t.parity, :], mix_normed[:], ALU.add)\
                        .then_inc(x_ready, 1)

            def any_row(t):
                if t.below(TILES):
                    pool.wait_ge(open_ready, t.n + 1)
                    pool.sem_inc(pace, 1)
                    nc.gpsimd.partition_all_reduce(any_open[:], open_row[:], P, bass.bass_isa.ReduceOp.max)\
                        .then_inc(pool_order, 1)
                    pool.wait_ge(pool_order, 1)
                    nc.gpsimd.tensor_copy(any_open_int[:], any_open[:]).then_inc(open_known, 1)
                    pool.sem_clear(pool_order)

            def step(tile):
                gate_up(tile(0))
                any_row(tile(0))
                inverse_roots(tile(0))
                add_mix(tile(-3))
                inverse_root_mid(tile(-1))

            steps(pool, step, *SPAN)

        @block.vector
        def _(dve):
            after, along, settle, restart = in_order(dve, dve_order)
            V = nc.vector
            dve.wait_ge(consts_ready, 6)
            after(V.memset(mean_var[:], 0.0))
            restart()

            def statistics(*sources):
                for which, src in sources:
                    along(V.bn_stats(stat6[:, which, :], src))
                settle()
                for which, _ in sources:
                    along(V.bn_aggr(mean_var[:, which, :], stat6[:, which, :]))
                settle()

            def apply(out, src, which):
                after(V.tensor_scalar(out, src, mean_var[:, which, 0:1], rstd[:, which:which + 1],
                                      ALU.subtract, ALU.mult))

            def make_mix(t):
                dve.wait_ge(mix_done, t.n + 1)
                after(V.scalar_tensor_tensor(mix[:], xn2[:, t.parity, :], prob8_sum[:], mix_bank[:, 0:H],
                                             ALU.mult, ALU.add))
                dve.sem_inc(mix_read, 1)

            def residual(t):
                apply(normed[:], down_bank[:, 0:H], DOWN)
                dve.sem_inc(down_read, 1)
                dve.wait_ge(res_loaded[t.parity], t.half * 16 + 16)
                wait(dve, x_ready, t.n - 1)
                dve.sem_inc(pace, 1)
                after(V.tensor_tensor(x_mid[:, t.parity, :], normed[:], x_res[:, t.parity, :], ALU.add))
                dve.sem_inc(x_mid_ready, 1)
                statistics((MID, x_mid[:, t.parity, :]))
                after(V.tensor_scalar(var_eps[:, MID:MID + 1], mean_var[:, MID, 1:2], LN_EPS, None, ALU.add))
                dve.sem_inc(mid_var, 1)

            def second_norm(t):
                dve.wait_ge(mid_rstd, t.n + 1)
                dve.sem_inc(pace, 1)
                apply(xn2[:, t.parity, :], x_mid[:, t.parity, :], MID)
                dve.sem_inc(xn2_ready, 1)

            def search(t):
                m = mag[:, t.parity, :]
                target = DROP + 3.5
                dve.wait_ge(guess_ready, t.n + 1)
                along(V.memset(lo[:], 0.0))
                along(V.memset(hi[:, 1:2], float(I)))
                along(V.tensor_scalar(hi[:, 0:1], mag_sum[:, t.parity, :], FAR / I, None, ALU.mult))
                after(V.tensor_scalar(slope[:], mag_sum[:, t.parity, :], 1.0 / (I * AROUND), None, ALU.mult))
                for n, move in enumerate(SEARCH):
                    at, to = place[n % 2], place[(n + 1) % 2]
                    if n == 0:
                        at = guess[:, t.parity, :]
                    else:
                        after(V.tensor_scalar(work[:], m, at[:, 0:1], 0.0, ALU.is_le, ALU.add,
                                              accum_out=at[:, 1:2]))
                    along(V.tensor_scalar(low[:], at[:, 1:2], float(DROP), None, ALU.is_lt))
                    if move == "slope":
                        along(V.tensor_scalar(short[:], at[:, 1:2], -1.0, target, ALU.mult, ALU.add))
                    after(V.tensor_scalar(far[:], at[:, 1:2], float(DROP), 1e30, ALU.is_lt, ALU.mult))
                    if move == "slope":
                        along(V.scalar_tensor_tensor(to[:, 0:1], short[:], slope[:], at[:, 0:1], ALU.mult, ALU.add))
                    if move:
                        along(V.scalar_tensor_tensor(lo[:], at[:, 0:2], low[:], lo[:], ALU.mult, ALU.max))
                    after(V.scalar_tensor_tensor(hi[:], at[:, 0:2], far[:], hi[:], ALU.add, ALU.min))
                    if move == "slope":
                        after(V.tensor_scalar(to[:, 0:1], to[:, 0:1], lo[:, 0:1], hi[:, 0:1], ALU.max, ALU.min))
                    elif move == "secant":
                        along(V.tensor_scalar(short[:], lo[:, 1:2], -1.0, target, ALU.mult, ALU.add))
                        after(V.tensor_tensor(gap[:], hi[:], lo[:], ALU.subtract))
                        after(V.reciprocal(slope[:], gap[:, 1:2]))
                        after(V.scalar_tensor_tensor(short[:], short[:], slope[:], gap[:, 0:1], ALU.mult, ALU.mult))
                        after(V.scalar_tensor_tensor(to[:, 0:1], short[:], lo[:, 0:1], hi[:, 0:1], ALU.add, ALU.min))
                along(V.tensor_scalar(rank[:], hi[:, 1:2], float(DROP), None, ALU.subtract))
                along(V.tensor_scalar(many[:], hi[:, 1:2], float(DROP + TOP - 1), None, ALU.is_gt))
                after(V.scalar_tensor_tensor(work[:], m, hi[:, 0:1], m, ALU.is_le, ALU.mult))
                after(V.max(top8[:], work[:]))
                after(V.scalar_tensor_tensor(logit8[:], iota8[:], rank[:], top8[:], ALU.is_equal, ALU.mult,
                                             accum_out=cut[:]))
                after(V.tensor_scalar(logit8[:], top8[:], cut[:], 0.0, ALU.is_gt, ALU.add, accum_out=above[:]))
                after(V.scalar_tensor_tensor(open_row[:], above[:], rank[:], many[:], ALU.not_equal, ALU.max))
                dve.sem_inc(open_ready, 1)

            def bitwise_search(t):
                m = mag[:, t.parity, :]

                def done(instruction):
                    dve.drain()

                done(V.memset(found[:], 0))
                done(V.memset(bit[:], 1 << 30))
                with dve.Fori(0, 31) as _:
                    done(V.tensor_tensor(trial[:], found[:], bit[:], ALU.bitwise_or))
                    done(V.tensor_scalar(work[:], m, trial[:].bitcast(F32), 0.0, ALU.is_lt, ALU.add,
                                         accum_out=above[:]))
                    done(V.tensor_scalar(take[:], above[:], float(DROP), None, ALU.is_lt))
                    done(V.copy_predicated(found[:], take[:], trial[:]))
                    done(V.tensor_scalar(bit[:], bit[:], 1, None, ALU.logical_shift_right))
                cut_bits = found[:].bitcast(F32)
                done(V.tensor_scalar(work[:], m, cut_bits, 0.0, ALU.is_lt, ALU.add, accum_out=above[:]))
                done(V.tensor_scalar(rank[:], above[:], -1.0, float(DROP), ALU.mult, ALU.add))
                done(V.tensor_scalar(work[:], m, cut_bits, None, ALU.is_equal))
                done(V.tensor_tensor_scan(act[:, 0:I], work[:], work[:], 0.0, ALU.add, ALU.bypass))
                done(V.scalar_tensor_tensor(work[:], act[:, 0:I], rank[:], work[:], ALU.is_gt, ALU.mult))
                done(V.scalar_tensor_tensor(work[:], m, cut_bits, work[:], ALU.is_gt, ALU.add))
                done(V.tensor_tensor(act[:, 0:I], work[:], up[:, t.parity, :], ALU.mult))

            def activate(t):
                dve.wait_ge(open_known, t.n + 1)
                wait(dve, actT_done, t.n * NR)
                dve.wait_ge(product_ready, t.n + 1)
                dve.sem_inc(pace, 1)
                along(V.scalar_tensor_tensor(act[:, 0:I], mag[:, t.parity, :], cut[:], up[:, t.parity, :],
                                             ALU.is_gt, ALU.mult))
                rows_open = V.value_load(any_open_int[0:1, 0:1])
                with dve.If(rows_open > 0):
                    settle()
                    bitwise_search(t)
                settle()
                dve.sem_inc(act_ready, 1)

            def shift_logits(t):
                if not t.looped and t.n == 0:
                    dve.wait_ge(router_in, 48)
                dve.wait_ge(logits_done, t.n + 1)
                after(V.tensor_tensor(logits[:], pick_bank[:, 0:E], router_b[:], ALU.add))
                after(V.max(logit8[:], logits[:]))
                after(V.tensor_scalar(neg_max[:], logit8[:, 0:1], -1.0, None, ALU.mult))
                dve.sem_inc(logits_ready, 1)

            def choose(t):
                dve.wait_ge(probs_ready, t.n + 1)
                dve.sem_inc(pace, 1)
                after(V.reciprocal(prob_sum[:], prob_sum[:]))
                after(V.tensor_scalar(probs[:], probs[:], prob_sum[:], None, ALU.mult))
                after(V.max(prob8[:], probs[:]))
                along(V.reduce_sum(prob8_sum[:], prob8[:], AX_X))
                after(V.match_replace(dense[:], prob8[:], probs[:], 0.0))
                after(V.tensor_tensor(dense[:], probs[:], dense[:], ALU.subtract))
                dve.sem_inc(dense_ready, 1)

            def step(tile):
                new, now, old, older, oldest = (tile(d) for d in (2, 0, -1, -2, -3))
                if now.below(TILES):
                    search(now)
                sources = []
                if oldest.below(TILES):
                    make_mix(oldest)
                    sources.append((MIX, mix[:]))
                if old.below(TILES):
                    dve.wait_ge(down_done, old.n + 1)
                    dve.sem_inc(pace, 1)
                    sources.append((DOWN, down_bank[:, 0:H]))
                if new.below(TILES):
                    dve.wait_ge(x_loaded[new.parity], new.half * 16 + 16)
                    sources.append((X, x_in[:, new.parity, :]))
                statistics(*sources)
                after(V.tensor_scalar(var_eps[:, 0:3], mean_var[:, 0:3, 1], LN_EPS, None, ALU.add))
                dve.sem_inc(vars_ready, 1)
                if older.below(TILES):
                    shift_logits(older)
                dve.wait_ge(rstds_ready, now.n + 3)
                dve.sem_inc(pace, 1)
                if oldest.below(TILES):
                    wait(dve, x_ready, oldest.n)
                    dve.sem_inc(pace, 1)
                    apply(mix_normed[:], mix[:], MIX)
                    dve.sem_inc(mix_normed_ready, 1)
                if new.below(TILES):
                    wait(dve, xnT_done, new.n)
                    dve.sem_inc(pace, 1)
                    apply(xn[:], x_in[:, new.parity, :], X)
                    dve.sem_inc(xn_ready, 1)
                if old.below(TILES):
                    residual(old)
                if now.below(TILES):
                    activate(now)
                if old.below(TILES):
                    second_norm(old)
                if older.below(TILES):
                    choose(older)
                restart()

            steps(dve, step, *SPAN)

        @block.scalar
        def _(act_eng):
            A = nc.scalar

            def move_xnT(t):
                if t.below(TILES):
                    act_eng.wait_ge(xnT_done, t.n + 1)
                    A.copy(xnT[:, t.parity, :, :], xt_bank[:, 0:H].rearrange("p (c n) -> p c n", c=HC))\
                        .then_inc(xnT_copied, 1)

            def gate_part(t):
                if not t.below(TILES):
                    return
                wait(act_eng, act_ready, t.n - 1)
                for j, (a, b) in enumerate(CH):
                    act_eng.wait_ge(mm_done, t.n * (2 * NC) + j + 1)
                    A.activation(gate[:, t.parity, a:b], mm[j % 2][:, 0:b - a], ACT.Silu).then_inc(mm_moved, 1)
                act_eng.wait_ge(mm_moved, t.n * (2 * NC) + NC)
                A.activation(mag[:, t.parity, :], gate[:, t.parity, :], ACT.Abs,
                             accum_out=mag_sum[:, t.parity, :]).then_inc(mag_ready, 1)
                act_eng.wait_ge(mag_ready, t.n + 1)
                A.activation(guess[:, t.parity, 0:1], mag_sum[:, t.parity, :], ACT.Copy, scale=GUESS / I)
                A.activation(minus_guess[:], mag_sum[:, t.parity, :], ACT.Copy, scale=-GUESS / I)\
                    .then_inc(guess_parts, 1)
                act_eng.wait_ge(guess_parts, t.n * 2 + 1)
                A.activation(signs[:], mag[:, t.parity, :], ACT.Sign, bias=minus_guess[:], accum_out=sign_sum[:])\
                    .then_inc(guess_parts, 1)
                act_eng.wait_ge(guess_parts, t.n * 2 + 2)
                A.activation(guess[:, t.parity, 1:2], sign_sum[:], ACT.Copy, scale=-0.5, bias=I / 2 + 0.25)\
                    .then_inc(guess_ready, 1)

            def up_part(t, parts):
                if not t.below(TILES):
                    return
                for j in parts:
                    a, b = CH[j]
                    act_eng.wait_ge(mm_done, t.n * (2 * NC) + NC + j + 1)
                    A.copy(up[:, t.parity, a:b], mm[(NC + j) % 2][:, 0:b - a]).then_inc(mm_moved, 1)

            def move_xn2T(t):
                if t.below(TILES):
                    act_eng.wait_ge(xn2T_done, t.n + 1)
                    A.copy(xn2T[:], xt_bank[:, 0:H].rearrange("p (c n) -> p c n", c=HC)).then_inc(xn2T_copied, 1)

            def exponentials(t):
                if t.below(TILES):
                    act_eng.wait_ge(logits_ready, t.n + 1)
                    A.activation(probs[:], logits[:], ACT.Exp, bias=neg_max[:], accum_out=prob_sum[:])\
                        .then_inc(probs_ready, 1)

            def move_actT(t):
                if t.below(TILES):
                    wait(act_eng, down_done, t.n)
                    for r, blocks in enumerate(ROUNDS):
                        act_eng.wait_ge(actT_done, t.n * NR + r + 1)
                        src = tp[(t.parity * NR + r) % 2][:, 0:len(blocks) * P]
                        A.copy(actT[:, blocks[0]:blocks[-1] + 1, :], src.rearrange("p (c n) -> p c n", n=P))\
                            .then_inc(actT_copied, 1)

            def move_denseT(t):
                if t.below(TILES):
                    act_eng.wait_ge(denseT_done, t.n + 1)
                    A.copy(denseT[:], pick_bank[0:E, 0:P]).then_inc(denseT_copied, 1)

            def step(tile):
                move_xn2T(tile(-2))
                gate_part(tile(1))
                up_part(tile(1), range(0, 1))
                exponentials(tile(-2))
                up_part(tile(1), range(1, NC))
                move_actT(tile(0))
                move_denseT(tile(-2))
                move_xnT(tile(2))

            steps(act_eng, step, *SPAN)

        @block.tensor
        def _(pe):
            T_ = nc.tensor
            pe.wait_ge(consts_ready, 6)

            def turn_x(t):
                if t.below(TILES):
                    pe.wait_ge(xn_ready, t.n + 1)
                    for c in range(HC):
                        last = T_.transpose(xt_bank[:, c * P:(c + 1) * P], xn[:, c * P:(c + 1) * P], ident[:])
                    last.then_inc(xnT_done, 1)

            def project(t, w, first):
                if not t.below(TILES):
                    return
                if first == 0:
                    pe.wait_ge(xnT_copied, t.n + 1)
                for j, (a, b) in enumerate(CH):
                    if not t.looped and t.n == 0 and (first == 0 or j == 0):
                        pe.wait_ge(gate_in[j] if first == 0 else up_in, 16)
                    wait(pe, mm_moved, t.n * (2 * NC) + first + j - 1)
                    for c in range(HC):
                        last = T_.matmul(mm[(first + j) % 2][:, 0:b - a], xnT[:, t.parity, c, :], w[:, c, a:b],
                                         start=(c == 0), stop=(c == HC - 1))
                    last.then_inc(mm_done, 1)

            def turn_x2(t):
                if t.below(TILES):
                    pe.wait_ge(xn2_ready, t.n + 1)
                    pe.wait_ge(xnT_copied, min(t.n + 4, TILES) if not t.looped else t.n + 4)
                    for c in range(HC):
                        last = T_.transpose(xt_bank[:, c * P:(c + 1) * P], xn2[:, t.parity, c * P:(c + 1) * P], ident[:])
                    last.then_inc(xn2T_done, 1)

            def route(t):
                if t.below(TILES):
                    if not t.looped and t.n == 0:
                        pe.wait_ge(router_in, 48)
                    pe.wait_ge(xn2T_copied, t.n + 1)
                    wait(pe, denseT_copied, t.n)
                    for c in range(HC):
                        last = T_.matmul(pick_bank[:, 0:E], xn2T[:, c, :], router_w[:, c, :],
                                         start=(c == 0), stop=(c == HC - 1))
                    last.then_inc(logits_done, 1)

            def turn_act_and_down(t):
                def turn_act(r):
                    wait(pe, actT_copied, t.n * NR + r - 1)
                    for k, c in enumerate(ROUNDS[r]):
                        last = T_.transpose(tp[(t.parity * NR + r) % 2][:, k * P:(k + 1) * P],
                                            act[:, c * P:(c + 1) * P], ident[:])
                    last.then_inc(actT_done, 1)

                if t.below(TILES):
                    pe.wait_ge(act_ready, t.n + 1)
                    turn_act(0)
                    turn_act(1)
                    if not t.looped and t.n == 0:
                        pe.wait_ge(down_in, 32)
                    wait(pe, down_read, t.n)
                    for r, blocks in enumerate(ROUNDS):
                        pe.wait_ge(actT_copied, t.n * NR + r + 1)
                        for c in blocks:
                            last = T_.matmul(down_bank[:, 0:H], actT[:, c, :], w_down[:, c, :],
                                             start=(c == 0), stop=(c == IC - 1))
                        if r + 2 < NR:
                            turn_act(r + 2)
                    last.then_inc(down_done, 1)

            def turn_dense(t):
                if t.below(TILES):
                    pe.wait_ge(dense_ready, t.n + 1)
                    pe.sem_inc(pace, 1)
                    T_.transpose(pick_bank[0:E, 0:P], dense[:], ident[:]).then_inc(denseT_done, 1)

            def mix_experts(t):
                if t.below(TILES):
                    pe.wait_ge(denseT_copied, t.n + 1)
                    wait(pe, mix_read, t.n)
                    T_.matmul(mix_bank[:, 0:H], denseT[:], expert_b[:], start=True, stop=True)\
                        .then_inc(mix_done, 1)

            def step(tile):
                turn_x2(tile(-2))
                project(tile(1), w_gate, 0)
                route(tile(-2))
                project(tile(1), w_up, NC)
                turn_act_and_down(tile(0))
                turn_dense(tile(-2))
                turn_x(tile(2))
                mix_experts(tile(-2))

            steps(pe, step, *SPAN)


class InProjection:

    def __init__(self, nc, ctx, weights):
        self.weights = weights
        rows, self.columns = weights.shape
        self.sbuf = ctx.enter_context(nc.sbuf_tensor("c_in_proj", [P, rows // P, self.columns], F32))
        self.z_in = ctx.enter_context(nc.semaphore("z_weights_in"))
        self.x_in = ctx.enter_context(nc.semaphore("x_weights_in"))

    def load(self, sp):
        half = self.columns // 2
        for cols, loaded in ((slice(0, half), self.x_in), (slice(half, 2 * half), self.z_in)):
            sp.dma_start(self.sbuf[:, :, cols], self.weights[:, cols].rearrange("(c p) d -> p c d", p=P))\
                .then_inc(loaded, 16)


def selective_scan(nc, io, projection, x_in_dram, x_out_dram):
    BATCHES, L, H = x_in_dram.shape
    D = projection.columns // 2
    N = io["A_log"].shape[1]
    K = io["conv_w"].shape[1]
    R = io["dt_proj"].shape[0]
    RBC = R + 2 * N
    HC, DC, TC = H // P, D // P, L // P
    G = 4
    GN = N // G
    GL = GN * L
    RMS_EPS = 1e-6
    PLAN = {
        0: [("out_part", 0), ("norm", 0)], 1: [("dt", 2), ("out_part", 1), ("y", -1), ("norm_apply", 0)],
        2: [("out_part", 2), ("turn", 0)], 3: [("out", 0), ("turn", 1)], 4: [("z_first", 0)],
        5: [("dt", 3), ("z", 0), ("y", 0), ("out_apply", 0)], 6: [("out_part", 4)], 7: [("out_part", 5)],
        8: [("x_first", 0)], 9: [("dt", 4), ("x", 0), ("y", 1)],
        11: [("convolve_first", 0), ("x_first", 1), ("x", 1)], 12: [("out_part", 6), ("convolve", 0)],
        13: [("out", 1), ("convolve_first", 1), ("dt", 5), ("x_first", 2), ("y", 2)],
        14: [("x", 2), ("convolve", 1)], 15: [("x_first", 3), ("x", 3)],
        16: [("convolve_first", 2), ("z_first", 1), ("convolve", 2)],
        17: [("convolve_first", 3), ("dt", 6), ("z", 1), ("y", 3)], 18: [("silu_x", 0), ("convolve", 3)],
        19: [("ssm_first", 0), ("out_apply", 1)], 20: [("ssm", 0)], 21: [("dt", 7), ("z_first", 2), ("y", 4)],
        22: [("z", 2)], 23: [("ssm_apply", 0)], 24: [("turn_ssm", 0)],
        25: [("dt", 8), ("z_first", 3), ("y", 5)], 26: [("z", 3)], 29: [("dt", 9), ("y", 6)],
        31: [("silu_z", 0)],
    }
    SLOTS = DC * G
    AHEAD = {"pool": 3, "act": 2, "dve": 0, "pe": 0, "sp": 0}
    BEHIND = {"act": {"turn": 1, "z": 1, "turn_ssm": 1, "dt": 1}, "dve": {"ssm": 1, "out": 1},
              "pool": {"ssm": 1, "out": 2, "dt": 1}, "pe": {}, "sp": {}}
    assert DC == 8 and TC == 2 and N % G == 0
    TASKS = {engine: [[] for _ in range(SLOTS)] for engine in AHEAD}
    for engine, behind in BEHIND.items():
        for slot, planned in PLAN.items():
            for name, n in planned:
                TASKS[engine][slot + behind.get(name, 0)].append((name, n))
    front = [task for slot in range(SLOTS) for task in PLAN.get(slot, [])
             if task[0] in ("turn", "x", "z", "ssm", "turn_ssm")]
    FRONT = {task: n for n, task in enumerate(front)}
    NF = len(front)
    x_in_b = x_in_dram.rearrange("b (k p) h -> b p k h", p=P)
    x_out_b = x_out_dram.rearrange("b (k p) h -> b p k h", p=P)
    bc_dram = [nc.dram_tensor(f"bc_rows{j}", [2 * N, L], F32) for j in range(2)]

    with ExitStack() as ctx:
        def sb(name, shape, dt=F32):
            return ctx.enter_context(nc.sbuf_tensor("c_" + name, shape, dt))

        def sem(name):
            return ctx.enter_context(nc.semaphore("c_" + name))

        in_proj = projection.sbuf
        out_proj = sb("out_proj", [P, DC, H])
        x_proj = sb("x_proj", [P, DC, RBC])
        dt_proj = sb("dt_proj", [R, D])
        A_neg = sb("A_neg", [P, DC, N])
        conv_w = sb("conv_w", [P, DC, K])
        conv_b = sb("conv_b", [P, DC])
        dt_bias = sb("dt_bias", [P, DC])
        D_skip = sb("D_skip", [P, DC])
        norm_w = sb("norm_w", [RBC, 1])
        ident = sb("ident", [P, P])
        minus_half = sb("minus_half", [P, TC * 4])
        x_in = sb("x_in", [P, TC, H])
        x_res = sb("x_res", [P, TC, H])
        x_out = sb("x_out", [P, TC, H])
        xn = sb("xn", [P, TC, H])
        xnT = sb("xnT", [P, HC, L])
        padded = sb("padded", [P, 2, 2, K - 1 + L])
        xc = sb("xc", [P, 2, DC, L])
        z = sb("z", [P, 2, DC, L])
        rbcT = sb("rbcT", [RBC, 2, L])
        B_all = sb("B_all", [P, 2, N, L])
        C_all = sb("C_all", [P, 2, N, L])
        dt = sb("dt", [P, 2, L])
        dtx = sb("dtx", [P, 2, L])
        soft = sb("soft", [P, L])
        relu = sb("relu", [P, L])
        state = sb("state", [P, G, GL])
        ssm = sb("ssm", [P, TC, RBC])
        square = sb("square", [P, TC, RBC])
        rms = sb("rms", [P, TC, 4])
        rms_inv = sb("rms_inv", [P, TC, 4])
        stat6 = sb("stat6", [P, 6])
        mean_var = sb("mean_var", [P, TC, 2])
        var_eps = sb("var_eps", [P, TC])
        rstd = sb("rstd", [P, TC])
        out_mean_var = sb("out_mean_var", [P, 2])
        out_var_eps = sb("out_var_eps", [P, 1])
        out_rstd = sb("out_rstd", [P, 1])
        decay = [ctx.enter_context(nc.psum_tensor(f"c_decay{j}", [P, GN, L], F32)) for j in range(2)]
        y_bank = [ctx.enter_context(nc.psum_tensor(f"c_y{j}", [P, 512], F32)) for j in range(2)]
        front_bank = ctx.enter_context(nc.psum_tensor("c_front", [P, 512], F32))
        back_bank = ctx.enter_context(nc.psum_tensor("c_back", [P, 512], F32))

        out_proj_in, small_in, A_in = sem("out_proj_in"), sem("small_in"), sem("A_in")
        consts_ready = sem("consts_ready")
        x_loaded, res_loaded, stored = sem("x_loaded"), sem("res_loaded"), sem("stored")
        rows_stored = sem("rows_stored")
        B_loaded, C_loaded = ([sem(f"{name}_loaded{g}") for g in range(G)] for name in "BC")
        A_ready = sem("A_ready")
        var_x, rstd_x, xn_ready = sem("var_x"), sem("rstd_x"), sem("xn_ready")
        front_done, front_read = sem("front_done"), sem("front_read")
        conv_done, xc_ready = sem("conv_done"), sem("xc_ready")
        z_ready = sem("z_ready")
        ssm_squares, ssm_rms, ssm_ready = sem("ssm_squares"), sem("ssm_rms"), sem("ssm_ready")
        dt_done, dt_parts, dt_ready = sem("dt_done"), sem("dt_parts"), sem("dt_ready")
        dt_split = sem("dt_split")
        decay_ready, input_ready = sem("decay_ready"), sem("input_ready")
        scanned, weighed, summed = sem("scanned"), sem("weighed"), sem("summed")
        y_skip, y_ready = sem("y_skip"), sem("y_ready")
        out_done, out_read, y_used = sem("out_done"), sem("out_read"), sem("y_used")
        var_out, rstd_out = sem("var_out"), sem("rstd_out")
        x_ready = sem("x_ready")
        dve_order = sem("dve_order")
        pace = sem("pace")
        block = ctx.enter_context(nc.Block())

        def batches(name_of, eng, main, tasks):
            def one(at, parity, previous, itself, following):
                before, now, after = ((at(d), (parity + d) % 2) for d in (-1, 0, 1))
                for slot in range(SLOTS):
                    ahead = slot + AHEAD[name_of]
                    if itself if ahead < SLOTS else following:
                        main(now if ahead < SLOTS else after, ahead % SLOTS // G, ahead % G)
                    for name, n in TASKS[name_of][slot]:
                        if name not in tasks:
                            continue
                        if name.startswith("out") or (name == "y" and n < 0):
                            batch, there = before, previous
                        elif name == "y" or (name == "dt" and n < DC):
                            batch, there = now, itself
                        else:
                            batch, there = after, following
                        if there:
                            tasks[name](batch, n % DC if name in ("y", "dt") else n)
                if "end" in tasks:
                    tasks["end"]()

            one(lambda d: -1 + d, 1, False, False, True)
            one(lambda d: d, 0, False, True, True)
            with eng.Fori(0, (BATCHES - 2) // 2) as pair:
                for k in range(2):
                    one(lambda d: pair * 2 + (1 + k + d), (1 + k) % 2, True, True, True)
            one(lambda d: BATCHES - 1 + d, (BATCHES - 1) % 2, True, True, False)
            one(lambda d: BATCHES + d, BATCHES % 2, True, False, False)

        def side_bank(b, task):
            first = isinstance(b, int) and b == 0
            return back_bank if first and FRONT[task] % 2 == 1 else front_bank

        def out_bank(b, k):
            return front_bank if k == 1 and isinstance(b, int) and b == BATCHES - 1 else back_bank

        def first_use(eng, t):
            if isinstance(t[0], int) and t[0] == 0:
                eng.wait_ge(small_in, 16 * 9)

        @block.sync
        def _(sp):
            def of(dram, b):
                return dram[b:b + 1] if isinstance(b, int) else dram[bass.ds(sp.snap(b), 1)]

            def load_x(b):
                sp.dma_start(x_in[:], of(x_in_b, b).rearrange("o p k h -> (o p) k h")).then_inc(x_loaded, 16)

            load_x(0)
            sp.dma_start(conv_w[:], io["conv_w"].rearrange("(j p) k -> p j k", p=P)).then_inc(small_in, 16)
            sp.dma_start(A_neg[:], io["A_log"].rearrange("(j p) n -> p j n", p=P)).then_inc(A_in, 16)
            for to, of_ in ((conv_b, "conv_b"), (dt_bias, "dt_bias"), (D_skip, "D_param")):
                sp.dma_start(to[:], io[of_]).then_inc(small_in, 16)
            for a, b, of_ in ((0, R, "dt_ln_w"), (R, R + N, "B_ln_w"), (R + N, RBC, "C_ln_w")):
                sp.dma_start(norm_w[a:b, :], io[of_].rearrange("(n o) -> n o", o=1)).then_inc(small_in, 16)
            sp.dma_start(x_proj[:], io["x_proj"].rearrange("(j p) e -> p j e", p=P)).then_inc(small_in, 16)
            sp.dma_start(dt_proj[:], io["dt_proj"]).then_inc(small_in, 16)
            sp.dma_start(out_proj[:], io["out_proj"].rearrange("(j p) h -> p j h", p=P)).then_inc(out_proj_in, 16)

            def norm(t, n):
                b, _ = t
                if isinstance(b, int) and b == 0:
                    return
                wait(sp, xn_ready, b)
                sp.sem_inc(pace, 1)
                load_x(b)

            def turn_ssm(t, n):
                b, parity = t
                sp.wait_ge(front_read, b * NF + FRONT["turn_ssm", 0] + 1)
                sp.sem_inc(pace, 1)
                sp.dma_start(bc_dram[parity].ap(), rbcT[R:RBC, parity, :]).then_inc(rows_stored, 16)
                sp.wait_ge(rows_stored, b * 16 + 16)
                sp.sem_inc(pace, 1)
                wait(sp, weighed, (b - 1) * (DC * G))
                sp.sem_inc(pace, 1)
                for g in range(G):
                    for rows, to, loaded in ((0, B_all, B_loaded), (N, C_all, C_loaded)):
                        states = slice(g * GN, (g + 1) * GN)
                        src = bc_dram[parity].ap()[rows + g * GN:rows + (g + 1) * GN, :]
                        sp.dma_start(to[:, parity, states, :].rearrange("p n l -> p (n l)"),
                                     src.rearrange("(o n) l -> o (n l)", o=1).to_broadcast([P, GL]))\
                            .then_inc(loaded[g], 16)

            def out(t, n):
                b, _ = t
                if n == 0:
                    src = of(x_in_b, b)
                    wait(sp, x_ready, b * TC)
                    sp.sem_inc(pace, 1)
                    sp.dma_start(x_res[:], src.rearrange("o p k h -> (o p) k h")).then_inc(res_loaded, 16)
                else:
                    dst = of(x_out_b, b)
                    sp.wait_ge(x_ready, b * TC + TC)
                    sp.sem_inc(pace, 1)
                    sp.dma_start(dst.rearrange("o p k h -> (o p) k h"), x_out[:]).then_inc(stored, 16)

            sp.sem_inc(stored, 16)
            batches("sp", sp, lambda t, j, g: None, {
                "norm": norm, "turn_ssm": turn_ssm, "out": out})
            sp.wait_ge(stored, 16 * (BATCHES + 1))

        @block.gpsimd
        def _(pool):
            X = nc.gpsimd
            X.memset(ident[:], 0.0).then_inc(consts_ready, 1)
            X.memset(minus_half[:], -0.5).then_inc(consts_ready, 1)
            X.memset(padded[:, :, :, 0:K - 1], 0.0).then_inc(consts_ready, 1)
            pool.wait_ge(consts_ready, 3)
            X.affine_select(out=ident[:], in_=ident[:], compare_op=ALU.not_equal, fill=1.0, base=0,
                            pattern=[[-1, P]], channel_multiplier=1).then_inc(consts_ready, 1)

            def main(t, j, g):
                b, parity = t
                q = b * (DC * G) + (j * G + g)
                if j == 0:
                    pool.wait_ge(B_loaded[g], b * 16 + 16)
                if g == 0:
                    pool.wait_ge(dt_ready, (b * DC + j) * 2 + 2)
                wait(pool, summed, q - (G - 1))
                a = dtx[:, j % 2, :].rearrange("p (o l) -> p o l", o=1).to_broadcast([P, GN, L])
                X.tensor_tensor(state[:, g, :].rearrange("p (n l) -> p n l", n=GN), a,
                                B_all[:, parity, g * GN:(g + 1) * GN, :], ALU.mult).then_inc(input_ready, 1)

            def norm(t, n):
                b, _ = t
                pool.wait_ge(var_x, b + 1)
                X.tensor_tensor(rstd[:], var_eps[:], minus_half[:, 0:TC], ALU.pow).then_inc(rstd_x, 1)

            def ssm_norm(t, n):
                b, _ = t
                pool.wait_ge(ssm_squares, b + 1)
                X.tensor_tensor(rms_inv[:].rearrange("p k s -> p (k s)"), rms[:].rearrange("p k s -> p (k s)"),
                                minus_half[:], ALU.pow).then_inc(ssm_rms, 1)

            def make_dt(t, j):
                b, parity = t
                n = b * DC + j
                pool.wait_ge(dt_parts, n + 1)
                wait(pool, decay_ready, (n - 1) * G)
                X.tensor_tensor(dt[:, j % 2, :], relu[:], soft[:], ALU.add).then_inc(dt_ready, 1)
                pool.wait_ge(dt_ready, n * 2 + 1)
                X.tensor_tensor(dtx[:, j % 2, :], dt[:, j % 2, :], xc[:, parity, j, :], ALU.mult)\
                    .then_inc(dt_ready, 1)

            def gate_y(t, j):
                b, parity = t
                if j == 0:
                    pool.wait_ge(z_ready, b + 1)
                pool.wait_ge(y_skip, b * DC + j + 1)
                X.tensor_tensor(xc[:, parity, j, :], xc[:, parity, j, :], z[:, parity, j, :], ALU.mult)\
                    .then_inc(y_ready, 1)

            def out(t, n):
                b, _ = t
                pool.wait_ge(var_out, b * TC + n + 1)
                X.tensor_tensor(out_rstd[:], out_var_eps[:], minus_half[:, 0:1], ALU.pow).then_inc(rstd_out, 1)

            batches("pool", pool, main, {
                "norm": norm, "ssm": ssm_norm, "dt": make_dt, "y": gate_y, "out": out})

        @block.scalar
        def _(act):
            A = nc.scalar
            exp_and_ln = "natural_log_exp_and_others"
            A.preload_act_table_set(exp_and_ln)
            act.wait_ge(A_in, 16)
            A.activation(A_neg[:], A_neg[:], ACT.Exp).then_inc(A_ready, 1)
            act.wait_ge(A_ready, 1)
            A.mul(A_neg[:], A_neg[:], -1.0).then_inc(A_ready, 1)
            act.wait_ge(A_ready, 2)

            def main(t, j, g):
                b, _ = t
                q = b * (DC * G) + (j * G + g)
                if g == 0:
                    act.wait_ge(dt_ready, (b * DC + j) * 2 + 1)
                wait(act, scanned, q - 1)
                for n in range(GN):
                    last = A.activation(decay[g % 2][:, n, 1:L], dt[:, j % 2, 1:L], ACT.Exp,
                                        scale=A_neg[:, j, g * GN + n:g * GN + n + 1])
                last.then_inc(decay_ready, 1)

            def bank_full(b, task):
                act.wait_ge(front_done, b * NF + FRONT[task] + 1)

            def turn(t, k):
                b, _ = t
                bank_full(b, ("turn", k))
                bank = side_bank(b, ("turn", k))
                A.copy(xnT[:, :, k * P:(k + 1) * P], bank[:, 0:H].rearrange("p (c n) -> p c n", c=HC))\
                    .then_inc(front_read, 1)

            def x_part(t, i):
                b, parity = t
                first_use(act, t)
                bank_full(b, ("x", i))
                wait(act, y_used, (b - 2) * (DC // 2) + i + 1)
                wait(act, conv_done, b * (DC // 2) + i - 1)
                bank = side_bank(b, ("x", i))
                for k in range(2):
                    j = 2 * i + k
                    A.activation(xc[:, parity, j, :], bank[:, k * L:(k + 1) * L], ACT.Identity,
                                 bias=conv_b[:, j:j + 1], scale=conv_w[:, j, K - 1:K])
                A.copy(padded[:, i % 2, :, K - 1:], bank[:, 0:2 * L].rearrange("p (k l) -> p k l", k=2))\
                    .then_inc(front_read, 1)

            def z_part(t, i):
                b, parity = t
                bank_full(b, ("z", i))
                bank = side_bank(b, ("z", i))
                A.copy(z[:, parity, 2 * i:2 * i + 2, :], bank[:, 0:2 * L].rearrange("p (k l) -> p k l", k=2))\
                    .then_inc(front_read, 1)

            def silu_x(t, n):
                b, parity = t
                act.wait_ge(conv_done, (b + 1) * (DC // 2))
                A.activation(xc[:, parity, :, :], xc[:, parity, :, :], ACT.Silu).then_inc(xc_ready, 1)
                A.preload_act_table_set(exp_and_ln)

            def silu_z(t, n):
                b, parity = t
                act.wait_ge(front_read, b * NF + NF)
                A.activation(z[:, parity, :, :], z[:, parity, :, :], ACT.Silu).then_inc(z_ready, 1)
                A.preload_act_table_set(exp_and_ln)

            def turn_ssm(t, n):
                b, parity = t
                first_use(act, t)
                bank_full(b, ("turn_ssm", 0))
                A.activation(rbcT[:, parity, :], side_bank(b, ("turn_ssm", 0))[0:RBC, 0:L], ACT.Copy, scale=norm_w[:])\
                    .then_inc(front_read, 1)

            def softplus(t, j):
                b, _ = t
                n = b * DC + j
                act.wait_ge(dt_done, n + 1)
                wait(act, dt_ready, n * 2)
                bias = dt_bias[:, j:j + 1]
                A.activation(relu[:], y_bank[(j + 1) % 2][:, L:2 * L], ACT.Relu, bias=bias)
                A.activation(soft[:], y_bank[(j + 1) % 2][:, L:2 * L], ACT.Abs, bias=bias).then_inc(dt_split, 1)
                act.wait_ge(dt_split, n * 3 + 1)
                A.activation(soft[:], soft[:], ACT.Exp, scale=-1.0).then_inc(dt_split, 1)
                act.wait_ge(dt_split, n * 3 + 2)
                A.activation(soft[:], soft[:], ACT.Ln, bias=1.0).then_inc(dt_split, 1)
                act.wait_ge(dt_split, n * 3 + 3)
                act.sem_inc(dt_parts, 1)

            batches("act", act, main, {
                "turn": turn, "x": x_part, "z": z_part, "silu_x": silu_x, "silu_z": silu_z,
                "turn_ssm": turn_ssm, "dt": softplus})

        @block.vector
        def _(dve):
            V = nc.vector
            after, along, _, restart = in_order(dve, dve_order)
            for j in range(2):
                after(V.memset(decay[j][:, :, 0:1], 0.0))
            dve.wait_ge(consts_ready, 4)
            restart()

            def main(t, j, g):
                b, parity = t
                q = b * (DC * G) + (j * G + g)
                if j == 0:
                    dve.wait_ge(C_loaded[g], b * 16 + 16)
                dve.wait_ge(decay_ready, q + 1)
                dve.wait_ge(input_ready, q + 1)
                V.tensor_tensor_scan(state[:, g, :], decay[g % 2][:].rearrange("p n l -> p (n l)"), state[:, g, :],
                                     0.0, ALU.mult, ALU.add).then_inc(scanned, 1)
                dve.wait_ge(scanned, q + 1)
                V.tensor_tensor(state[:, g, :], state[:, g, :],
                                C_all[:, parity, g * GN:(g + 1) * GN, :].rearrange("p n l -> p (n l)"), ALU.mult)\
                    .then_inc(weighed, 1)

            def norm(t, n):
                b, _ = t
                dve.wait_ge(x_loaded, b * 16 + 16)
                wait(dve, front_done, (b - 1) * NF + TC)
                for k in range(TC):
                    after(V.bn_stats(stat6[:], x_in[:, k, :]))
                    after(V.bn_aggr(mean_var[:, k, :], stat6[:]))
                after(V.tensor_scalar(var_eps[:], mean_var[:, :, 1], LN_EPS, None, ALU.add))
                dve.sem_inc(var_x, 1)

            def norm_apply(t, n):
                b, _ = t
                dve.wait_ge(rstd_x, b + 1)
                dve.sem_inc(pace, 1)
                for k in range(TC):
                    after(V.tensor_scalar(xn[:, k, :], x_in[:, k, :], mean_var[:, k, 0:1], rstd[:, k:k + 1],
                                          ALU.subtract, ALU.mult))
                dve.sem_inc(xn_ready, 1)

            def convolve(t, i, k):
                b, parity = t
                first_use(dve, t)
                if k == 0:
                    dve.wait_ge(front_read, b * NF + FRONT["x", i] + 1)
                    dve.sem_inc(pace, 1)
                j = 2 * i + k
                for tap in range(K - 1):
                    after(V.scalar_tensor_tensor(xc[:, parity, j, :], padded[:, i % 2, k, tap:tap + L],
                                                 conv_w[:, j, tap:tap + 1], xc[:, parity, j, :], ALU.mult, ALU.add))
                if k == 1:
                    dve.sem_inc(conv_done, 1)

            def ssm_part(t, n):
                b, _ = t
                dve.wait_ge(front_done, b * NF + FRONT["ssm", 0] + 1)
                wait(dve, front_done, (b - 1) * NF + FRONT["turn_ssm", 0] + 1)
                bank = side_bank(b, ("ssm", 0))
                after(V.tensor_copy(ssm[:], bank[:, 0:TC * RBC].rearrange("p (k e) -> p k e", k=TC)))
                dve.sem_inc(front_read, 1)
                after(V.tensor_tensor(square[:], ssm[:], ssm[:], ALU.mult))
                after(V.reduce_sum(rms[:], square[:].rearrange("p k (s n) -> p k s n", n=N), AX_X))
                after(V.tensor_tensor(rms[:, :, 0], rms[:, :, 0], rms[:, :, 1], ALU.add))
                after(V.tensor_scalar(rms[:, :, 0], rms[:, :, 0], N / R, None, ALU.mult))
                after(V.tensor_copy(rms[:, :, 1], rms[:, :, 0]))
                after(V.tensor_scalar(rms[:], rms[:], 1.0 / N, RMS_EPS, ALU.mult, ALU.add))
                dve.sem_inc(ssm_squares, 1)

            def ssm_apply(t, n):
                b, _ = t
                dve.wait_ge(ssm_rms, b + 1)
                dve.sem_inc(pace, 1)
                scale = rms_inv[:].rearrange("p k (s o) -> p k s o", o=1).to_broadcast([P, TC, 4, N])
                after(V.tensor_tensor(ssm[:].rearrange("p k (s n) -> p k s n", n=N),
                                      ssm[:].rearrange("p k (s n) -> p k s n", n=N), scale, ALU.mult))
                dve.sem_inc(ssm_ready, 1)

            def skip_y(t, j):
                b, parity = t
                dve.wait_ge(summed, b * (DC * G) + (j + 1) * G)
                V.scalar_tensor_tensor(xc[:, parity, j, :], xc[:, parity, j, :], D_skip[:, j:j + 1],
                                       y_bank[j % 2][:, 0:L], ALU.mult, ALU.add).then_inc(y_skip, 1)

            def out(t, k):
                b, _ = t
                dve.wait_ge(out_done, b * TC + k + 1)
                dve.sem_inc(pace, 1)
                after(V.bn_stats(stat6[:], out_bank(b, k)[:, 0:H]))
                after(V.bn_aggr(out_mean_var[:], stat6[:]))
                after(V.tensor_scalar(out_var_eps[:], out_mean_var[:, 1:2], LN_EPS, None, ALU.add))
                dve.sem_inc(var_out, 1)

            def out_apply(t, k):
                b, _ = t
                if k == 0:
                    dve.wait_ge(stored, b * 16 + 16)
                dve.wait_ge(rstd_out, b * TC + k + 1)
                dve.sem_inc(pace, 1)
                after(V.tensor_scalar(x_out[:, k, :], out_bank(b, k)[:, 0:H], out_mean_var[:, 0:1], out_rstd[:],
                                      ALU.subtract, ALU.mult))
                dve.sem_inc(out_read, 1)
                if k == 0:
                    dve.wait_ge(res_loaded, b * 16 + 16)
                after(V.tensor_tensor(x_out[:, k, :], x_out[:, k, :], x_res[:, k, :], ALU.add))
                dve.sem_inc(x_ready, 1)

            batches("dve", dve, main, {
                "norm": norm, "norm_apply": norm_apply,
                "convolve_first": lambda t, i: convolve(t, i, 0), "convolve": lambda t, i: convolve(t, i, 1), "ssm": ssm_part, "ssm_apply": ssm_apply,
                "y": skip_y, "out": out, "out_apply": out_apply, "end": restart})

        @block.tensor
        def _(pe):
            T_ = nc.tensor
            pe.wait_ge(consts_ready, 4)

            def main(t, j, g):
                b, _ = t
                q = b * (DC * G) + (j * G + g)
                if g == 0:
                    wait(pe, y_skip, b * DC + j - 1)
                    if not isinstance(b, int) or b * DC + j + 1 < BATCHES * DC:
                        pe.wait_ge(dt_split, (b * DC + j + 1) * 3 + 1)
                pe.wait_ge(weighed, q + 1)
                for n in range(GN):
                    last = T_.matmul(y_bank[j % 2][:, 0:L], ident[:], state[:, g, n * L:(n + 1) * L],
                                     start=(g == 0 and n == 0), stop=(g == G - 1 and n == GN - 1))
                last.then_inc(summed, 1)

            def bank_free(b, task):
                if isinstance(b, int) and b == 0 and FRONT[task] <= FRONT["ssm", 0]:
                    wait(pe, front_read, max(FRONT[task] - 1, min(FRONT[task], TC)))
                else:
                    wait(pe, front_read, b * NF + FRONT[task])

            def turn(t, k):
                b, _ = t
                pe.wait_ge(xn_ready, b + 1)
                bank_free(b, ("turn", k))
                bank = side_bank(b, ("turn", k))
                for c in range(HC):
                    last = T_.transpose(bank[:, c * P:(c + 1) * P], xn[:, k, c * P:(c + 1) * P], ident[:])
                last.then_inc(front_done, 1)

            def project(name, t, i, k):
                b, _ = t
                if k == 0:
                    if isinstance(b, int) and b == 0 and i == 0:
                        pe.wait_ge(projection.z_in if name == "z" else projection.x_in, 16)
                    bank_free(b, (name, i))
                bank = side_bank(b, (name, i))
                col = (2 * i + k + (0 if name == "x" else DC)) * P
                for c in range(HC):
                    last = T_.matmul(bank[:, k * L:(k + 1) * L], in_proj[:, c, col:col + P], xnT[:, c, :],
                                     start=(c == 0), stop=(c == HC - 1))
                if k == 1:
                    last.then_inc(front_done, 1)

            def ssm_part(t, k):
                b, parity = t
                first_use(pe, t)
                if k == 0:
                    pe.wait_ge(xc_ready, b + 1)
                    bank_free(b, ("ssm", 0))
                bank = side_bank(b, ("ssm", 0))
                for j in range(DC):
                    last = T_.matmul(bank[:, k * RBC:(k + 1) * RBC], xc[:, parity, j, k * P:(k + 1) * P],
                                     x_proj[:, j, :], start=(j == 0), stop=(j == DC - 1))
                if k == TC - 1:
                    last.then_inc(front_done, 1)

            def turn_ssm(t, n):
                b, parity = t
                pe.wait_ge(ssm_ready, b + 1)
                bank_free(b, ("turn_ssm", 0))
                pe.sem_inc(pace, 1)
                for k in range(TC):
                    last = T_.transpose(side_bank(b, ("turn_ssm", 0))[0:RBC, k * P:(k + 1) * P], ssm[:, k, :], ident[:])
                last.then_inc(front_done, 1)

            def dt_part(t, j):
                b, parity = t
                n = b * DC + j
                pe.wait_ge(front_read, b * NF + FRONT["turn_ssm", 0] + 1)
                wait(pe, y_skip, n - 2)
                T_.matmul(y_bank[(j + 1) % 2][:, L:2 * L], dt_proj[:, j * P:(j + 1) * P], rbcT[0:R, parity, :],
                          start=True, stop=True).then_inc(dt_done, 1)

            def out(t, k, part):
                b, parity = t
                bank = out_bank(b, k)
                if isinstance(b, int) and b == 0:
                    pe.wait_ge(out_proj_in, 16)
                if part == 0 and bank is front_bank:
                    pe.wait_ge(front_read, BATCHES * NF)
                elif part == 0:
                    wait(pe, out_read, b * TC + k)
                    if isinstance(b, int) and b == 0 and k == 0:
                        pe.wait_ge(front_read, NF)
                first = part * (DC // 4)
                pe.wait_ge(y_ready, b * DC + (first + DC // 4))
                for j in range(first, first + DC // 4):
                    last = T_.matmul(bank[:, 0:H], xc[:, parity, j, k * P:(k + 1) * P], out_proj[:, j, :],
                                     start=(j == 0), stop=(j == DC - 1))
                if part == 3:
                    last.then_inc(out_done, 1)
                if k == TC - 1:
                    pe.sem_inc(y_used, 1)

            batches("pe", pe, main, {
                "turn": turn,
                "x_first": lambda t, i: project("x", t, i, 0), "x": lambda t, i: project("x", t, i, 1),
                "z_first": lambda t, i: project("z", t, i, 0), "z": lambda t, i: project("z", t, i, 1),
                "ssm_first": lambda t, n: ssm_part(t, 0), "ssm": lambda t, n: ssm_part(t, 1),
                "turn_ssm": turn_ssm, "dt": dt_part,
                "out_part": lambda t, n: out(t, n // 4, n % 4), "out": lambda t, k: out(t, k, 3)})


def gated_lora(nc, io, x_in_dram, x_out_dram):
    tokens, H = x_in_dram.shape
    OUT = io["ffn_w"].shape[1]
    HID, E = io["gw2"].shape
    ER = io["lora_B"].shape[0]
    R = ER // E
    TILES = tokens // P
    HC = H // P
    SIDE = HID + ER
    CAPACITY = int(3.0 * tokens / E)
    ALPHA = 1.0 / R
    LOADS = 4
    PER = 512 // P
    x_in_t = x_in_dram.rearrange("(t p) h -> p t h", p=P)
    x_out_t = x_out_dram.rearrange("(t p) h -> t p h", p=P)
    assert TILES % 2 == 0 and TILES * E * 2 <= 512

    with ExitStack() as ctx:
        def sb(name, shape, dt=F32):
            return ctx.enter_context(nc.sbuf_tensor("d_" + name, shape, dt))

        def bank(name):
            return ctx.enter_context(nc.psum_tensor("d_" + name, [P, 512], F32))

        def sem(name):
            return ctx.enter_context(nc.semaphore("d_" + name))

        ffn_w = sb("ffn_w", [P, HC, OUT])
        side_w = sb("side_w", [P, HC, SIDE])
        lora_B = sb("lora_B", [ER, OUT])
        gw2 = sb("gw2", [HID, E])
        rows = {name: sb(name, [P, n]) for name, n in
                (("gb1", HID), ("ln_gamma", HID), ("ln_beta", HID), ("gb2", E))}
        ident = sb("ident", [P, P])
        ones = sb("ones", [P, P])
        minus_half = sb("minus_half", [P, TILES])
        iota_e = sb("iota_e", [P, TILES, E])
        x_all = sb("x_all", [P, TILES, H])
        side_all = sb("side_all", [P, TILES, SIDE])
        xn = sb("xn", [P, 2, H])
        xnT = sb("xnT", [P, 2, HC, P])
        stat6 = sb("stat6", [P, 2, 6])
        mean_var = sb("mean_var", [P, TILES, 2])
        out_mean_var = sb("out_mean_var", [P, 2, 2])
        out_var_eps = sb("out_var_eps", [P, 2])
        out_rstd = sb("out_rstd", [P, 2])
        out_normed = sb("out_normed", [P, OUT])
        hid_rstd = sb("hid_rstd", [P, TILES])
        var_eps = sb("var_eps", [P, TILES])
        rstd = sb("rstd", [P, TILES])
        hid = sb("hid", [P, TILES, HID])
        hid2 = sb("hid2", [P, TILES, HID])
        hidT = sb("hidT", [HID, TILES, P])
        scores = sb("scores", [P, TILES, E])
        key = sb("key", [P, TILES, E])
        equal = sb("equal", [P, TILES, E])
        best = sb("best", [P, 2, TILES])
        first = sb("first", [P, TILES])
        chosen = sb("chosen", [P, 2, TILES, E])
        share = sb("share", [P, 2, TILES])
        odds = sb("odds", [P, TILES])
        counts = sb("counts", [P, 2, E])
        weight = sb("weight", [P, TILES, E])
        tmp = sb("tmp", [P, 2, ER])
        tmpT = sb("tmpT", [ER, 2, P])

        turn_bank = [bank(f"turn{j}") for j in range(2)]
        out_bank = [bank(f"out{j}") for j in range(4)]
        side_bank = out_bank[2:]
        gate_bank = bank("gate")
        count_bank = bank("count")
        hid_bank = [turn_bank[1], count_bank]

        x_loaded = [sem(f"x_loaded{j}") for j in range(LOADS)]
        side_in, lora_in, ffn_in, rows_in = sem("side_in"), sem("lora_in"), sem("ffn_in"), sem("rows_in")
        consts_ready = sem("consts_ready")
        var_ready, rstd_ready = sem("var_ready"), sem("rstd_ready")
        xn_ready, turned, xnT_ready = sem("xn_ready"), sem("turned"), sem("xnT_ready")
        side_done, side_moved = sem("side_done"), sem("side_moved")
        hid_var, hid_rstd_ready = sem("hid_var"), sem("hid_rstd_ready")
        hid_ready, hid_turned, hidT_ready = sem("hid_ready"), sem("hid_turned"), sem("hidT_ready")
        scores_done, gap_ready, odds_ready = sem("scores_done"), sem("gap_ready"), sem("odds_ready")
        chosen_ready, counted, weight_ready = sem("chosen_ready"), sem("counted"), sem("weight_ready")
        xn_again, turned_again, xnT_again = sem("xn_again"), sem("turned_again"), sem("xnT_again")
        main_done = sem("main_done")
        tmp_ready, tmp_turned, tmpT_ready = sem("tmp_ready"), sem("tmp_turned"), sem("tmpT_ready")
        out_done, out_var, out_rstd_ready, out_read = (sem("out_done"), sem("out_var"), sem("out_rstd_ready"),
                                                       sem("out_read"))
        x_ready, stored = sem("x_ready"), sem("stored")
        dve_order = sem("dve_order")
        pace = sem("pace")
        block = ctx.enter_context(nc.Block())

        def over_tiles(eng, body, first, loop_from, unrolled, rounds, last):
            for t in range(first, loop_from):
                body(t, t % unrolled)
            with eng.Fori(0, rounds) as n:
                for k in range(loop_from, loop_from + unrolled):
                    body(n * unrolled + k, k % unrolled)
            for t in range(loop_from + rounds * unrolled, last + 1):
                body(t, t % unrolled)

        def is_tile(t):
            return not isinstance(t, int) or 0 <= t < TILES

        FIRST_ROUND = (-1, 1, 2, (TILES - 2) // 2, TILES - 1)
        AHEAD = 3
        SECOND_ROUND = (0, 2, 4, (TILES - 8) // 4, TILES - 1)

        def at(t):
            return t if isinstance(t, int) else bass.ds(t, 1)

        def tile_of(tensor, t):
            return tensor[:, t, :] if isinstance(t, int) else \
                tensor[:, bass.ds(t, 1), :].rearrange("p o n -> p (o n)")

        @block.sync
        def _(sp):
            step = TILES // LOADS

            def load_side_weights():
                for cols, name in ((slice(0, HID), "gw1"), (slice(HID, SIDE), "lora_A")):
                    sp.dma_start(side_w[:, :, cols], io[name].rearrange("(c p) o -> p c o", p=P)).then_inc(side_in, 16)

            for j in range(LOADS):
                if j == 1:
                    load_side_weights()
                sp.dma_start(x_all[:, j * step:(j + 1) * step, :], x_in_t[:, j * step:(j + 1) * step, :])\
                    .then_inc(x_loaded[j], 16)
            for name, row in rows.items():
                n = row.shape[1]
                sp.dma_start(row[:], io[name].rearrange("(o n) -> o n", o=1).to_broadcast([P, n]))\
                    .then_inc(rows_in, 16)

            sp.dma_start(ffn_w[:], io["ffn_w"].rearrange("(c p) o -> p c o", p=P)).then_inc(ffn_in, 16)
            sp.dma_start(lora_B[:], io["lora_B"]).then_inc(lora_in, 16)
            sp.dma_start(gw2[:], io["gw2"]).then_inc(lora_in, 16)

            def store(t, k):
                dst = x_out_t[t:t + 1] if isinstance(t, int) else x_out_t[bass.ds(sp.snap(t), 1)]
                src = tile_of(x_all, t if isinstance(t, int) else sp.snap(t))
                sp.wait_ge(x_ready, t + 1)
                sp.sem_inc(pace, 1)
                sp.dma_start(dst.rearrange("o p h -> (o p) h"), src).then_inc(stored, 16)

            over_tiles(sp, store, 0, 2, 2, TILES // 2 - 1, TILES - 1)
            sp.wait_ge(stored, 16 * TILES)

        @block.gpsimd
        def _(pool):
            X = nc.gpsimd
            X.memset(ident[:], 0.0).then_inc(consts_ready, 1)
            X.memset(minus_half[:], -0.5).then_inc(consts_ready, 1)
            X.memset(ones[:], 1.0).then_inc(consts_ready, 1)
            X.iota(iota_e[:], pattern=[[0, TILES], [1, E]], base=0, channel_multiplier=0,
                   allow_small_or_imprecise_dtypes=True).then_inc(consts_ready, 1)
            pool.wait_ge(consts_ready, 4)
            X.affine_select(out=ident[:], in_=ident[:], compare_op=ALU.not_equal, fill=1.0, base=0,
                            pattern=[[-1, P]], channel_multiplier=1).then_inc(consts_ready, 1)

            def scale(t, k):
                if is_tile(t):
                    wait(pool, tmp_turned, t - 1)
                    pool.sem_inc(pace, 1)
                    w = tile_of(weight, t).rearrange("p (e o) -> p e o", o=1).to_broadcast([P, E, R])
                    X.tensor_tensor(tmp[:, k % 2, :].rearrange("p (e r) -> p e r", e=E),
                                    tile_of(side_all, t)[:, HID:].rearrange("p (e r) -> p e r", e=E), w, ALU.mult)\
                        .then_inc(tmp_ready, 1)

            def inverse_root(t, k):
                pool.wait_ge(out_var, t + 1)
                X.tensor_tensor(out_rstd[:, k % 2:k % 2 + 1], out_var_eps[:, k % 2:k % 2 + 1], minus_half[:, 0:1],
                                ALU.pow).then_inc(out_rstd_ready, 1)

            step = TILES // LOADS
            for j in range(LOADS):
                pool.wait_ge(var_ready, j + 1)
                X.tensor_tensor(rstd[:, j * step:(j + 1) * step], var_eps[:, j * step:(j + 1) * step],
                                minus_half[:, 0:step], ALU.pow).then_inc(rstd_ready, 1)
            pool.wait_ge(side_moved, TILES)
            pool.wait_ge(hid_var, 1)
            X.tensor_tensor(hid_rstd[:], var_eps[:], minus_half[:], ALU.pow).then_inc(hid_rstd_ready, 1)
            pool.wait_ge(weight_ready, 1)
            scale(0, 0)
            scale(1, 1)

            def second(t, k):
                scale(t + 2, k + 2)
                inverse_root(t, k)

            over_tiles(pool, second, *SECOND_ROUND)

        @block.vector
        def _(dve):
            V = nc.vector
            after, along, _, restart = in_order(dve, dve_order)
            dve.wait_ge(consts_ready, 5)

            def normalise(t, k, ready):
                V.tensor_scalar(xn[:, k % 2, :], tile_of(x_all, t), tile_of(mean_var, t)[:, 0:1],
                                rstd[:, at(t)] if not isinstance(t, int) else rstd[:, t:t + 1],
                                ALU.subtract, ALU.mult).then_inc(ready, 1)

            step = TILES // LOADS
            for j in range(LOADS + 1):
                if j < LOADS:
                    dve.wait_ge(x_loaded[j], 16)
                    for pair in range(j * step, (j + 1) * step, 2):
                        along(V.bn_stats(stat6[:, 0, :], x_all[:, pair, :]))
                        after(V.bn_stats(stat6[:, 1, :], x_all[:, pair + 1, :]))
                        along(V.bn_aggr(mean_var[:, pair, :], stat6[:, 0, :]))
                        after(V.bn_aggr(mean_var[:, pair + 1, :], stat6[:, 1, :]))
                    after(V.tensor_scalar(var_eps[:, j * step:(j + 1) * step], mean_var[:, j * step:(j + 1) * step, 1],
                                          LN_EPS, None, ALU.add))
                    dve.sem_inc(var_ready, 1)
                if j >= 1:
                    dve.wait_ge(rstd_ready, j)
                    for t in range((j - 1) * step, j * step):
                        wait(dve, turned, t - 1)
                        normalise(t, t, xn_ready)
            restart()

            def renormalise(t, k):
                if is_tile(t):
                    wait(dve, turned_again, t - 1)
                    dve.sem_inc(pace, 1)
                    normalise(t, k, xn_again)

            dve.wait_ge(turned, TILES)
            renormalise(0, 0)
            renormalise(1, 1)

            def spread(a, n):
                return a.rearrange("p (t o) -> p t o", o=1).to_broadcast([P, TILES, n])

            def every(a, n):
                return a.rearrange("p (o n) -> p o n", o=1).to_broadcast([P, TILES, n])

            dve.wait_ge(side_moved, TILES)
            dve.wait_ge(rows_in, 64)
            after(V.tensor_tensor(hid[:], side_all[:, :, 0:HID], every(rows["gb1"][:], HID), ALU.add))
            after(V.reduce_sum(first[:], hid[:], AX_X))
            after(V.tensor_scalar(first[:], first[:], 1.0 / HID, None, ALU.mult))
            after(V.tensor_tensor(hid[:], hid[:], spread(first[:], HID), ALU.subtract))
            after(V.tensor_tensor(hid2[:], hid[:], hid[:], ALU.mult))
            after(V.reduce_sum(first[:], hid2[:], AX_X))
            after(V.tensor_scalar(var_eps[:], first[:], 1.0 / HID, LN_EPS, ALU.mult, ALU.add))
            dve.sem_inc(hid_var, 1)
            dve.wait_ge(hid_rstd_ready, 1)
            after(V.tensor_tensor(hid[:], hid[:], spread(hid_rstd[:], HID), ALU.mult))
            after(V.tensor_tensor(hid[:], hid[:], every(rows["ln_gamma"][:], HID), ALU.mult))
            after(V.tensor_tensor(hid[:], hid[:], every(rows["ln_beta"][:], HID), ALU.add))
            after(V.tensor_scalar(hid[:], hid[:], 0.0, None, ALU.max))
            dve.sem_inc(hid_ready, 1)
            renormalise(2, 2)
            dve.wait_ge(scores_done, 1)
            after(V.tensor_tensor(scores[:], gate_bank[:, 0:TILES * E].rearrange("p (t e) -> p t e", e=E),
                                  every(rows["gb2"][:], E), ALU.add))
            for k in range(2):
                after(V.tensor_reduce(best[:, k, :], scores[:], AX_X, ALU.max))
                after(V.tensor_tensor(equal[:], scores[:], spread(best[:, k, :], E), ALU.is_equal))
                after(V.scalar_tensor_tensor(key[:], equal[:], -64.0, iota_e[:], ALU.mult, ALU.add))
                after(V.tensor_reduce(first[:], key[:], AX_X, ALU.min))
                after(V.tensor_tensor(chosen[:, k, :, :], key[:], spread(first[:], E), ALU.is_equal))
                if k == 0:
                    after(V.scalar_tensor_tensor(scores[:], chosen[:, 0, :, :], -3e38, scores[:],
                                                 ALU.mult, ALU.add))
            dve.sem_inc(chosen_ready, 1)
            after(V.tensor_tensor(odds[:], best[:, 1, :], best[:, 0, :], ALU.subtract))
            dve.sem_inc(gap_ready, 1)
            renormalise(3, 3)
            dve.wait_ge(odds_ready, 1)
            after(V.tensor_scalar(share[:, 0, :], odds[:], 1.0, None, ALU.add))
            after(V.reciprocal(share[:, 0, :], share[:, 0, :]))
            after(V.tensor_tensor(share[:, 1, :], odds[:], share[:, 0, :], ALU.mult))
            dve.wait_ge(counted, 1)
            after(V.reduce_sum(counts[:], count_bank[:, 0:2 * TILES * E]
                               .rearrange("p (k t e) -> p k e t", k=2, e=E), AX_X))
            after(V.tensor_scalar(counts[:], counts[:], float(CAPACITY), ALPHA, ALU.is_le, ALU.mult))
            for k in range(2):
                after(V.tensor_tensor(chosen[:, k, :, :], chosen[:, k, :, :], spread(share[:, k, :], E), ALU.mult))
                after(V.tensor_tensor(chosen[:, k, :, :], chosen[:, k, :, :], every(counts[:, k, :], E), ALU.mult))
            after(V.tensor_tensor(weight[:], chosen[:, 0, :, :], chosen[:, 1, :, :], ALU.add))
            dve.sem_inc(weight_ready, 1)
            restart()

            renormalise(4, 4)

            def second(t, k):
                place = k % 2
                dve.wait_ge(out_done, t + 1)
                dve.sem_inc(pace, 1)
                after(V.bn_stats(stat6[:, 0, :], out_bank[k][:, 0:OUT]))
                after(V.bn_aggr(out_mean_var[:, place, :], stat6[:, 0, :]))
                after(V.tensor_scalar(out_var_eps[:, place:place + 1], out_mean_var[:, place, 1:2], LN_EPS, None,
                                      ALU.add))
                dve.sem_inc(out_var, 1)
                renormalise(t + AHEAD + 2, k + AHEAD + 2)
                dve.wait_ge(out_rstd_ready, t + 1)
                dve.sem_inc(pace, 1)
                after(V.tensor_scalar(out_normed[:], out_bank[k][:, 0:OUT], out_mean_var[:, place, 0:1],
                                      out_rstd[:, place:place + 1], ALU.subtract, ALU.mult))
                dve.sem_inc(out_read, 1)
                after(V.tensor_tensor(tile_of(x_all, t), tile_of(x_all, t), out_normed[:], ALU.add))
                dve.sem_inc(x_ready, 1)
                restart()

            over_tiles(dve, second, *SECOND_ROUND)

        @block.scalar
        def _(act):
            A = nc.scalar

            def move_x(t, k, done, used, ready):
                if is_tile(t):
                    act.wait_ge(done, t + 1)
                    wait(act, used, t - 1)
                    act.sem_inc(pace, 1)
                    bank_of = turn_bank[k % 2] if done is turned else turn_bank[0]
                    A.copy(xnT[:, k % 2, :, :], bank_of[:, 0:H].rearrange("p (c n) -> p c n", c=HC)).then_inc(ready, 1)

            def first(t, k):
                move_x(t + 1, k + 1, turned, side_done, xnT_ready)
                if is_tile(t):
                    act.wait_ge(side_done, t + 1)
                    act.sem_inc(pace, 1)
                    A.copy(tile_of(side_all, t), side_bank[k % 2][:, 0:SIDE]).then_inc(side_moved, 1)

            def move_x_again(t, k):
                move_x(t, k, turned_again, main_done, xnT_again)

            def move_tmp(t, k):
                if is_tile(t):
                    act.wait_ge(tmp_turned, t + 1)
                    wait(act, out_done, t - 1)
                    act.sem_inc(pace, 1)
                    A.copy(tmpT[:, k % 2, :], turn_bank[1][0:ER, 0:P]).then_inc(tmpT_ready, 1)

            over_tiles(act, first, *FIRST_ROUND)
            act.wait_ge(side_done, TILES)
            move_x_again(0, 0)
            move_x_again(1, 1)
            for r in range(TILES // PER):
                act.wait_ge(hid_turned, r + 1)
                A.copy(hidT[:, r * PER:(r + 1) * PER, :],
                       hid_bank[r % 2][0:HID, :].rearrange("p (t n) -> p t n", n=P)).then_inc(hidT_ready, 1)
            move_x_again(2, 2)
            act.wait_ge(gap_ready, 1)
            A.activation(odds[:], odds[:], ACT.Exp).then_inc(odds_ready, 1)
            move_x_again(3, 3)
            move_tmp(0, 0)

            def second(t, k):
                move_tmp(t + 1, k + 1)
                move_x_again(t + AHEAD + 1, k + AHEAD + 1)

            over_tiles(act, second, *SECOND_ROUND)

        @block.tensor
        def _(pe):
            T_ = nc.tensor
            pe.wait_ge(consts_ready, 5)

            def turn(k, to, done):
                for c in range(HC):
                    last = T_.transpose(to[:, c * P:(c + 1) * P], xn[:, k % 2, c * P:(c + 1) * P], ident[:])
                last.then_inc(done, 1)

            def first(t, k):
                if is_tile(t + 1):
                    pe.wait_ge(xn_ready, t + 2)
                    wait(pe, xnT_ready, t)
                    pe.sem_inc(pace, 1)
                    turn(k + 1, turn_bank[(k + 1) % 2], turned)
                if is_tile(t):
                    if isinstance(t, int) and t == 0:
                        pe.wait_ge(side_in, 32)
                    pe.wait_ge(xnT_ready, t + 1)
                    wait(pe, side_moved, t - 1)
                    pe.sem_inc(pace, 1)
                    for c in range(HC):
                        last = T_.matmul(side_bank[k % 2][:, 0:SIDE], xnT[:, k % 2, c, :], side_w[:, c, :],
                                         start=(c == 0), stop=(c == HC - 1))
                    last.then_inc(side_done, 1)

            def turn_again(t, k):
                if is_tile(t):
                    pe.wait_ge(xn_again, t + 1)
                    wait(pe, xnT_again, t)
                    pe.sem_inc(pace, 1)
                    turn(k, turn_bank[0], turned_again)

            def main(t, k):
                if is_tile(t):
                    pe.wait_ge(xnT_again, t + 1)
                    wait(pe, out_read, t - 3)
                    pe.sem_inc(pace, 1)
                    for c in range(HC):
                        last = T_.matmul(out_bank[k % 4][:, 0:OUT], xnT[:, k % 2, c, :], ffn_w[:, c, :],
                                         start=(c == 0), stop=False)
                    last.then_inc(main_done, 1)

            def turn_tmp(t, k):
                if is_tile(t):
                    pe.wait_ge(tmp_ready, t + 1)
                    wait(pe, tmpT_ready, t)
                    pe.sem_inc(pace, 1)
                    T_.transpose(turn_bank[1][0:ER, 0:P], tmp[:, k % 2, :], ident[:]).then_inc(tmp_turned, 1)

            def lora(t, k):
                pe.wait_ge(tmpT_ready, t + 1)
                pe.sem_inc(pace, 1)
                T_.matmul(out_bank[k % 4][:, 0:OUT], tmpT[:, k % 2, :], lora_B[:], start=False, stop=True)\
                    .then_inc(out_done, 1)

            over_tiles(pe, first, *FIRST_ROUND)
            pe.wait_ge(ffn_in, 16)
            pe.wait_ge(lora_in, 32)
            pe.wait_ge(xnT_ready, TILES)
            pe.wait_ge(side_moved, TILES)
            for t in range(2):
                turn_again(t, t)
                main(t, t)
            pe.wait_ge(hid_ready, 1)
            for r in range(TILES // PER):
                if r >= 2:
                    pe.wait_ge(hidT_ready, r - 1)
                for k in range(PER):
                    last = T_.transpose(hid_bank[r % 2][0:HID, k * P:(k + 1) * P], hid[:, r * PER + k, :], ident[:])
                last.then_inc(hid_turned, 1)
            pe.wait_ge(hidT_ready, TILES // PER)
            for t in range(TILES):
                last = T_.matmul(gate_bank[:, t * E:(t + 1) * E], hidT[:, t, :], gw2[:], start=True, stop=True)
            last.then_inc(scores_done, 1)
            turn_again(2, 2)
            main(2, 2)
            pe.wait_ge(chosen_ready, 1)
            T_.matmul(count_bank[:, 0:2 * TILES * E], ones[:], chosen[:].rearrange("p k t e -> p (k t e)"),
                      start=True, stop=True).then_inc(counted, 1)

            turn_again(3, 3)
            turn_tmp(0, 0)

            def second(t, k):
                turn_tmp(t + 1, k + 1)
                lora(t, k)
                turn_again(t + AHEAD + 1, k + AHEAD + 1)
                main(t + AHEAD, k + AHEAD)

            over_tiles(pe, second, *SECOND_ROUND)


def _program(nc, io, x, out):
    batches, length, H = x.shape
    after_mlp = nc.dram_tensor("x_after_router", [batches * length, H], F32).ap()
    after_scan = nc.dram_tensor("x_after_scan", [batches * length, H], F32).ap()
    with ExitStack() as ctx:
        projection = InProjection(nc, ctx, io["in_proj"])
        mlp_and_router(nc, io, projection, x.rearrange("b s h -> (b s) h"), after_mlp)
        selective_scan(nc, io, projection, after_mlp.rearrange("(b s) h -> b s h", b=batches),
                       after_scan.rearrange("(b s) h -> b s h", b=batches))
    gated_lora(nc, io, after_scan, out.rearrange("b s h -> (b s) h"))


_AS_IS = {"router_bias": "L0_ffn_router_bias", "expert_bias": "L0_ffn_expert_bias",
          "conv_w": "L1_attn_conv_w", "A_log": "L1_attn_A_log",
          "dt_ln_w": "L1_attn_dt_ln_w", "B_ln_w": "L1_attn_B_ln_w", "C_ln_w": "L1_attn_C_ln_w",
          "in_proj": "L1_attn_in_proj_w",
          "gb1": "L1_ffn_gb1", "ln_gamma": "L1_ffn_ln_gamma", "ln_beta": "L1_ffn_ln_beta", "gb2": "L1_ffn_gb2"}
_COLUMNS = {"conv_b": "L1_attn_conv_b", "dt_bias": "L1_attn_dt_bias", "D_param": "L1_attn_D_param"}
_TURNED = {"w_gate": "L0_attn_w_gate", "w_up": "L0_attn_w_up", "w_down": "L0_attn_w_down",
           "router_w": "L0_ffn_router_weight",
           "x_proj": "L1_attn_x_proj_w", "dt_proj": "L1_attn_dt_proj_w", "out_proj": "L1_attn_out_proj_w",
           "ffn_w": "L1_ffn_weight", "gw1": "L1_ffn_gw1", "gw2": "L1_ffn_gw2"}
def kernel(**inputs):
    import numpy as _np
    import concourse.bacc as _bacc
    from concourse import mybir as _mybir
    from concourse.bass_utils import run_bass_kernel_spmd as _run

    nc = _bacc.Bacc("TRN2", target_bir_lowering=False, num_devices=1)
    arrays = {"x": _np.ascontiguousarray(inputs["L0_attn_x"])}
    for name, source in _AS_IS.items():
        arrays[name] = _np.ascontiguousarray(inputs[source])
    for name, source in _TURNED.items():
        arrays[name] = _np.ascontiguousarray(_np.asarray(inputs[source]).T)
    for name, source in _COLUMNS.items():
        arrays[name] = _np.ascontiguousarray(_np.asarray(inputs[source]).reshape(-1, 128).T)
    lora_a, lora_b = _np.asarray(inputs["L1_ffn_lora_A"]), _np.asarray(inputs["L1_ffn_lora_B"])
    arrays["lora_A"] = _np.ascontiguousarray(lora_a.transpose(1, 0, 2).reshape(lora_a.shape[1], -1))
    arrays["lora_B"] = _np.ascontiguousarray(lora_b.reshape(-1, lora_b.shape[2]))
    io = {name: nc.dram_tensor(name, a.shape, _mybir.dt.from_np(a.dtype), kind="ExternalInput").ap()
          for name, a in arrays.items()}
    x = io.pop("x")
    out = nc.dram_tensor("out", x.shape, _mybir.dt.float32, kind="ExternalOutput").ap()
    _program(nc, io, x, out)
    return _run(nc, [arrays], core_ids=[0]).results[0]["out"]
```
